# Optimizing a Trainium2 kernel written in Bass

```python
import numpy as np
import jax
import jax.numpy as jnp

def _softmax(x, axis=-1):
    return jax.nn.softmax(x, axis=axis)

def _gelu(x):
    return jax.nn.gelu(x, approximate=True)

def _silu(x):
    return jax.nn.silu(x)

def _sigmoid(x):
    return jax.nn.sigmoid(x)

def _layernorm(x, axis=-1, eps=1e-05):
    m = jnp.mean(x, axis=axis, keepdims=True)
    v = jnp.var(x, axis=axis, keepdims=True)
    return (x - m) / jnp.sqrt(v + eps)

def _scatter_add(tgt, idx, src, axis=0):
    return tgt.at[idx].add(src)

def _segment_sum(src, seg, n):
    return jax.ops.segment_sum(src, seg, n)
kernel_name = 'mk_decoder_postln_d2_seqx_r8_5cd9e2'

def setup_inputs(seed: int=0):
    np.random.seed(seed)
    _w = jnp.asarray

    def _rec_inputs():
        import jax
        import jax.numpy as jnp
        _rk = jax.random.key(seed)
        x = 7.22e-05 + 1 * jax.random.normal(jax.random.fold_in(_rk, 1), (32, 64, 128), jnp.float32)
        _lenS = 64 - jax.random.randint(jax.random.fold_in(_rk, 7), (32,), 0, max(1, 64 // 4) + 1, jnp.int32)
        _lenS2 = 64 - jax.random.randint(jax.random.fold_in(_rk, 8), (32,), 0, max(1, 64 // 4) + 1, jnp.int32)
        _ctx_1024P = jax.random.normal(jax.random.fold_in(_rk, 11), (32, 16, 128), jnp.float32)
        _ctx_1024c = jax.random.dirichlet(jax.random.fold_in(_rk, 511), 0.3 * jnp.ones((16,), jnp.float32), (32, 64))
        _ctx_1024t = jnp.einsum('bsk,bkd->bsd', _ctx_1024c, _ctx_1024P)
        _ctx_1024t = _ctx_1024t * jax.lax.rsqrt(jnp.mean(jnp.square(_ctx_1024t)) + 1e-12) * 0.953939
        ctx_1024 = 4.13588e-05 + 0.999923 * (_ctx_1024t + 0.3 * jax.random.normal(jax.random.fold_in(_rk, 611), (32, 64, 128), jnp.float32))
        return (x, ctx_1024)
    x, ctx_1024 = _rec_inputs()

    def _L0_attn_setup():
        import jax, jax.numpy as jnp
        import numpy as np
        H = 16
        W = 32
        D_MODEL = 128
        D_FF = 512
        EPS = 1e-05

        def _layernorm(x, g, b):
            mu = jnp.mean(x, axis=-1, keepdims=True)
            var = jnp.mean(jnp.square(x - mu), axis=-1, keepdims=True)
            return (x - mu) * jax.lax.rsqrt(var + EPS) * g + b

        def _sliding_attn(q, k, v, w):
            B, Hh, S, d = q.shape
            nc = S // w
            qc = q.reshape(B, Hh, nc, w, d)
            kp = jnp.pad(k, ((0, 0), (0, 0), (w, w), (0, 0)))
            vp = jnp.pad(v, ((0, 0), (0, 0), (w, w), (0, 0)))
            idx = (jnp.arange(nc) * w)[:, None] + jnp.arange(3 * w)[None, :]
            kc = kp[:, :, idx, :]
            vc = vp[:, :, idx, :]
            scores = jnp.einsum('bhcqd,bhckd->bhcqk', qc, kc)
            q_pos = jnp.arange(nc)[:, None, None] * w + jnp.arange(w)[None, :, None]
            k_pos = jnp.arange(nc)[:, None, None] * w - w + jnp.arange(3 * w)[None, None, :]
            rel = k_pos - q_pos
            valid = (jnp.abs(rel) <= w) & (k_pos >= 0) & (k_pos < S)
            scores = jnp.where(valid[None, None], scores, jnp.float32(-1000000000.0))
            p = jax.nn.softmax(scores, axis=-1)
            out = jnp.einsum('bhcqk,bhckd->bhcqd', p, vc)
            return out.reshape(B, Hh, S, d)
        key = jax.random.key(seed)
        ks = jax.random.split(key, 8)
        B, S = (2, 512)
        src = jax.random.normal(ks[0], (B, S, D_MODEL), dtype=jnp.float32)
        ln1_g = jnp.ones((D_MODEL,), jnp.float32)
        ln1_b = jnp.zeros((D_MODEL,), jnp.float32)
        ln2_g = jnp.ones((D_MODEL,), jnp.float32)
        ln2_b = jnp.zeros((D_MODEL,), jnp.float32)
        W1 = jax.random.normal(ks[1], (D_MODEL, D_FF), jnp.float32) * 0.02
        b1 = jnp.zeros((D_FF,), jnp.float32)
        W2 = jax.random.normal(ks[2], (D_FF, D_MODEL), jnp.float32) * 0.02
        b2 = jnp.zeros((D_MODEL,), jnp.float32)
        return {'src': src, 'ln1_g': ln1_g, 'ln1_b': ln1_b, 'ln2_g': ln2_g, 'ln2_b': ln2_b, 'W1': W1, 'b1': b1, 'W2': W2, 'b2': b2}
    _L0_attn_all = _L0_attn_setup()
    _L0_attn_in = {k: v for k, v in _L0_attn_all.items() if k in ('ln1_g', 'ln1_b', 'ln2_g', 'ln2_b', 'W1', 'b1', 'W2', 'b2')}
    del _L0_attn_all

    def _L0_xattn_setup():
        import jax, jax.numpy as jnp
        import numpy as np
        B, S, D, H, W = (2, 512, 128, 16, 16)
        HD = D // H
        key = jax.random.key(seed)
        ks = jax.random.split(key, 10)
        std = 0.02
        mk_w = lambda k: jax.random.normal(k, (D, D), jnp.float32) * std
        mk_b = lambda k: jax.random.normal(k, (D,), jnp.float32) * std
        return {'query': jax.random.normal(ks[0], (B, S, D), jnp.float32), 'kv': jax.random.normal(ks[1], (B, S, D), jnp.float32), 'Wq': mk_w(ks[2]), 'bq': mk_b(ks[3]), 'Wk': mk_w(ks[4]), 'bk': mk_b(ks[5]), 'Wv': mk_w(ks[6]), 'bv': mk_b(ks[7]), 'Wo': mk_w(ks[8]), 'bo': mk_b(ks[9]), 'is_causal': 1}
    _L0_xattn_all = _L0_xattn_setup()
    _L0_xattn_in = {k: v for k, v in _L0_xattn_all.items() if k in ('Wq', 'bq', 'Wk', 'bk', 'Wv', 'bv', 'Wo', 'bo')}
    del _L0_xattn_all

    def _L0_ffn_setup():
        import jax, jax.numpy as jnp
        import numpy as np
        B, S, D = (2, 256, 128)
        E, K, H = (8, 2, 512)
        CAP_FACTOR = 1.0

        def _moe_forward(x, wg, w1, b1, w2, b2):
            Bb, Ss, Dd = x.shape
            T = Bb * Ss
            cap = int(K * CAP_FACTOR * ((T + E - 1) // E))
            xt = x.reshape(T, Dd)
            logits = xt @ wg
            scores = jax.nn.softmax(logits, axis=-1)
            gates_k, idx_k = jax.lax.top_k(scores, K)
            gates_k = gates_k / jnp.sum(gates_k, axis=-1, keepdims=True)
            masks = jax.nn.one_hot(idx_k, E, dtype=jnp.int32)
            m = jnp.transpose(masks, (1, 0, 2)).reshape(K * T, E)
            locs_full = jnp.cumsum(m, axis=0) - 1
            loc = jnp.sum(locs_full * m, axis=-1)
            loc = loc.reshape(K, T).T
            valid = (loc < cap).astype(xt.dtype)
            loc_c = jnp.clip(loc, 0, cap - 1)
            contrib = (xt[:, None, :] * valid[:, :, None]).reshape(T * K, Dd)
            disp = jnp.zeros((E, cap, Dd), xt.dtype)
            disp = disp.at[idx_k.reshape(-1), loc_c.reshape(-1)].add(contrib)
            h = jax.nn.relu(jnp.einsum('ecd,edh->ech', disp, w1) + b1[:, None, :])
            out = jnp.einsum('ech,ehd->ecd', h, w2) + b2[:, None, :]
            gathered = out[idx_k, loc_c]
            y = jnp.einsum('tk,tkd->td', gates_k * valid, gathered)
            return y.reshape(Bb, Ss, Dd)
        key = jax.random.key(seed)
        ks = jax.random.split(key, 6)
        scale_in = 1.0 / np.sqrt(D)
        scale_h = 1.0 / np.sqrt(H)
        return {'x': jax.random.normal(ks[0], (B, S, D), jnp.float32), 'wg': jax.random.normal(ks[1], (D, E), jnp.float32) * scale_in, 'w1': jax.random.normal(ks[2], (E, D, H), jnp.float32) * scale_in, 'b1': jnp.zeros((E, H), jnp.float32), 'w2': jax.random.normal(ks[3], (E, H, D), jnp.float32) * scale_h, 'b2': jnp.zeros((E, D), jnp.float32)}
    _L0_ffn_all = _L0_ffn_setup()
    _L0_ffn_in = {k: v for k, v in _L0_ffn_all.items() if k in ('wg', 'w1', 'b1', 'w2', 'b2')}
    del _L0_ffn_all

    def _L1_attn_setup():
        import jax, jax.numpy as jnp
        import numpy as np
        B, T, D, C = (4, 1024, 128, 64)
        key = jax.random.key(seed)
        k1, k2, k3 = jax.random.split(key, 3)
        out = jax.random.normal(k1, (B, T, D), jnp.float32)
        W_write = jax.random.normal(k2, (D, D), jnp.float32) / np.float32(np.sqrt(D))
        W_read = jax.random.normal(k3, (D, D), jnp.float32) / np.float32(np.sqrt(D))
        decay = jnp.float32(4.6)
        log_alpha = jnp.log(jnp.float32(0.03))
        return {'out': out, 'W_write': W_write, 'W_read': W_read, 'decay': decay, 'log_alpha': log_alpha}
    _L1_attn_all = _L1_attn_setup()
    _L1_attn_in = {k: v for k, v in _L1_attn_all.items() if k in ('W_write', 'W_read', 'decay', 'log_alpha')}
    del _L1_attn_all

    def _L1_xattn_setup():
        import jax, jax.numpy as jnp
        import numpy as np
        B, T, D = (8, 256, 128)
        key = jax.random.key(seed)
        k1, k2, k3, k4 = jax.random.split(key, 4)
        k = jax.random.normal(k1, (B, T, D), dtype=jnp.float32)
        v = jax.random.normal(k2, (B, T, D), dtype=jnp.float32)
        w = jax.random.uniform(k3, (D,), dtype=jnp.float32, minval=0.0005, maxval=0.008)
        u = 0.1 * jax.random.normal(k4, (D,), dtype=jnp.float32)
        return {'k': k, 'v': v, 'w': w, 'u': u}
    _L1_xattn_all = _L1_xattn_setup()
    _L1_xattn_in = {k: v for k, v in _L1_xattn_all.items() if k in ('w', 'u')}
    del _L1_xattn_all

    def _L1_ffn_setup():
        import jax, jax.numpy as jnp
        import numpy as np
        B, S, D, H, F = (4, 512, 128, 16, 512)
        CAP = 0.125
        ROPE_BASE = 10000.0

        def rmsnorm(x, g):
            return x * jax.lax.rsqrt(jnp.mean(x * x, -1, keepdims=True) + 1e-06) * g

        def rope(t, pos):
            hd = t.shape[-1]
            inv = 1.0 / ROPE_BASE ** (jnp.arange(0, hd, 2, dtype=jnp.float32) / hd)
            f = pos[:, None, :, None].astype(jnp.float32) * inv
            emb = jnp.concatenate([f, f], axis=-1)
            cos, sin = (jnp.cos(emb), jnp.sin(emb))
            rot = jnp.concatenate([-t[..., hd // 2:], t[..., :hd // 2]], axis=-1)
            return t * cos + rot * sin
        key = jax.random.key(seed)
        ks = jax.random.split(key, 9)
        scale = 0.02
        x = jax.random.normal(ks[0], (B, S, D), jnp.float32)
        causal = jnp.where(jnp.tril(jnp.ones((S, S), bool)), 0.0, -1000000000.0).astype(jnp.float32)
        attention_mask = jnp.broadcast_to(causal[None, None], (B, 1, S, S))
        position_ids = jnp.broadcast_to(jnp.arange(S, dtype=jnp.int32), (B, S))
        return {'x': x, 'attention_mask': attention_mask, 'position_ids': position_ids, 'router_w': jax.random.normal(ks[1], (D, 1), jnp.float32) * scale, 'router_b': jnp.zeros((1,), jnp.float32), 'wq': jax.random.normal(ks[2], (D, D), jnp.float32) * scale, 'wk': jax.random.normal(ks[3], (D, D), jnp.float32) * scale, 'wv': jax.random.normal(ks[4], (D, D), jnp.float32) * scale, 'wo': jax.random.normal(ks[5], (D, D), jnp.float32) * scale, 'w1': jax.random.normal(ks[6], (D, F), jnp.float32) * scale, 'w2': jax.random.normal(ks[7], (F, D), jnp.float32) * scale, 'ln1': jnp.ones((D,), jnp.float32), 'ln2': jnp.ones((D,), jnp.float32)}
    _L1_ffn_all = _L1_ffn_setup()
    _L1_ffn_in = {k: v for k, v in _L1_ffn_all.items() if k in ('attention_mask', 'position_ids', 'router_w', 'router_b', 'wq', 'wk', 'wv', 'wo', 'w1', 'w2', 'ln1', 'ln2')}
    del _L1_ffn_all
    return {'x': x, 'ctx_1024': ctx_1024, 'L0_attn_ln1_g': _L0_attn_in['ln1_g'], 'L0_attn_ln1_b': _L0_attn_in['ln1_b'], 'L0_attn_ln2_g': _L0_attn_in['ln2_g'], 'L0_attn_ln2_b': _L0_attn_in['ln2_b'], 'L0_attn_W1': _L0_attn_in['W1'], 'L0_attn_b1': _L0_attn_in['b1'], 'L0_attn_W2': _L0_attn_in['W2'], 'L0_attn_b2': _L0_attn_in['b2'], 'L0_xattn_Wq': _L0_xattn_in['Wq'], 'L0_xattn_bq': _L0_xattn_in['bq'], 'L0_xattn_Wk': _L0_xattn_in['Wk'], 'L0_xattn_bk': _L0_xattn_in['bk'], 'L0_xattn_Wv': _L0_xattn_in['Wv'], 'L0_xattn_bv': _L0_xattn_in['bv'], 'L0_xattn_Wo': _L0_xattn_in['Wo'], 'L0_xattn_bo': _L0_xattn_in['bo'], 'L0_ffn_wg': _L0_ffn_in['wg'], 'L0_ffn_w1': _L0_ffn_in['w1'], 'L0_ffn_b1': _L0_ffn_in['b1'], 'L0_ffn_w2': _L0_ffn_in['w2'], 'L0_ffn_b2': _L0_ffn_in['b2'], 'L1_attn_W_write': _L1_attn_in['W_write'], 'L1_attn_W_read': _L1_attn_in['W_read'], 'L1_attn_decay': _L1_attn_in['decay'], 'L1_attn_log_alpha': _L1_attn_in['log_alpha'], 'L1_xattn_w': _L1_xattn_in['w'], 'L1_xattn_u': _L1_xattn_in['u'], 'L1_ffn_attention_mask': _L1_ffn_in['attention_mask'], 'L1_ffn_position_ids': _L1_ffn_in['position_ids'], 'L1_ffn_router_w': _L1_ffn_in['router_w'], 'L1_ffn_router_b': _L1_ffn_in['router_b'], 'L1_ffn_wq': _L1_ffn_in['wq'], 'L1_ffn_wk': _L1_ffn_in['wk'], 'L1_ffn_wv': _L1_ffn_in['wv'], 'L1_ffn_wo': _L1_ffn_in['wo'], 'L1_ffn_w1': _L1_ffn_in['w1'], 'L1_ffn_w2': _L1_ffn_in['w2'], 'L1_ffn_ln1': _L1_ffn_in['ln1'], 'L1_ffn_ln2': _L1_ffn_in['ln2']}

def reference(x, ctx_1024, L0_attn_ln1_g, L0_attn_ln1_b, L0_attn_ln2_g, L0_attn_ln2_b, L0_attn_W1, L0_attn_b1, L0_attn_W2, L0_attn_b2, L0_xattn_Wq, L0_xattn_bq, L0_xattn_Wk, L0_xattn_bk, L0_xattn_Wv, L0_xattn_bv, L0_xattn_Wo, L0_xattn_bo, L0_ffn_wg, L0_ffn_w1, L0_ffn_b1, L0_ffn_w2, L0_ffn_b2, L1_attn_W_write, L1_attn_W_read, L1_attn_decay, L1_attn_log_alpha, L1_xattn_w, L1_xattn_u, L1_ffn_attention_mask, L1_ffn_position_ids, L1_ffn_router_w, L1_ffn_router_b, L1_ffn_wq, L1_ffn_wk, L1_ffn_wv, L1_ffn_wo, L1_ffn_w1, L1_ffn_w2, L1_ffn_ln1, L1_ffn_ln2):
    import jax
    import jax.numpy as jnp

    def _L0_attn_ref(src, ln1_g, ln1_b, ln2_g, ln2_b, W1, b1, W2, b2):
        import jax, jax.numpy as jnp
        import numpy as np
        H = 16
        W = 32
        D_MODEL = 128
        D_FF = 512
        EPS = 1e-05

        def _layernorm(x, g, b):
            mu = jnp.mean(x, axis=-1, keepdims=True)
            var = jnp.mean(jnp.square(x - mu), axis=-1, keepdims=True)
            return (x - mu) * jax.lax.rsqrt(var + EPS) * g + b

        def _sliding_attn(q, k, v, w):
            B, Hh, S, d = q.shape
            nc = S // w
            qc = q.reshape(B, Hh, nc, w, d)
            kp = jnp.pad(k, ((0, 0), (0, 0), (w, w), (0, 0)))
            vp = jnp.pad(v, ((0, 0), (0, 0), (w, w), (0, 0)))
            idx = (jnp.arange(nc) * w)[:, None] + jnp.arange(3 * w)[None, :]
            kc = kp[:, :, idx, :]
            vc = vp[:, :, idx, :]
            scores = jnp.einsum('bhcqd,bhckd->bhcqk', qc, kc)
            q_pos = jnp.arange(nc)[:, None, None] * w + jnp.arange(w)[None, :, None]
            k_pos = jnp.arange(nc)[:, None, None] * w - w + jnp.arange(3 * w)[None, None, :]
            rel = k_pos - q_pos
            valid = (jnp.abs(rel) <= w) & (k_pos >= 0) & (k_pos < S)
            scores = jnp.where(valid[None, None], scores, jnp.float32(-1000000000.0))
            p = jax.nn.softmax(scores, axis=-1)
            out = jnp.einsum('bhcqk,bhckd->bhcqd', p, vc)
            return out.reshape(B, Hh, S, d)
        B, S, _ = src.shape
        d_head = D_MODEL // H
        qkv = src.reshape(B, S, H, d_head).transpose(0, 2, 1, 3)
        attn = _sliding_attn(qkv, qkv, qkv, W)
        attn = attn.transpose(0, 2, 1, 3).reshape(B, S, D_MODEL)
        x = _layernorm(src + attn, ln1_g, ln1_b)
        ff = jnp.maximum(x @ W1 + b1, 0.0) @ W2 + b2
        return _layernorm(x + ff, ln2_g, ln2_b)

    def _L0_xattn_ref(query, kv, Wq, bq, Wk, bk, Wv, bv, Wo, bo, is_causal):
        import jax, jax.numpy as jnp
        import numpy as np
        B, S, D, H, W = (2, 512, 128, 16, 16)
        HD = D // H
        b, s, d = query.shape

        def split_heads(x):
            return x.reshape(b, s, H, HD).transpose(0, 2, 1, 3)
        Q = split_heads(query @ Wq.T + bq)
        K = split_heads(kv @ Wk.T + bk)
        V = split_heads(kv @ Wv.T + bv)
        pad = W - 1
        Kp = jnp.pad(K, ((0, 0), (0, 0), (pad, 0), (0, 0)))
        Vp = jnp.pad(V, ((0, 0), (0, 0), (pad, 0), (0, 0)))
        idx = jnp.arange(s)[:, None] + jnp.arange(W)[None, :]
        Kw = Kp[:, :, idx]
        Vw = Vp[:, :, idx]
        scores = jnp.einsum('bhsd,bhswd->bhsw', Q, Kw) / np.sqrt(HD).astype(np.float32)
        if is_causal:
            mask = jnp.arange(W)[None, :] <= jnp.arange(s)[:, None]
            scores = jnp.where(mask[None, None], scores, -jnp.inf)
        attn = jax.nn.softmax(scores, axis=-1)
        out = jnp.einsum('bhsw,bhswd->bhsd', attn, Vw)
        out = out.transpose(0, 2, 1, 3).reshape(b, s, d)
        return out @ Wo.T + bo

    def _L0_ffn_ref(x, wg, w1, b1, w2, b2):
        import jax, jax.numpy as jnp
        import numpy as np
        B, S, D = (2, 256, 128)
        E, K, H = (8, 2, 512)
        CAP_FACTOR = 1.0

        def _moe_forward(x, wg, w1, b1, w2, b2):
            Bb, Ss, Dd = x.shape
            T = Bb * Ss
            cap = int(K * CAP_FACTOR * ((T + E - 1) // E))
            xt = x.reshape(T, Dd)
            logits = xt @ wg
            scores = jax.nn.softmax(logits, axis=-1)
            gates_k, idx_k = jax.lax.top_k(scores, K)
            gates_k = gates_k / jnp.sum(gates_k, axis=-1, keepdims=True)
            masks = jax.nn.one_hot(idx_k, E, dtype=jnp.int32)
            m = jnp.transpose(masks, (1, 0, 2)).reshape(K * T, E)
            locs_full = jnp.cumsum(m, axis=0) - 1
            loc = jnp.sum(locs_full * m, axis=-1)
            loc = loc.reshape(K, T).T
            valid = (loc < cap).astype(xt.dtype)
            loc_c = jnp.clip(loc, 0, cap - 1)
            contrib = (xt[:, None, :] * valid[:, :, None]).reshape(T * K, Dd)
            disp = jnp.zeros((E, cap, Dd), xt.dtype)
            disp = disp.at[idx_k.reshape(-1), loc_c.reshape(-1)].add(contrib)
            h = jax.nn.relu(jnp.einsum('ecd,edh->ech', disp, w1) + b1[:, None, :])
            out = jnp.einsum('ech,ehd->ecd', h, w2) + b2[:, None, :]
            gathered = out[idx_k, loc_c]
            y = jnp.einsum('tk,tkd->td', gates_k * valid, gathered)
            return y.reshape(Bb, Ss, Dd)
        return _moe_forward(x, wg, w1, b1, w2, b2)

    def _L1_attn_ref(out, W_write, W_read, decay, log_alpha):
        import jax, jax.numpy as jnp
        import numpy as np
        B, T, D, C = (4, 1024, 128, 64)
        Bd, Td, Dd = out.shape
        nC = Td // C
        out32 = out.astype(jnp.float32)
        gamma = jax.nn.sigmoid(decay)
        log_gamma = jnp.log(gamma)
        v = out32 @ W_write.T
        wk = jnp.pad(out32[:, :-1], ((0, 0), (1, 0), (0, 0)))
        rk = out32
        p = jnp.arange(C)
        diffs = jnp.maximum(p[:, None] - 1 - p[None, :], 0)
        causal = (p[:, None] > p[None, :]).astype(jnp.float32)
        M = jnp.exp(diffs * log_gamma) * causal
        dec_inter = gamma ** p
        gw = gamma ** (C - 1 - p)
        gC = gamma ** C

        def chunk(x):
            return x.reshape(Bd, nC, C, Dd).transpose(1, 0, 2, 3)
        rk_c, wk_c, v_c = (chunk(rk), chunk(wk), chunk(v))

        def body(W, xs):
            r, w, vv = xs
            inter = jnp.einsum('bde,bce->bcd', W, r) * dec_inter[None, :, None]
            S = jnp.einsum('bcd,bed->bce', r, w)
            intra = jnp.einsum('bce,bed->bcd', S * M, vv)
            W_new = gC * W + jnp.einsum('bcd,bce->bde', vv * gw[None, :, None], w)
            return (W_new, inter + intra)
        W0 = jnp.zeros((Bd, Dd, Dd), jnp.float32)
        _, reads = jax.lax.scan(body, W0, (rk_c, wk_c, v_c))
        reads = reads.transpose(1, 0, 2, 3).reshape(Bd, Td, Dd)
        alpha = jnp.exp(log_alpha)
        return out + alpha * (reads @ W_read.T).astype(out.dtype)

    def _L1_xattn_ref(k, v, w, u):
        import jax, jax.numpy as jnp
        import numpy as np
        B, T, D = (8, 256, 128)
        Tn = k.shape[-2]
        kt = jnp.moveaxis(k, -2, 0)
        vt = jnp.moveaxis(v, -2, 0)
        ed = jnp.exp(-w)
        eg = jnp.exp(w)

        def step(carry, xs):
            A, Bm = carry
            kk, vv, t = xs
            out = A + jnp.exp(u + kk) * (vv * Bm + jnp.maximum(t - 1.0, 0.0))
            inc = jnp.where(t == 0.0, 0.0, 1.0)
            A = ed * A + inc * jnp.exp(kk) * vv
            Bm = eg * Bm + inc * jnp.exp(-kk)
            return ((A, Bm), out)
        A0 = jnp.zeros_like(kt[0])
        B0 = jnp.zeros_like(kt[0])
        ts = jnp.arange(Tn, dtype=k.dtype)
        (_, _), out = jax.lax.scan(step, (A0, B0), (kt, vt, ts))
        return jnp.moveaxis(out, 0, -2)

    def _L1_ffn_ref(x, attention_mask, position_ids, router_w, router_b, wq, wk, wv, wo, w1, w2, ln1, ln2):
        import jax, jax.numpy as jnp
        import numpy as np
        B, S, D, H, F = (4, 512, 128, 16, 512)
        CAP = 0.125
        ROPE_BASE = 10000.0

        def rmsnorm(x, g):
            return x * jax.lax.rsqrt(jnp.mean(x * x, -1, keepdims=True) + 1e-06) * g

        def rope(t, pos):
            hd = t.shape[-1]
            inv = 1.0 / ROPE_BASE ** (jnp.arange(0, hd, 2, dtype=jnp.float32) / hd)
            f = pos[:, None, :, None].astype(jnp.float32) * inv
            emb = jnp.concatenate([f, f], axis=-1)
            cos, sin = (jnp.cos(emb), jnp.sin(emb))
            rot = jnp.concatenate([-t[..., hd // 2:], t[..., :hd // 2]], axis=-1)
            return t * cos + rot * sin
        b, s, d = x.shape
        hd = d // H
        weights = (x @ router_w)[..., 0] + router_b[0]
        k = int(CAP * s)
        topv, topi = jax.lax.top_k(weights, k)
        thr = topv[:, -1]
        sel_mask = (weights > thr[:, None]).astype(x.dtype)
        kc = k - 1
        sel_idx = jnp.sort(topi[:, :kc], axis=1)
        bidx = jnp.arange(b)[:, None]
        x_sel = x[bidx, sel_idx]
        pos_sel = position_ids[bidx, sel_idx]
        w_sel = weights[bidx, sel_idx]
        m = attention_mask[:, 0]
        m_sel = m[bidx[:, :, None], sel_idx[:, :, None], sel_idx[:, None, :]]
        hn = rmsnorm(x_sel, ln1)

        def heads(t):
            return t.reshape(b, kc, H, hd).transpose(0, 2, 1, 3)
        q = rope(heads(hn @ wq), pos_sel)
        kk = rope(heads(hn @ wk), pos_sel)
        v = heads(hn @ wv)
        sc = jnp.einsum('bhqd,bhkd->bhqk', q, kk) / np.sqrt(hd).astype(np.float32)
        sc = sc + m_sel[:, None]
        a = jax.nn.softmax(sc, axis=-1)
        o = jnp.einsum('bhqk,bhkd->bhqd', a, v).transpose(0, 2, 1, 3).reshape(b, kc, d) @ wo
        x1 = x_sel + o
        x2 = x1 + jax.nn.gelu(rmsnorm(x1, ln2) @ w1) @ w2
        proc = x2 * w_sel[..., None]
        out = jnp.zeros_like(x).at[bidx, sel_idx].set(proc)
        return out + x * (1.0 - sel_mask)[..., None]
    x = _layernorm(x + _L0_attn_ref(x, L0_attn_ln1_g, L0_attn_ln1_b, L0_attn_ln2_g, L0_attn_ln2_b, L0_attn_W1, L0_attn_b1, L0_attn_W2, L0_attn_b2), axis=-1)
    x = _layernorm(x + _L0_xattn_ref(x, ctx_1024, L0_xattn_Wq, L0_xattn_bq, L0_xattn_Wk, L0_xattn_bk, L0_xattn_Wv, L0_xattn_bv, L0_xattn_Wo, L0_xattn_bo, 1), axis=-1)
    x = _layernorm(x + _L0_ffn_ref(x, L0_ffn_wg, L0_ffn_w1, L0_ffn_b1, L0_ffn_w2, L0_ffn_b2), axis=-1)
    x = _layernorm(x + _L1_attn_ref(x, L1_attn_W_write, L1_attn_W_read, L1_attn_decay, L1_attn_log_alpha), axis=-1)
    x = _layernorm(x + _L1_xattn_ref(x, ctx_1024, L1_xattn_w, L1_xattn_u), axis=-1)
    x = _layernorm(x + _L1_ffn_ref(x, L1_ffn_attention_mask, L1_ffn_position_ids, L1_ffn_router_w, L1_ffn_router_b, L1_ffn_wq, L1_ffn_wk, L1_ffn_wv, L1_ffn_wo, L1_ffn_w1, L1_ffn_w2, L1_ffn_ln1, L1_ffn_ln2), axis=-1)
    return x

_drawn_inputs = setup_inputs


def setup_inputs(seed=0):
    import zlib

    import numpy as np

    out = dict(_drawn_inputs(seed))
    spreads = {'L0_attn_ln1_g': (1.0, 0.2),
     'L0_attn_ln1_b': (0.0, 0.1),
     'L0_attn_ln2_g': (1.0, 0.2),
     'L0_attn_ln2_b': (0.0, 0.1),
     'L0_attn_b1': (0.0, 0.1),
     'L0_attn_b2': (0.0, 0.1),
     'L0_ffn_b1': (0.0, 0.1),
     'L0_ffn_b2': (0.0, 0.1),
     'L1_ffn_ln1': (1.0, 0.6),
     'L1_ffn_ln2': (1.0, 0.6)}
    factors = {'L0_xattn_Wq': 3.826,
     'L0_xattn_bq': 8.0,
     'L0_xattn_Wk': 3.997,
     'L0_xattn_bk': 8.0,
     'L0_xattn_bv': 2.776,
     'L1_ffn_router_w': 8.0,
     'L1_ffn_wq': 8.0,
     'L1_ffn_wk': 8.0,
     'L1_ffn_wv': 8.0,
     'L1_ffn_wo': 8.0,
     'L1_ffn_w1': 8.0,
     'L1_ffn_w2': 8.0}
    for name, (base, spread) in spreads.items():
        noise = np.random.default_rng([zlib.crc32(name.encode()), seed]).standard_normal(out[name].shape)
        drawn = base * np.exp(spread * noise) if base else spread * noise
        out[name] = jnp.asarray(drawn.astype(out[name].dtype))
    for name, factor in factors.items():
        out[name] = (out[name] * factor).astype(out[name].dtype)
    return out
```

```python
from contextlib import ExitStack

import numpy as np
import concourse.bass as bass
from concourse import mybir

F32 = mybir.dt.float32
BF16 = mybir.dt.bfloat16
I32 = mybir.dt.int32
ALU = mybir.AluOpType
ACT = mybir.ActivationFunctionType
AX = mybir.AxisListType.X

B, S, D = 32, 64, 128
T = B * S
P = 128
NT = T // P
NQ = NT // 4
H, HD = 16, 8
F = 512
FC = F // P
E, TOPK = 8, 2
CAP = TOPK * ((T + E - 1) // E)
LN_EPS = 1e-5
RMS_EPS = 1e-6
NEG = -1e30
KEEP = int(0.125 * S)
NSEL = KEEP - 1
BPS = P // KEEP
NS = B // BPS
BT = NT // NS
VW = 2 * (HD + 1)


def constants():
    p = np.arange(P)
    pos, seq = p % S, p // S
    k = np.arange(S)
    c = {}
    c["ident"] = np.eye(P)
    c["band"] = np.where(np.abs(pos[:, None] - k[None, :]) <= 32, 0.0, NEG)
    W = 16
    ok = (k[None] <= pos[:, None]) & (k[None] >= pos[:, None] - (W - 1)) & (k[None] <= 2 * pos[:, None] - (W - 1))
    c["window"] = np.where(ok, 0.0, NEG)
    npad = np.where(pos < W - 1, np.minimum(pos + 1, W - 1 - pos), 0)
    c["npad"] = npad[:, None]
    c["pad_ceiling"] = np.where(npad > 0, 0.0, -NEG)[:, None]
    c["head_of_row"] = ((p % 64)[:, None] // HD == np.arange(8)[None])
    c["earlier_row"] = p[:, None] < p[None, :]
    c["ones"] = np.ones((P, P))
    c["fold"] = pos[:, None] == k[None]
    for b in (0, 1):
        c[f"dup{b}"] = (seq[:, None] == b) & (pos[:, None] == pos[None, :])
    same = seq[:, None] == seq[None, :]
    c["same_seq"] = same
    c["same_seq_before"] = same & (p[None, :] < p[:, None])
    c["row_index"] = np.tile(p[None, :], (P, 1))
    c["decay_steps"] = np.maximum(p[None, :] - 2 - p[:, None], 0)
    c["causal"] = same & (p[None, :] > p[:, None] + 1)
    c["steps"] = np.tile(np.maximum(k - 1.0, 0.0)[None], (P, 8))
    c["carry"] = np.tile((k > 0)[None], (P, 8))
    c["first_choice"] = np.tile(E - np.arange(E)[None], (P, 1))
    c["slot_base"] = KEEP * ((2 * np.arange(NT)[None] + seq[:, None]) % BPS) + 1
    sp, sk = p % 64, k
    c["slot_block"] = np.where((sp[:, None] // KEEP == sk[None] // KEEP) & (sk[None] % KEEP < NSEL), 0.0, NEG)
    c["inv_freq"] = np.tile((1.0 / np.float32(10000.0) ** (np.arange(0, HD, 2, dtype=np.float32) / np.float32(HD)))[None], (P, 1))
    c["scan_carry"] = np.tile((np.arange(2 * NT) > 0)[None], (P, E))
    at, cols = {}, []
    n = 0
    for name, a in c.items():
        a = np.asarray(a, np.float32)
        at[name] = (n, a.shape[1])
        n += a.shape[1]
        cols.append(a)
    return at, np.ascontiguousarray(np.concatenate(cols, 1))


CONST_AT, CONST = constants()


def build(nc, io):
    with ExitStack() as ctx:
        def sb(name, shape, dt=F32):
            return ctx.enter_context(nc.sbuf_tensor(name, [P] + shape, dt))

        def sem(name):
            return ctx.enter_context(nc.semaphore(name))

        x_tok = sb("x_tok", [NT, D])
        x_side = sb("x_side", [NT, D])
        work = sb("work", [NT, D])
        xT = sb("xT", [T + 1])
        ctxT = sb("ctxT", [T])
        q_diag = sb("q_diag", [NT, 2, P])
        k_comp = sb("k_comp", [NT, 2, S])
        v_pair = sb("v_pair", [B, H // 2, VW])
        k_heads = sb("k_heads", [2, 2, 8, S])
        probs = sb("probs", [2, H * S])
        probsT = sb("probsT", [2, H * S])
        neg_max = sb("neg_max", [2, H])
        neg_max0 = sb("neg_max0", [4, H])
        pad_exp = sb("pad_exp", [4, H])
        denom = sb("denom", [2, H])
        r_denom = sb("r_denom", [2, H])
        stats = sb("stats", [NT, 6])
        mv = sb("mv", [NT, 2])
        var_e = sb("var_e", [NT, 1])
        rstd = sb("rstd", [NT, 1])
        neg_half = sb("neg_half", [NT])
        con = sb("con", [CONST.shape[1]])
        ident_bf = sb("ident_bf", [P], BF16)
        mask_bf = sb("mask_bf", [2, S], BF16)
        rows = sb("rows", [8, D])
        cols = sb("cols", [64])
        aw1 = sb("aw1", [F])
        aw2 = sb("aw2", [FC, D])
        wq = sb("wq", [D])
        wk = sb("wk", [D])
        wv = sb("wv", [D])
        wo = sb("wo", [D])
        wg = sb("wg", [E])
        mw1 = sb("mw1", [E, F])
        mw2 = sb("mw2", [E, FC, D])
        mb1 = sb("mb1", [E, FC])
        mb2 = sb("mb2", [D])
        hT = sb("hT", [2, FC, 512])

        hT_flat = hT[:, :, :, :].rearrange("p a f n -> p (a f n)")
        wcomb = sb("wcomb", [4 * P])
        decay = sb("decay", [P])
        seq_mask = sb("seq_mask", [3, P])
        pos_i = sb("pos_i", [NT], I32)
        w_pos = sb("w_pos", [2, NT])
        fqkv = sb("fqkv", [3 * D])
        wqkv = sb("wqkv", [3 * D])
        fwo = sb("fwo", [D])
        fw1 = sb("fw1", [F])
        fw2 = sb("fw2", [FC, D])
        slot_x0 = sb("slot_x0", [NS, D])
        slot_x = sb("slot_x", [NS, D])
        slot_wp = sb("slot_wp", [2 * NS])
        slot_mask = sb("slot_mask", [NS, S])
        slot_s = sb("slot_s", [8])
        slot_angle = sb("slot_angle", [2, NS, 4])
        slot_trig = sb("slot_trig", [2, NS, 4])
        routing = sb("routing", [2048])
        ROUTE = {"onehot": 0, "logits": 256, "eq": 384, "gate": 512, "tot": 640, "run": 896, "at": 1152, "m0": 1408,
                 "m1": 1424, "c": 1440, "e": 1456, "gt": 1472, "tie": 1488, "ge": 1504}

        def route(name, n):
            return routing[:, ROUTE[name]:ROUTE[name] + n]

        def sel(t):
            return mw1[:, t // 4, (t % 4) * P:(t % 4 + 1) * P]

        def selT(t):
            return mw1[:, 4 + t // 4, (t % 4) * P:(t % 4 + 1) * P]

        def rope_z(g, which, half):
            at = 3072 + g * 512 + which * 256 + half * P
            return hT_flat[:, at:at + P]

        def scrap(i):
            return probsT[:, :, :].rearrange("p a n -> p (a n)")[:, i * P:(i + 1) * P]

        def seqs(ap):
            return ap.rearrange("p (b s) -> p b s", s=S)

        def rec_b(q, i):
            return hT[:, q % 2, i]

        def con_at(name):
            a, n = CONST_AT[name]
            return con[:, a:a + n]

        ident = con_at("ident")
        COL = {"bq": 0, "bk": 2, "b1": 4, "u": 8, "w": 9, "ln1": 10, "ln2": 11, "router": 12, "decay": 13,
               "log_alpha": 14, "router_b": 15, "half_alpha": 16, "log_gamma": 17, "ed": 18, "eg": 19, "t": 20, "t2": 21, "t3": 22}

        def col(name, n=1):
            return cols[:, COL[name]:COL[name] + n]

        bank = ctx.enter_context(nc.psum_tensor("bank", [P, 8, 512], F32))

        s_con = sem("s_con")
        s_x = sem("s_x")
        s_attn_in = sem("s_attn_in")
        s_w = sem("s_w")
        s_w2 = sem("s_w2")
        s_out = sem("s_out")
        s_setup = sem("s_setup")
        stage_end = sem("stage_end")
        s_dve = sem("s_dve")
        s_pool = sem("s_pool")
        s_act = sem("s_act")
        s_pe = sem("s_pe")

        def names(stage, *what):
            return {n: sem(f"{stage}_{n}") for n in what}

        class Chain:
            def __init__(self, eng, s):
                self.eng, self.s, self.n = eng, s, 0

            def __call__(self, ins):
                self.n += 1
                ins.then_inc(self.s, 1)
                self.eng.wait_ge(self.s, self.n)

        def end_stage(eng, n):
            eng.drain().then_inc(stage_end, 1)
            eng.wait_ge(stage_end, 4 * n)

        ATT = ("spread", "scores", "shifted", "exp", "transposed", "evacuated", "weighted", "taken", "max", "pad")
        att = {s: names(s, *ATT) for s in ("self", "cross", "slots")}
        LNS = ("stats", "rstd", "y", "yT", "yT_out")
        ln = {s: names(s, *LNS) for s in ("ln1", "ln2", "ln3", "ln4", "ln5", "ln6", "ln7", "ln8")}
        s_h, s_hT, s_o, s_o_free, s_h_free = (sem(n) for n in ("ffn_h", "ffn_hT", "ffn_out", "ffn_out_free", "ffn_h_free"))
        s_mh, s_mhT, s_mo, s_mo_free, s_mh_free = (sem(n) for n in ("moe_h", "moe_hT", "moe_out", "moe_out_free", "moe_h_free"))
        s_side = sem("s_side")
        s_qkv, s_qv_free, s_k_free = sem("s_qkv"), sem("s_qv_free"), sem("s_k_free")
        s_oT, s_oTs, s_wo, s_wo_free = sem("s_oT"), sem("s_oTs"), sem("s_wo"), sem("s_wo_free")
        s_r = names("route", "logits", "chosen", "ranks", "gap", "exp", "gates", "gatesT", "gatesT_sb", "bias")
        s_lin = names("lin", "w", "w_sb", "consts", "one_plus", "scores", "masked", "v", "v_sb", "read", "taken")
        s_rec = names("rec", "ready", "rates", "exp", "ekv", "sum", "tok", "taken")
        s_sel = names("sel", "weights", "wcol", "rows", "ranked", "sel", "half", "half_sb", "gathered", "turned", "selT", "back")
        s_slot = names("slot", "squares", "rms", "hn", "pe", "act", "angle", "trig", "rope", "keys", "values")

        block = ctx.enter_context(nc.Block())

        def head_view(ap):
            return ap.rearrange("p (h k) -> p h k", k=S)

        o_view = bank[:, 6, 0:H * (HD + 1)].rearrange("p (h e) -> p h e", e=HD + 1)

        def att_spread(pool, s, n):
            hm = con_at("head_of_row")[:, None, :, None].to_broadcast([P, 2, 8, S])
            for i in range(n):
                if i >= 2:
                    pool.wait_ge(s["scores"], i - 1)
                nc.gpsimd.tensor_tensor(k_heads[:, i % 2], k_comp[:, i, :, None, :].to_broadcast([P, 2, 8, S]),
                                        hm, ALU.mult).then_inc(s["spread"], 1)

        def att_pe(pe, s, n, mask_lhs, mask_of):
            def scores(i):
                pe.wait_ge(s["spread"], i + 1)
                if i >= 2:
                    pe.wait_ge(s["shifted"], i - 1)
                for g in (0, 1):
                    out = bank[:, 2 * (i % 2) + g, :]
                    nc.tensor.matmul(out, q_diag[:, i, g], k_heads[:, i % 2, g].rearrange("p h k -> p (h k)"),
                                     start=True, stop=False)
                    last = nc.tensor.matmul(out, mask_lhs, mask_of(i), start=False, stop=True)
                last.then_inc(s["scores"], 1)

            def turn(i):
                pe.wait_ge(s["exp"], i + 1)
                if i >= 1:
                    pe.wait_ge(s["evacuated"], i)
                for hp in range(H // 2):
                    last = nc.tensor.transpose(bank[:, 4 + hp // 4, (hp % 4) * P:(hp % 4 + 1) * P],
                                               probs[:, i % 2, hp * P:(hp + 1) * P], ident)
                last.then_inc(s["transposed"], 1)

            def weigh(i):
                pe.wait_ge(s["evacuated"], i + 1)
                if i >= 1:
                    pe.wait_ge(s["taken"], i)
                for b in (0, 1):
                    for hp in range(H // 2):
                        at = hp * P + b * S
                        last = nc.tensor.matmul(bank[b * S:(b + 1) * S, 6, hp * VW:(hp + 1) * VW],
                                                probsT[:, i % 2, at:at + S], v_pair[:, 2 * i + b, hp],
                                                start=True, stop=True)
                last.then_inc(s["weighted"], 1)

            for i in range(n + 2):
                if i < n:
                    scores(i)
                if 1 <= i <= n:
                    turn(i - 1)
                if i >= 2:
                    weigh(i - 2)

        def att_act(act, s, n, pad):
            def evac(i):
                act.wait_ge(s["transposed"], i + 1)
                if i >= 2:
                    act.wait_ge(s["weighted"], i - 1)
                nc.scalar.copy(probsT[:, i % 2], bank[:, 4:6, :].rearrange("p a n -> p (a n)")).then_inc(s["evacuated"], 1)

            for i in range(n):
                if i >= 1:
                    evac(i - 1)
                if pad:
                    act.wait_ge(s["max"], i + 1)
                    if i >= 4:
                        act.wait_ge(s["taken"], i - 3)
                    nc.scalar.activation(pad_exp[:, i % 4], neg_max0[:, i % 4], ACT.Exp).then_inc(s["pad"], 1)
                act.wait_ge(s["shifted"], i + 1)
                nc.scalar.activation(probs[:, i % 2], probs[:, i % 2], ACT.Exp).then_inc(s["exp"], 1)
            evac(n - 1)

        def att_dve(dve, s, n, pad, link):
            def shift(i):
                m = neg_max[:, i % 2]
                sc = bank[:, 2 * (i % 2):2 * (i % 2) + 2, :].rearrange("p a (h k) -> p (a h) k", k=S)
                dve.wait_ge(s["scores"], i + 1)
                link(nc.vector.tensor_reduce(m, sc, AX, ALU.max, negate=True))
                if pad:
                    link(nc.vector.tensor_scalar(m, m, con_at("pad_ceiling"), None, ALU.min))
                    if i >= 4:
                        dve.wait_ge(s["pad"], i - 3)
                    nc.vector.tensor_scalar(neg_max0[:, i % 4], m, 0.0, None, ALU.min).then_inc(s["max"], 1)
                if i >= 2:
                    dve.wait_ge(s["transposed"], i - 1)
                nc.vector.tensor_tensor(head_view(probs[:, i % 2]), sc, m[:, :, None].to_broadcast([P, H, S]),
                                        ALU.add).then_inc(s["shifted"], 1)

            def take(i):
                d, r = denom[:, i % 2], r_denom[:, i % 2]
                dve.wait_ge(s["weighted"], i + 1)
                if pad:
                    dve.wait_ge(s["pad"], i + 1)
                    link(nc.vector.scalar_tensor_tensor(d, pad_exp[:, i % 4], con_at("npad"), o_view[:, :, HD],
                                                        ALU.mult, ALU.add))
                    link(nc.vector.reciprocal(r, d))
                else:
                    link(nc.vector.reciprocal(r, o_view[:, :, HD]))
                nc.vector.tensor_tensor(work[:, i].rearrange("p (h d) -> p h d", d=HD), o_view[:, :, 0:HD],
                                        r[:, :, None].to_broadcast([P, H, HD]), ALU.mult).then_inc(s["taken"], 1)

            for i in range(n + 2):
                if i < n:
                    shift(i)
                if i >= 2:
                    take(i - 2)

        def ln_stats(s, t):
            def f(link):
                link(nc.vector.bn_stats(stats[:, t], work[:, t]))
                nc.vector.bn_aggr(mv[:, t], stats[:, t]).then_inc(s["stats"], 1)
            return f

        def ln_apply(dve, s, t, out):
            dve.wait_ge(s["rstd"], t + 1)
            return nc.vector.tensor_scalar(out, work[:, t], mv[:, t, 0:1], rstd[:, t], ALU.subtract, ALU.mult)

        def ln_dve(dve, s, link, head, tail, lag=2):
            for t in range(NT + lag):
                if t < NT:
                    head(t)
                    ln_stats(s, t)(link)
                if t >= lag:
                    tail(t - lag)

        def rstd_of(pool, s, t, link, eps=LN_EPS):
            pool.wait_ge(s["stats"], t + 1)
            link(nc.gpsimd.tensor_scalar(var_e[:, t], mv[:, t, 1:2], eps, None, ALU.add))
            nc.gpsimd.tensor_tensor(rstd[:, t], var_e[:, t], neg_half[:, t:t + 1], ALU.pow).then_inc(s["rstd"], 1)

        def ln_pool(pool, s, link, eps=LN_EPS):
            for t in range(NT):
                rstd_of(pool, s, t, link, eps)

        def ln_pe(pe, s, quad, banks, src):
            bk = banks[quad % 2]
            if quad >= 2:
                pe.wait_ge(s["yT_out"], quad - 1)
            for j in range(4):
                t = 4 * quad + j
                pe.wait_ge(s["y"], t + 1)
                last = nc.tensor.transpose(bank[:, bk, j * P:(j + 1) * P], src[:, t], ident)
            last.then_inc(s["yT"], 1)

        def ln_act(act, s, quad, banks):
            act.wait_ge(s["yT"], quad + 1)
            nc.scalar.copy(xT[:, quad * 512:(quad + 1) * 512], bank[:, banks[quad % 2], :]).then_inc(s["yT_out"], 1)

        LOADS = ((rows[:, :, :], "rows"), (cols[:, 0:16], "cols"), (aw1[:, :], "L0_attn_W1"),
                 (aw2[:, :, :], "L0_attn_W2"), (wq[:, :], "wq"), (wk[:, :], "wk"), (wv[:, :], "wv"),
                 (wo[:, :], "wo"), (wg[:, :], "L0_ffn_wg"), (ctxT[:, :], "ctxT"), (mw1[:, :, :], "mw1"),
                 (mw2[:, :, :, :], "mw2"), (mb1[:, :, :], "mb1"), (mb2[0:E, :], "L0_ffn_b2"),
                 (wcomb[:, 0:2 * P], "w_read_write"), (seq_mask[:, :, :], "seq_mask"), (pos_i[:, :], "pos"),
                 (fqkv[:, :], "fqkv"), (fwo[:, :], "L1_ffn_wo"), (fw1[:, :], "L1_ffn_w1"), (fw2[:, :, :], "fw2"))
        N_W = len(LOADS)

        @block.sync
        def _(sp):
            sp.dma_start(con[:, :], io["const"]).then_inc(s_con, 16)
            sp.dma_start(k_comp[:, :, :, :], io["k_self"]).then_inc(s_attn_in, 16)
            sp.dma_start(q_diag[:, :, :, :], io["q_self"]).then_inc(s_attn_in, 16)
            sp.dma_start(v_pair[:, :, :, :], io["v_self"]).then_inc(s_attn_in, 16)
            sp.dma_start(x_tok[:, :, :], io["x"]).then_inc(s_x, 16)
            for dst, src in LOADS:
                sp.dma_start(dst, io[src]).then_inc(s_w, 16)
            sp.wait_ge(s_w, 16 * N_W)
            sp.wait_ge(s_x, 16)
            for q in range(NQ):
                sp.wait_ge(ln["ln8"]["y"], 4 * q + 4)
                sp.dma_start(io["out"][:, 4 * q:4 * q + 4], x_tok[:, 4 * q:4 * q + 4]).then_inc(s_out, 16)
            sp.wait_ge(s_out, 16 * NQ)

        @block.gpsimd
        def _(pool):
            link = Chain(pool, s_pool)
            tt, ts = nc.gpsimd.tensor_tensor, nc.gpsimd.tensor_scalar
            link(nc.gpsimd.memset(neg_half[:, :], -0.5))
            nc.gpsimd.memset(xT[:, T:T + 1], 0.0).then_inc(s_setup, 1)
            pool.wait_ge(s_con, 16)
            pool.wait_ge(s_attn_in, 48)
            att_spread(pool, att["self"], NT)
            end_stage(pool, 1)
            ln_pool(pool, ln["ln1"], link)
            end_stage(pool, 2)
            for q in range(NQ):
                side = x_side[:, 4 * q:4 * q + 4]
                tt(side, side, rows[:, 4:5].to_broadcast([P, 4, D]), ALU.add).then_inc(s_side, 1)
            for t in range(NT + 2):
                if t < NT:
                    rstd_of(pool, ln["ln2"], t, link)
                if t >= 2:
                    rstd_of(pool, ln["ln3"], t - 2, link)
            end_stage(pool, 3)
            for q in range(NQ):
                tt(x_side[:, 4 * q:4 * q + 4], x_tok[:, 4 * q:4 * q + 4], rows[:, 6:7].to_broadcast([P, 4, D]),
                   ALU.add)
            end_stage(pool, 4)
            att_spread(pool, att["cross"], NT)
            end_stage(pool, 5)
            ln_pool(pool, ln["ln4"], link)
            end_stage(pool, 6)
            end_stage(pool, 7)
            ln_pool(pool, ln["ln5"], link)
            end_stage(pool, 8)
            ln_pool(pool, ln["ln6"], link, LN_EPS / 4)
            end_stage(pool, 9)
            for q in range(NQ):
                if q >= 2:
                    pool.wait_ge(s_rec["sum"], q - 1)
                pool.wait_ge(s_rec["exp"], q + 1)
                tt(seqs(rec_b(q, 1))[:, :, 2:S], seqs(rec_b(q, 0))[:, :, 1:S - 1],
                   seqs(ctxT[:, q * 512:(q + 1) * 512])[:, :, 1:S - 1], ALU.mult).then_inc(s_rec["ekv"], 1)
                if q >= 1:
                    for t in range(4 * q - 4, 4 * q):
                        rstd_of(pool, ln["ln7"], t, link)
            for t in range(NT - 4, NT):
                rstd_of(pool, ln["ln7"], t, link)
            end_stage(pool, 10)
            end_stage(pool, 11)
            def rms(n):
                pool.wait_ge(s_slot["squares"], n)
                link(ts(slot_s[:, 2:4], slot_s[:, 0:2], 1.0 / D, RMS_EPS, ALU.mult, ALU.add))
                tt(slot_s[:, 4:6], slot_s[:, 2:4], neg_half[:, 0:2], ALU.pow).then_inc(s_slot["rms"], 1)
            rms(1)
            pool.wait_ge(s_slot["keys"], 1)
            att_spread(pool, att["slots"], NS)
            rms(2)
            end_stage(pool, 12)
            ln_pool(pool, ln["ln8"], link)
            end_stage(pool, 13)

        @block.tensor
        def _(pe):
            mm, tr = nc.tensor.matmul, nc.tensor.transpose

            def cols4(bk, j, n=P):
                return bank[:, bk, j * n:(j + 1) * n]

            pe.wait_ge(s_con, 16)
            pe.wait_ge(s_attn_in, 48)
            pe.wait_ge(s_setup, 3)
            mb = lambda j: (lambda i: mask_bf[:, j, None, :].to_broadcast([P, 8, S]))
            att_pe(pe, att["self"], NT, ident_bf[:, :], mb(0))
            end_stage(pe, 1)
            for q in range(NQ):
                ln_pe(pe, ln["ln1"], q, (0, 1), x_side)
            end_stage(pe, 2)
            pe.wait_ge(s_w, 16 * N_W)
            for q in range(NQ + 1):
                if q < NQ:
                    for f in range(FC):
                        if q >= 1:
                            pe.wait_ge(s_hT, FC * (q - 1) + f + 1)
                        mm(bank[:, f], aw1[:, f * P:(f + 1) * P], xT[:, q * 512:(q + 1) * 512], start=True, stop=True)\
                            .then_inc(s_h, 1)
                if q >= 1:
                    u = q - 1
                    pe.wait_ge(s_hT, FC * u + FC)
                    if u >= 2:
                        pe.wait_ge(s_o_free, 4 * (u - 1))
                    for j in range(4):
                        for f in range(FC):
                            last = mm(cols4(4 + u % 2, j), hT[:, u % 2, f, j * P:(j + 1) * P], aw2[:, f],
                                      start=f == 0, stop=f == FC - 1)
                        last.then_inc(s_o, 1)
                if q >= 2:
                    ln_pe(pe, ln["ln3"], q - 2, (6, 7), x_tok)
            ln_pe(pe, ln["ln3"], NQ - 1, (6, 7), x_tok)
            end_stage(pe, 3)
            for q in range(NQ):
                b0 = 4 * (q % 2)
                if q >= 2:
                    pe.wait_ge(s_qv_free, q - 1)
                    pe.wait_ge(s_k_free, q - 1)
                for w, src, bk in ((wq, xT, b0), (wk, ctxT, b0 + 1)):
                    sv = src[:, q * 512:(q + 1) * 512].rearrange("p (t b s) -> p t b s", b=2, s=S)
                    for g in (0, 1):
                        for b in (0, 1):
                            mm(bank[b * 64:(b + 1) * 64, bk, g * 256:(g + 1) * 256], w[:, g * 64:(g + 1) * 64],
                               sv[:, :, b, :], start=True, stop=True)
                for j in range(8):
                    at = (8 * q + j) * S
                    for h in (0, 1):
                        last = mm(bank[h * 64:(h + 1) * 64, b0 + 2, j * 64:(j + 1) * 64], ctxT[:, at:at + S],
                                  wv[:, :].rearrange("p (a h e) -> p a h e", h=2, e=HD)[:, :, h], start=True, stop=True)
                last.then_inc(s_qkv, 1)
            end_stage(pe, 4)
            att_pe(pe, att["cross"], NT, ident_bf[:, :], mb(1))
            end_stage(pe, 5)
            for q in range(NQ + 3):
                if q < NQ:
                    if q >= 2:
                        pe.wait_ge(s_oTs, q - 1)
                    for j in range(4):
                        last = tr(cols4(q % 2, j), work[:, 4 * q + j], ident)
                    last.then_inc(s_oT, 1)
                if 1 <= q <= NQ:
                    u = q - 1
                    pe.wait_ge(s_oTs, u + 1)
                    if u >= 2:
                        pe.wait_ge(s_wo_free, 4 * (u - 1))
                    for j in range(4):
                        mm(cols4(2 + u % 2, j), probsT[:, u % 2, j * P:(j + 1) * P], wo[:, :], start=True, stop=True)\
                            .then_inc(s_wo, 1)
                if 2 <= q <= NQ + 1:
                    ln_pe(pe, ln["ln4"], q - 2, (4, 5), x_tok)
                if q >= 3:
                    u = q - 3
                    pe.wait_ge(ln["ln4"]["yT_out"], u + 1)
                    for t in range(4 * u, 4 * u + 4):
                        last = mm(bank[:, 6, t * E:(t + 1) * E], xT[:, t * P:(t + 1) * P], wg[:, :], start=True, stop=True)
            last.then_inc(s_r["logits"], 1)
            end_stage(pe, 6)
            pe.wait_ge(s_r["chosen"], 1)
            oh = route("onehot", 2 * NT * E)
            mm(bank[:, 0, 0:256], con_at("earlier_row"), oh, start=True, stop=True).then_inc(s_r["ranks"], 1)
            mm(bank[:, 1, 0:256], con_at("ones"), oh, start=True, stop=True).then_inc(s_r["ranks"], 1)
            pe.wait_ge(s_r["gates"], 1)
            for q in range(NQ):
                for j in range(4):
                    last = tr(bank[0:E, 2 + q, j * P:(j + 1) * P], route("gate", NT * E)[:, (4 * q + j) * E:(4 * q + j + 1) * E],
                              ident)
                last.then_inc(s_r["gatesT"], 1)
            for q in range(NQ):
                bk = (6, 7, 2, 3)[q]
                pe.wait_ge(s_r["gatesT_sb"], q + 1)
                for j in range(4):
                    t = 4 * q + j
                    last = mm(cols4(bk, j), hT_flat[0:E, t * P:(t + 1) * P], mb2[0:E, :], start=True, stop=True)
                last.then_inc(s_r["bias"], 1)
            end_stage(pe, 7)
            for u in range(NQ * E + 1):
                q, e = u // E, u % E
                if u < NQ * E:
                    for f in range(FC):
                        if u >= 1:
                            pe.wait_ge(s_mhT, FC * (u - 1) + f + 1)
                        mm(bank[:, f], mw1[:, e, f * P:(f + 1) * P], xT[:, q * 512:(q + 1) * 512], start=True, stop=True)\
                            .then_inc(s_mh, 1)
                if u >= 1:
                    v = u - 1
                    pe.wait_ge(s_mhT, FC * v + FC)
                    if v >= 2:
                        pe.wait_ge(s_mo_free, v - 1)
                    for j in range(4):
                        for f in range(FC):
                            last = mm(cols4(4 + v % 2, j), hT[:, v % 2, f, j * P:(j + 1) * P], mw2[:, v % E, f],
                                      start=f == 0, stop=f == FC - 1)
                    last.then_inc(s_mo, 1)
                if u % E == 2 and u > E:
                    ln_pe(pe, ln["ln5"], u // E - 1, (6, 7), x_tok)
            ln_pe(pe, ln["ln5"], NQ - 1, (6, 7), x_tok)
            end_stage(pe, 8)
            tr(bank[:, 7, 0:P], wcomb[:, P:2 * P], ident).then_inc(s_lin["w"], 1)
            pe.wait_ge(s_lin["w_sb"], 1)
            mm(bank[:, 6, 0:P], wcomb[:, 0:P], wcomb[:, 2 * P:3 * P], start=True, stop=True).then_inc(s_lin["w"], 1)
            pe.wait_ge(s_lin["w_sb"], 2)
            for q in range(NQ + 2):
                if q < NQ:
                    if q >= 2:
                        pe.wait_ge(s_lin["masked"], q - 1)
                        pe.wait_ge(s_lin["v_sb"], q - 1)
                    for j in range(4):
                        at = (4 * q + j) * P
                        last = mm(cols4(q % 2, j), xT[:, at:at + P], xT[:, at:at + P], start=True, stop=True)
                    last.then_inc(s_lin["scores"], 1)
                    for j in range(4):
                        at = (4 * q + j) * P
                        last = mm(cols4(2 + q % 2, j), xT[:, at + 1:at + P + 1], wcomb[:, 3 * P:4 * P], start=True, stop=True)
                    last.then_inc(s_lin["v"], 1)
                if 1 <= q <= NQ:
                    u = q - 1
                    pe.wait_ge(s_lin["masked"], u + 1)
                    pe.wait_ge(s_lin["v_sb"], u + 1)
                    if u >= 2:
                        pe.wait_ge(s_lin["taken"], 4 * (u - 1))
                    for j in range(4):
                        mm(cols4(4 + u % 2, j), probs[:, u % 2, j * P:(j + 1) * P], probsT[:, u % 2, j * P:(j + 1) * P],
                           start=True, stop=True).then_inc(s_lin["read"], 1)
                if q >= 2:
                    ln_pe(pe, ln["ln6"], q - 2, (6, 7), x_tok)
            end_stage(pe, 9)
            for q in range(NQ + 1):
                if q < NQ:
                    pe.wait_ge(s_rec["sum"], q + 1)
                    if q >= 2:
                        pe.wait_ge(s_rec["taken"], q - 1)
                    for j in range(4):
                        last = tr(cols4(q % 2, j), probsT[:, q % 2, j * P:(j + 1) * P], ident)
                    last.then_inc(s_rec["tok"], 1)
                if q >= 1:
                    ln_pe(pe, ln["ln7"], q - 1, (2, 3), x_tok)
            end_stage(pe, 10)
            for t in range(NT):
                last = mm(bank[:, 0, t:t + 1], xT[:, t * P:(t + 1) * P], col("router"), start=True, stop=True)
            last.then_inc(s_sel["weights"], 1)
            pe.wait_ge(s_sel["wcol"], 1)
            for q in range(NQ):
                if q >= 2:
                    pe.wait_ge(s_sel["ranked"], 4 * (q - 1))
                for j in range(4):
                    t = 4 * q + j
                    last = tr(cols4(1 + q % 2, j), w_pos[:, 0, t:t + 1].to_broadcast([P, P]), ident)
                last.then_inc(s_sel["rows"], 1)
            for t in range(NT):
                g, i = t // BT, t % BT
                pe.wait_ge(s_sel["sel"], t + 1)
                mm(bank[:, 3, g * P:(g + 1) * P], sel(t), x_tok[:, t], start=i == 0, stop=i == BT - 1)
            for t in range(NT):
                g, i = t // BT, t % BT
                mm(bank[:, 4, 2 * g:2 * g + 2], sel(t), w_pos[:, :, t], start=i == 0, stop=i == BT - 1)
            for q in range(NQ + 1):
                if q < NQ:
                    if q >= 2:
                        pe.wait_ge(s_sel["half_sb"], q - 1)
                    for j in range(4):
                        t = 4 * q + j
                        last = mm(cols4(5 + q % 2, j), seq_mask[:, min(t, 2)], sel(t), start=True, stop=True)
                    last.then_inc(s_sel["half"], 1)
                if q >= 1:
                    pe.wait_ge(s_sel["half_sb"], q)
                    for j in range(4):
                        t = 4 * (q - 1) + j
                        g, i = t // BT, t % BT
                        last = mm(bank[:, 7, g * P:(g + 1) * P], probs[:, (q - 1) % 2, j * P:(j + 1) * P], sel(t),
                                  start=i == 0, stop=i == BT - 1)
            last.then_inc(s_sel["gathered"], 1)
            pe.wait_ge(s_sel["ranked"], NT)
            for q in range(NQ):
                bk = (0, 1, 2, 0)[q]
                if q == 3:
                    pe.wait_ge(s_sel["selT"], 1)
                for j in range(4):
                    last = tr(cols4(bk, j), sel(4 * q + j), ident)
                last.then_inc(s_sel["turned"], 1)
            end_stage(pe, 11)
            pe.wait_ge(s_slot["hn"], 1)
            for g in range(NS):
                last = tr(cols4(0, g), hT_flat[:, g * P:(g + 1) * P], ident)
            last.then_inc(s_slot["pe"], 1)
            pe.wait_ge(s_slot["act"], 1)
            for g in range(NS):
                last = mm(bank[:, 1 + g, 0:3 * D], hT_flat[:, 256 + g * P:256 + (g + 1) * P], wqkv[:, :], start=True, stop=True)
            last.then_inc(s_slot["pe"], 1)
            pe.wait_ge(s_slot["rope"], 1)
            for g in range(NS):
                for half in (0, 1):
                    tr(cols4(3, 2 * g + half), rope_z(g, 0, half), ident)
                    last = mm(cols4(4, 2 * g + half, S), rope_z(g, 1, half), con_at("fold"), start=True, stop=True)
            pe.wait_ge(s_slot["act"], 2)
            for g in range(NS):
                for b in (0, 1):
                    last = mm(cols4(5, 2 * g + b), con_at(f"dup{b}"), hT_flat[:, 512 + g * P:512 + (g + 1) * P], start=True, stop=True)
            last.then_inc(s_slot["pe"], 1)
            pe.wait_ge(s_slot["keys"], 1)
            pe.wait_ge(s_slot["values"], 1)
            att_pe(pe, att["slots"], NS, ident, lambda i: slot_mask[:, i, None, :].to_broadcast([P, 8, S]))
            pe.wait_ge(att["slots"]["taken"], NS)
            for g in range(NS):
                last = tr(cols4(7, g), work[:, g], ident)
            last.then_inc(s_slot["pe"], 1)
            pe.wait_ge(s_slot["act"], 3)
            for g in range(NS):
                last = mm(cols4(7, 2 + g), hT_flat[:, g * P:(g + 1) * P], fwo[:, :], start=True, stop=True)
            last.then_inc(s_slot["pe"], 1)
            pe.wait_ge(s_slot["hn"], 2)
            for g in range(NS):
                last = tr(cols4(0, g), hT_flat[:, g * P:(g + 1) * P], ident)
            last.then_inc(s_slot["pe"], 1)
            pe.wait_ge(s_slot["act"], 4)
            for f in range(FC):
                last = mm(bank[:, 1 + f // 2, (f % 2) * 256:(f % 2 + 1) * 256], fw1[:, f * P:(f + 1) * P], hT_flat[:, 256:512],
                          start=True, stop=True)
            last.then_inc(s_slot["pe"], 1)
            pe.wait_ge(s_slot["act"], 5)
            for g in range(NS):
                for f in range(FC):
                    at = 1024 + f * 256 + g * P
                    last = mm(cols4(3, g), hT_flat[:, at:at + P], fw2[:, f], start=f == 0, stop=f == FC - 1)
            last.then_inc(s_slot["pe"], 1)
            end_stage(pe, 12)
            for q in range(NQ):
                for j in range(4):
                    t = 4 * q + j
                    last = mm(cols4(4 + q, j), selT(t), slot_x[:, t // BT], start=True, stop=True)
                last.then_inc(s_sel["back"], 1)
            end_stage(pe, 13)

        @block.scalar
        def _(act):
            link = Chain(act, s_act)
            A, cp = nc.scalar.activation, nc.scalar.copy
            att_act(act, att["self"], NT, False)
            end_stage(act, 1)
            for q in range(NQ):
                ln_act(act, ln["ln1"], q, (0, 1))
            end_stage(act, 2)
            act.wait_ge(s_w, 16 * N_W)
            for q in range(NQ):
                if q >= 2:
                    act.wait_ge(s_o, 4 * (q - 1))
                for f in range(FC):
                    act.wait_ge(s_h, FC * q + f + 1)
                    A(hT[:, q % 2, f], bank[:, f], ACT.Relu, bias=cols[:, COL["b1"] + f:COL["b1"] + f + 1]).then_inc(s_hT, 1)
                if q >= 2:
                    ln_act(act, ln["ln3"], q - 2, (6, 7))
            ln_act(act, ln["ln3"], NQ - 2, (6, 7))
            ln_act(act, ln["ln3"], NQ - 1, (6, 7))
            end_stage(act, 3)
            for q in range(NQ):
                act.wait_ge(s_qkv, q + 1)
                for g in (0, 1):
                    last = A(k_comp[:, 4 * q:4 * q + 4, g, :],
                             bank[:, 4 * (q % 2) + 1, g * 256:(g + 1) * 256].rearrange("p (t s) -> p t s", s=S),
                             ACT.Identity, bias=cols[:, COL["bk"] + g:COL["bk"] + g + 1])
                last.then_inc(s_k_free, 1)
            end_stage(act, 4)
            att_act(act, att["cross"], NT, True)
            end_stage(act, 5)
            for q in range(NQ + 2):
                if q < NQ:
                    act.wait_ge(s_oT, q + 1)
                    if q >= 2:
                        act.wait_ge(s_wo, 4 * (q - 1))
                    cp(probsT[:, q % 2, 0:512], bank[:, q % 2]).then_inc(s_oTs, 1)
                if q >= 2:
                    ln_act(act, ln["ln4"], q - 2, (4, 5))
            end_stage(act, 6)
            act.wait_ge(s_r["gap"], 1)
            A(route("e", NT), route("e", NT), ACT.Exp).then_inc(s_r["exp"], 1)
            for q in range(NQ):
                act.wait_ge(s_r["gatesT"], q + 1)
                cp(hT_flat[0:E, q * 512:(q + 1) * 512], bank[0:E, 2 + q]).then_inc(s_r["gatesT_sb"], 1)
            end_stage(act, 7)
            for u in range(NQ * E):
                if u >= 2:
                    act.wait_ge(s_mo, u - 1)
                for f in range(FC):
                    act.wait_ge(s_mh, FC * u + f + 1)
                    A(hT[:, u % 2, f], bank[:, f], ACT.Relu, bias=mb1[:, u % E, f:f + 1]).then_inc(s_mhT, 1)
                if u % E == 3 and u > E:
                    ln_act(act, ln["ln5"], u // E - 1, (6, 7))
            ln_act(act, ln["ln5"], NQ - 1, (6, 7))
            end_stage(act, 8)
            link(A(col("t"), col("decay"), ACT.Exp, scale=-1.0))
            A(col("t3"), col("log_alpha"), ACT.Exp).then_inc(s_lin["consts"], 1)
            act.wait_ge(s_lin["one_plus"], 1)
            link(A(col("log_gamma"), col("t2"), ACT.Ln))
            link(nc.scalar.mul(col("log_gamma"), col("log_gamma"), -1.0))
            A(decay[:, :], con_at("decay_steps"), ACT.Exp, scale=col("log_gamma")).then_inc(s_lin["consts"], 1)
            act.wait_ge(s_lin["w"], 1)
            cp(wcomb[:, 2 * P:3 * P], bank[:, 7, 0:P]).then_inc(s_lin["w_sb"], 1)
            act.wait_ge(s_lin["w"], 2)
            cp(wcomb[:, 3 * P:4 * P], bank[:, 6, 0:P]).then_inc(s_lin["w_sb"], 1)
            for q in range(NQ + 2):
                if q < NQ:
                    act.wait_ge(s_lin["v"], q + 1)
                    if q >= 2:
                        act.wait_ge(s_lin["read"], 4 * (q - 1))
                    cp(probsT[:, q % 2, 0:512], bank[:, 2 + q % 2]).then_inc(s_lin["v_sb"], 1)
                if q >= 2:
                    ln_act(act, ln["ln6"], q - 2, (6, 7))
            end_stage(act, 9)
            act.wait_ge(s_rec["ready"], 1)
            A(col("ed"), col("w"), ACT.Exp, scale=-1.0)
            A(col("eg"), col("w"), ACT.Exp).then_inc(s_rec["rates"], 1)
            for q in range(NQ + 1):
                if q < NQ:
                    k = xT[:, q * 512:(q + 1) * 512]
                    if q >= 2:
                        act.wait_ge(s_rec["sum"], q - 1)
                    A(rec_b(q, 0), k, ACT.Exp)
                    A(seqs(rec_b(q, 2))[:, :, 2:S], seqs(k)[:, :, 1:S - 1], ACT.Exp, scale=-1.0)
                    A(rec_b(q, 3), k, ACT.Exp, bias=col("u")).then_inc(s_rec["exp"], 1)
                if q >= 1:
                    u = q - 1
                    act.wait_ge(s_rec["tok"], u + 1)
                    cp(work[:, 4 * u:4 * u + 4].rearrange("p t d -> p (t d)"), bank[:, u % 2]).then_inc(s_rec["taken"], 1)
            for q in range(NQ):
                ln_act(act, ln["ln7"], q, (2, 3))
            end_stage(act, 10)
            for q in range(NQ):
                act.wait_ge(s_sel["half"], q + 1)
                if q >= 2:
                    act.wait_ge(s_sel["half"], q + 1)
                cp(probs[:, q % 2, 0:512], bank[:, 5 + q % 2]).then_inc(s_sel["half_sb"], 1)
            for q in range(NQ):
                act.wait_ge(s_sel["turned"], q + 1)
                cp(mw1[:, 4 + q, :], bank[:, (0, 1, 2, 0)[q]]).then_inc(s_sel["selT"], 1)
            end_stage(act, 11)
            act.wait_ge(s_slot["angle"], 1)
            A(slot_trig[:, :, :, :], slot_angle[:, :, :, :], ACT.Sin).then_inc(s_slot["trig"], 1)
            act.wait_ge(s_slot["pe"], 1)
            cp(hT_flat[:, 256:512], bank[:, 0, 0:256]).then_inc(s_slot["act"], 1)
            act.wait_ge(s_slot["pe"], 2)
            cp(hT_flat[:, 512:768].rearrange("p (g n) -> p g n", g=NS), bank[:, 1:3, 2 * D:3 * D]).then_inc(s_slot["act"], 1)
            act.wait_ge(s_slot["pe"], 3)
            cp(q_diag[:, 0:NS].rearrange("p t g n -> p (t g n)"), bank[:, 3])
            cp(k_comp[:, 0:NS].rearrange("p t g n -> p (t g n)"), bank[:, 4, 0:256]).then_inc(s_slot["keys"], 1)
            att_act(act, att["slots"], NS, False)
            act.wait_ge(s_slot["pe"], 4)
            cp(hT_flat[:, 0:256], bank[:, 7, 0:256]).then_inc(s_slot["act"], 1)
            act.wait_ge(s_slot["pe"], 6)
            cp(hT_flat[:, 256:512], bank[:, 0, 0:256]).then_inc(s_slot["act"], 1)
            act.wait_ge(s_slot["pe"], 7)
            A(hT_flat[:, 1024:2048], bank[:, 1:3, :].rearrange("p a n -> p (a n)"), ACT.Gelu_apprx_tanh).then_inc(s_slot["act"], 1)
            end_stage(act, 12)
            end_stage(act, 13)

        @block.vector
        def _(dve):
            link = Chain(dve, s_dve)
            tt, ts, stt, cp = nc.vector.tensor_tensor, nc.vector.tensor_scalar, nc.vector.scalar_tensor_tensor, nc.vector.tensor_copy
            dve.wait_ge(s_con, 16)
            cp(ident_bf[:, :], ident).then_inc(s_setup, 1)
            a = CONST_AT["band"][0]
            cp(mask_bf[:, :, :].rearrange("p a n -> p (a n)"), con[:, a:a + 2 * S]).then_inc(s_setup, 1)
            att_dve(dve, att["self"], NT, False, link)
            end_stage(dve, 1)
            dve.wait_ge(s_x, 16)
            dve.wait_ge(s_w, 16 * N_W)
            s = ln["ln1"]

            def head(t):
                link(tt(work[:, t], work[:, t], x_tok[:, t], ALU.add))

            def tail(t):
                link(ln_apply(dve, s, t, x_side[:, t]))
                link(tt(x_side[:, t], x_side[:, t], rows[:, 0], ALU.mult))
                tt(x_side[:, t], x_side[:, t], rows[:, 1], ALU.add).then_inc(s["y"], 1)
            ln_dve(dve, s, link, head, tail)
            end_stage(dve, 2)
            for t in range(NT + 4):
                if t < NT:
                    dve.wait_ge(s_side, t // 4 + 1)
                    dve.wait_ge(s_o, t + 1 if t < 0 else 4 * (t // 4) + 4)
                    x = tt(work[:, t], bank[:, 4 + (t // 4) % 2, (t % 4) * P:(t % 4 + 1) * P], x_side[:, t], ALU.add)
                    x.then_inc(s_o_free, 1)
                    dve.wait_ge(s_o_free, t + 1)
                    ln_stats(ln["ln2"], t)(link)
                if 2 <= t < NT + 2:
                    u = t - 2
                    link(ln_apply(dve, ln["ln2"], u, work[:, u]))
                    link(tt(work[:, u], work[:, u], rows[:, 2], ALU.mult))
                    link(tt(work[:, u], work[:, u], rows[:, 3], ALU.add))
                    link(tt(work[:, u], work[:, u], x_tok[:, u], ALU.add))
                    ln_stats(ln["ln3"], u)(link)
                if t >= 4:
                    ln_apply(dve, ln["ln3"], t - 4, x_tok[:, t - 4]).then_inc(ln["ln3"]["y"], 1)
            end_stage(dve, 3)
            for q in range(NQ):
                b0 = 4 * (q % 2)
                dve.wait_ge(s_qkv, q + 1)
                for b in (0, 1):
                    r = slice(64 * b, 64 * b + 64)
                    for g in (0, 1):
                        ts(q_diag[r, 4 * q:4 * q + 4, g, 64 * b:64 * b + 64],
                           bank[r, b0, g * 256:(g + 1) * 256].rearrange("p (t s) -> p t s", s=S),
                           cols[r, COL["bq"] + g:COL["bq"] + g + 1], HD ** -0.5, ALU.add, ALU.mult)
                    last = tt(v_pair[r, 8 * q:8 * q + 8, :, b * (HD + 1):b * (HD + 1) + HD],
                              bank[r, b0 + 2].rearrange("p (j a e) -> p j a e", a=H // 2, e=HD),
                              rows[r, 5].rearrange("p (a h e) -> p a h e", h=2, e=HD)[:, None, :, b]
                              .to_broadcast([64, 8, H // 2, HD]), ALU.add)
                last.then_inc(s_qv_free, 1)
            end_stage(dve, 4)
            att_dve(dve, att["cross"], NT, True, link)
            end_stage(dve, 5)
            s = ln["ln4"]

            def head(t):
                dve.wait_ge(s_wo, 4 * (t // 4) + 4)
                tt(work[:, t], bank[:, 2 + (t // 4) % 2, (t % 4) * P:(t % 4 + 1) * P], x_side[:, t], ALU.add).then_inc(s_wo_free, 1)
                dve.wait_ge(s_wo_free, t + 1)

            def tail(t):
                ln_apply(dve, ln["ln4"], t, x_tok[:, t]).then_inc(ln["ln4"]["y"], 1)
            ln_dve(dve, s, link, head, tail)
            end_stage(dve, 6)
            def v3(name):
                return route(name, NT * E).rearrange("p (t e) -> p t e", e=E)

            def over_e(ap):
                return ap[:, :, None].to_broadcast([P, NT, E])
            lg, eq = v3("logits"), v3("eq")
            first = con_at("first_choice")[:, None, :].to_broadcast([P, NT, E])
            dve.wait_ge(s_r["logits"], 1)
            link(cp(route("logits", NT * E), bank[:, 6, 0:NT * E]))
            one = route("onehot", 2 * NT * E).rearrange("p (k t e) -> p k t e", k=2, e=E)
            for k in (0, 1):
                m, c = route("m%d" % k, NT), route("c", NT)
                link(nc.vector.tensor_reduce(m, lg, AX, ALU.max))
                link(tt(eq, lg, over_e(m), ALU.is_equal))
                link(tt(eq, eq, first, ALU.mult))
                link(nc.vector.tensor_reduce(c, eq, AX, ALU.max))
                last = tt(one[:, k], eq, over_e(c), ALU.is_equal)
                if k == 0:
                    link(last)
                    link(stt(lg, one[:, 0], -3e38, lg, ALU.mult, ALU.add))
                else:
                    last.then_inc(s_r["chosen"], 1)
            tt(route("e", NT), route("m1", NT), route("m0", NT), ALU.subtract).then_inc(s_r["gap"], 1)
            dve.wait_ge(s_r["exp"], 1)
            link(ts(route("m0", NT), route("e", NT), 1.0, None, ALU.add))
            link(nc.vector.reciprocal(route("m0", NT), route("m0", NT)))
            link(tt(route("m1", NT), route("e", NT), route("m0", NT), ALU.mult))
            tot, run, at = route("tot", 256), route("run", 256), route("at", 256)
            dve.wait_ge(s_r["ranks"], 2)
            link(cp(tot.rearrange("p (e n) -> p n e", e=E), bank[:, 1, 0:256].rearrange("p (n e) -> p n e", e=E)))
            link(nc.vector.tensor_tensor_scan(run, con_at("scan_carry"), tot, 0.0, ALU.mult, ALU.add))
            link(tt(run, run, tot, ALU.subtract))
            link(tt(at.rearrange("p (n e) -> p n e", e=E), bank[:, 0, 0:256].rearrange("p (n e) -> p n e", e=E),
                    run.rearrange("p (e n) -> p n e", e=E), ALU.add))
            link(stt(at, at, float(CAP), route("onehot", 256), ALU.is_lt, ALU.mult))
            at4 = at.rearrange("p (k t e) -> p k t e", k=2, e=E)
            link(tt(v3("gate"), at4[:, 0], over_e(route("m0", NT)), ALU.mult))
            link(tt(v3("eq"), at4[:, 1], over_e(route("m1", NT)), ALU.mult))
            tt(v3("gate"), v3("gate"), v3("eq"), ALU.add).then_inc(s_r["gates"], 1)
            for q in range(NQ):
                dve.wait_ge(s_r["bias"], q + 1)
                tt(work[:, 4 * q:4 * q + 4], bank[:, (6, 7, 2, 3)[q]].rearrange("p (t d) -> p t d", d=D),
                   x_tok[:, 4 * q:4 * q + 4], ALU.add)
            end_stage(dve, 7)
            s = ln["ln5"]
            for u in range(NQ * E):
                q, e = u // E, u % E
                dve.wait_ge(s_mo, u + 1)
                if e >= 1:
                    dve.wait_ge(s_mo_free, u)
                for j in range(4):
                    t = 4 * q + j
                    last = stt(work[:, t], bank[:, 4 + u % 2, j * P:(j + 1) * P], route("gate", NT * E)[:, t * E + e:t * E + e + 1],
                               work[:, t], ALU.mult, ALU.add)
                last.then_inc(s_mo_free, 1)
                if e == E - 1:
                    dve.wait_ge(s_mo_free, u + 1)
                    for j in range(4):
                        ln_stats(s, 4 * q + j)(link)
                if (e == 0 and q > 0) or u == NQ * E - 1:
                    for t in range(4 * (q - 1), 4 * q) if e == 0 else range(4 * q, 4 * q + 4):
                        ln_apply(dve, s, t, x_tok[:, t]).then_inc(s["y"], 1)
            end_stage(dve, 8)
            s = ln["ln6"]
            dve.wait_ge(s_lin["consts"], 1)
            link(ts(col("half_alpha"), col("t3"), 0.5, None, ALU.mult))
            ts(col("t2"), col("t"), 1.0, None, ALU.add).then_inc(s_lin["one_plus"], 1)
            dve.wait_ge(s_lin["consts"], 2)
            link(tt(decay[:, :], decay[:, :], con_at("causal"), ALU.mult))
            for q in range(NQ + 2):
                if q < NQ:
                    dve.wait_ge(s_lin["scores"], q + 1)
                    if q >= 2:
                        dve.wait_ge(s_lin["read"], 4 * (q - 1))
                    tt(probs[:, q % 2, 0:512].rearrange("p (t n) -> p t n", n=P), bank[:, q % 2].rearrange("p (t n) -> p t n", n=P),
                       decay[:, None, :].to_broadcast([P, 4, P]), ALU.mult).then_inc(s_lin["masked"], 1)
                if 1 <= q <= NQ:
                    for t in range(4 * q - 4, 4 * q):
                        dve.wait_ge(s_lin["read"], 4 * q)
                        stt(work[:, t], bank[:, 4 + (q - 1) % 2, (t % 4) * P:(t % 4 + 1) * P], col("half_alpha"), x_tok[:, t],
                            ALU.mult, ALU.add).then_inc(s_lin["taken"], 1)
                        dve.wait_ge(s_lin["taken"], t + 1)
                        ln_stats(s, t)(link)
                if q >= 2:
                    for t in range(4 * q - 8, 4 * q - 4):
                        ln_apply(dve, s, t, x_tok[:, t]).then_inc(s["y"], 1)
            end_stage(dve, 9)
            s = ln["ln7"]
            for j in (0, 1):
                for i in (1, 2):
                    last = nc.vector.memset(seqs(rec_b(j, i))[:, :, 0:2], 0.0)
            last.then_inc(s_rec["ready"], 1)
            dve.wait_ge(s_rec["rates"], 1)
            ed, eg = probsT[:, 0, 512:1024], probsT[:, 1, 512:1024]
            link(ts(ed, con_at("carry"), col("ed"), None, ALU.mult))
            link(ts(eg, con_at("carry"), col("eg"), None, ALU.mult))
            for q in range(NQ + 2):
                if q < NQ:
                    a, bb, m = probs[:, q % 2, 0:512], probs[:, q % 2, 512:1024], probsT[:, q % 2, 0:512]
                    c = ctxT[:, q * 512:(q + 1) * 512]
                    dve.wait_ge(s_rec["exp"], q + 1)
                    link(nc.vector.tensor_tensor_scan(bb, eg, rec_b(q, 2), 0.0, ALU.mult, ALU.add))
                    dve.wait_ge(s_rec["ekv"], q + 1)
                    link(nc.vector.tensor_tensor_scan(a, ed, rec_b(q, 1), 0.0, ALU.mult, ALU.add))
                    link(tt(bb, bb, c, ALU.mult))
                    link(tt(bb, bb, con_at("steps"), ALU.add))
                    link(tt(bb, bb, rec_b(q, 3), ALU.mult))
                    link(tt(bb, bb, a, ALU.add))
                    if q >= 2:
                        dve.wait_ge(s_rec["tok"], q - 1)
                    tt(m, bb, xT[:, q * 512:(q + 1) * 512], ALU.add).then_inc(s_rec["sum"], 1)
                if 1 <= q <= NQ:
                    dve.wait_ge(s_rec["taken"], q)
                    for t in range(4 * q - 4, 4 * q):
                        ln_stats(s, t)(link)
                if q >= 2:
                    for t in range(4 * q - 8, 4 * q - 4):
                        ln_apply(dve, s, t, x_tok[:, t]).then_inc(s["y"], 1)
            end_stage(dve, 10)
            cp(w_pos[:, 1], pos_i[:, :])
            dve.wait_ge(s_sel["weights"], 1)
            ts(w_pos[:, 0], bank[:, 0, 0:NT], col("router_b"), None, ALU.add).then_inc(s_sel["wcol"], 1)
            dve.wait_ge(s_sel["wcol"], 1)
            gt, tie, ge = route("gt", NT), route("tie", NT), route("ge", NT)
            for t in range(NT):
                dve.wait_ge(s_sel["rows"], t // 4 + 1)
                if t >= 5:
                    dve.wait_ge(s_sel["ranked"], t - 4)
                row = bank[:, 1 + (t // 4) % 2, (t % 4) * P:(t % 4 + 1) * P]
                for n, op, m, o in ((0, ALU.is_gt, "same_seq", gt), (1, ALU.is_equal, "same_seq_before", tie), (2, ALU.is_ge, "same_seq", ge)):
                    last = stt(scrap((t % 5) * 3 + n), row, w_pos[:, 0, t:t + 1], con_at(m), op, ALU.mult, accum_out=o[:, t:t + 1])
                last.then_inc(s_sel["ranked"], 1)
            dve.wait_ge(s_sel["ranked"], NT)
            link(tt(gt, gt, tie, ALU.add))
            link(ts(tie, gt, float(NSEL), None, ALU.is_lt))
            link(tt(gt, gt, con_at("slot_base"), ALU.add))
            link(tt(gt, gt, tie, ALU.mult))
            link(ts(gt, gt, -1.0, None, ALU.add))
            link(ts(ge, ge, float(NSEL), 1.0, ALU.is_gt, ALU.add))
            for t in range(NT):
                ts(sel(t), con_at("row_index"), gt[:, t:t + 1], None, ALU.is_equal).then_inc(s_sel["sel"], 1)
            dve.wait_ge(s_sel["gathered"], 1)
            cp(slot_x0[:, :, :].rearrange("p g d -> p (g d)"), bank[:, 3, 0:NS * D])
            cp(slot_wp[:, :], bank[:, 4, 0:2 * NS])
            for b in (0, 1):
                r = slice(64 * b, 64 * b + 64)
                tt(slot_mask[r], bank[r, 7, 0:NS * P].rearrange("p (g b k) -> p g b k", b=2, k=S)[:, :, b],
                   con_at("slot_block")[r, None, :].to_broadcast([64, NS, S]), ALU.add)
            end_stage(dve, 11)
            def squares_of(src):
                for g in range(NS):
                    last = stt(scrap(g + 4 * (src is slot_x)), src[:, g], 1.0, src[:, g], ALU.mult, ALU.mult,
                               accum_out=slot_s[:, g:g + 1])
                last.then_inc(s_slot["squares"], 1)

            def scaled(src, n):
                dve.wait_ge(s_slot["rms"], n)
                for g in range(NS):
                    last = ts(hT_flat[:, g * P:(g + 1) * P], src[:, g], slot_s[:, 4 + g:5 + g], None, ALU.mult)
                last.then_inc(s_slot["hn"], 1)
            ts(wqkv[:, 0:D], fqkv[:, 0:D], col("ln1"), HD ** -0.5, ALU.mult, ALU.mult)
            ts(wqkv[:, D:3 * D], fqkv[:, D:3 * D], col("ln1"), None, ALU.mult)
            link(ts(fw1[:, :], fw1[:, :], col("ln2"), None, ALU.mult))
            squares_of(slot_x0)
            link(nc.vector.memset(hT_flat[:, 3072:4096], 0.0))
            ang, k = slot_angle[:, 0], slot_angle[:, 1]
            for g in range(NS):
                link(ts(ang[:, g], con_at("inv_freq"), slot_wp[:, 2 * g + 1:2 * g + 2], None, ALU.mult))
            link(ts(k, ang, float(1 / (2 * np.pi)), 12582912.0, ALU.mult, ALU.add))
            link(ts(k, k, -12582912.0, None, ALU.add))
            link(stt(ang, k, -6.28125, ang, ALU.mult, ALU.add))
            link(stt(ang, k, float(-(2 * np.pi - 6.28125)), ang, ALU.mult, ALU.add))
            link(ts(ang, ang, 3.1415925, -3.1415925, ALU.min, ALU.max))
            link(stt(k, ang, -1.0, ang, ALU.mult, ALU.max))
            ts(k, k, -1.0, float(np.pi / 2), ALU.mult, ALU.add).then_inc(s_slot["angle"], 1)
            scaled(slot_x0, 1)
            dve.wait_ge(s_slot["trig"], 1)
            dve.wait_ge(s_slot["act"], 2)
            for g in range(NS):
                qk = bank[:, 1 + g, 0:2 * D].rearrange("p (h e) -> p h e", e=HD)
                lo, hi = qk[:, :, 0:4], qk[:, :, 4:8]
                sin = slot_trig[:, 0, g, None, :].to_broadcast([P, 2 * H, 4])
                cos = slot_trig[:, 1, g, None, :].to_broadcast([P, 2 * H, 4])
                part = lambda i: hT_flat[:, 2048 + i * 128:2048 + (i + 1) * 128]
                for i, (x, y) in enumerate(((lo, cos), (hi, sin), (hi, cos), (lo, sin))):
                    last = tt(part(4 * g + i).rearrange("p (h e) -> p h e", e=4), x, y, ALU.mult)
                link(last)
                for b in (0, 1):
                    r = slice(64 * b, 64 * b + 64)
                    z = hT_flat[r, 3072 + g * 512:3072 + (g + 1) * 512].rearrange("p (x b h e) -> p x b h e", b=2, h=8, e=HD)[:, :, b]
                    pr = lambda i: part(4 * g + i)[r].rearrange("p (x h e) -> p x h e", h=8, e=4)
                    tt(z[:, :, :, 0:4], pr(0), pr(1), ALU.subtract)
                    last = tt(z[:, :, :, 4:8], pr(2), pr(3), ALU.add)
            last.then_inc(s_slot["rope"], 1)
            dve.wait_ge(s_slot["pe"], 3)
            for h in (0, 1):
                r = slice(64 * h, 64 * h + 64)
                last = cp(v_pair[r, 0:2 * NS, :, h * (HD + 1):h * (HD + 1) + HD],
                          bank[r, 5].rearrange("p (j a h e) -> p j a h e", a=H // 2, h=2, e=HD)[:, :, :, h])
            last.then_inc(s_slot["values"], 1)
            att_dve(dve, att["slots"], NS, False, link)
            dve.wait_ge(s_slot["pe"], 5)
            link(tt(slot_x[:, :, :].rearrange("p g d -> p (g d)"), bank[:, 7, 256:512], slot_x0[:, :, :].rearrange("p g d -> p (g d)"), ALU.add))
            squares_of(slot_x)
            scaled(slot_x, 2)
            dve.wait_ge(s_slot["pe"], 8)
            link(tt(slot_x[:, :, :].rearrange("p g d -> p (g d)"), bank[:, 3, 0:256], slot_x[:, :, :].rearrange("p g d -> p (g d)"), ALU.add))
            for g in range(NS):
                ts(slot_x[:, g], slot_x[:, g], slot_wp[:, 2 * g:2 * g + 1], None, ALU.mult)
            end_stage(dve, 12)
            s = ln["ln8"]

            def head(t):
                dve.wait_ge(s_sel["back"], t // 4 + 1)
                link(stt(work[:, t], x_tok[:, t], ge[:, t:t + 1], bank[:, 4 + t // 4, (t % 4) * P:(t % 4 + 1) * P], ALU.mult, ALU.add))

            def tail(t):
                ln_apply(dve, s, t, x_tok[:, t]).then_inc(s["y"], 1)
            ln_dve(dve, s, link, head, tail)
            end_stage(dve, 13)


def lay_out(i):
    f = lambda n: np.asarray(i[n])
    x, c = f("x"), f("ctx_1024")
    a = {"const": CONST}
    a["x"] = x.reshape(NT, P, D).transpose(1, 0, 2)
    xr = x.reshape(NT, 2, S, 2, 64).transpose(1, 4, 0, 3, 2)
    a["k_self"] = xr.reshape(P, NT, 2, S)
    q = np.zeros((2, 64, NT, 2, 2, S), np.float32)
    q[0, :, :, :, 0], q[1, :, :, :, 1] = xr[0], xr[1]
    a["q_self"] = q.reshape(P, NT, 2, P)
    v = np.zeros((2, S, B, H // 2, 2, HD + 1), np.float32)
    xv = x.reshape(B, S, H // 2, 2, HD).transpose(3, 1, 0, 2, 4)
    for h in (0, 1):
        v[h, :, :, :, h, 0:HD] = xv[h]
        v[h, :, :, :, h, HD] = 1.0
    a["v_self"] = v.reshape(P, B, H // 2, VW)
    a["ctxT"] = c.reshape(T, D).T
    a["rows"] = np.tile(np.stack([f(n) for n in ("L0_attn_ln1_g", "L0_attn_ln1_b", "L0_attn_ln2_g", "L0_attn_ln2_b",
                                                 "L0_attn_b2", "L0_xattn_bv", "L0_xattn_bo", "L0_xattn_bo")])[None], (P, 1, 1))
    one = lambda n: np.broadcast_to(f(n).reshape(1, 1), (P, 1))
    two = lambda n: np.tile(f(n).reshape(2, 64).T, (2, 1))
    a["cols"] = np.concatenate([two("L0_xattn_bq"), two("L0_xattn_bk"), f("L0_attn_b1").reshape(FC, P).T,
                                f("L1_xattn_u")[:, None], f("L1_xattn_w")[:, None], f("L1_ffn_ln1")[:, None],
                                f("L1_ffn_ln2")[:, None], f("L1_ffn_router_w"), one("L1_attn_decay"),
                                one("L1_attn_log_alpha"), one("L1_ffn_router_b")], 1)
    a["L0_attn_W1"] = f("L0_attn_W1")
    a["L0_attn_W2"] = f("L0_attn_W2").reshape(FC, P, D).transpose(1, 0, 2)
    for n, m in (("wq", "L0_xattn_Wq"), ("wk", "L0_xattn_Wk"), ("wv", "L0_xattn_Wv"), ("wo", "L0_xattn_Wo")):
        a[n] = f(m).T
    a["L0_ffn_wg"] = f("L0_ffn_wg")
    a["mw1"] = f("L0_ffn_w1").transpose(1, 0, 2)
    a["mw2"] = f("L0_ffn_w2").reshape(E, FC, P, D).transpose(2, 0, 1, 3)
    a["mb1"] = f("L0_ffn_b1").reshape(E, FC, P).transpose(2, 0, 1)
    a["L0_ffn_b2"] = f("L0_ffn_b2")
    a["w_read_write"] = np.concatenate([f("L1_attn_W_write"), f("L1_attn_W_read")], 1)
    mask = f("L1_ffn_attention_mask")[:, 0, :S, :S]
    m = np.zeros((2, S, 3, 2, S), np.float32)
    for t in range(3):
        for b in (0, 1):
            m[b, :, t, b] = mask[min(2 * t + b, len(mask) - 1)]
    a["seq_mask"] = m.reshape(P, 3, P)
    pos = f("L1_ffn_position_ids")[:, :S]
    a["pos"] = pos[np.minimum(np.arange(B), len(pos) - 1)].reshape(NT, P).T
    a["fqkv"] = np.concatenate([f("L1_ffn_wq"), f("L1_ffn_wk"), f("L1_ffn_wv")], 1)
    a["L1_ffn_wo"], a["L1_ffn_w1"] = f("L1_ffn_wo"), f("L1_ffn_w1")
    a["fw2"] = f("L1_ffn_w2").reshape(FC, P, D).transpose(1, 0, 2)
    return {n: np.ascontiguousarray(v) for n, v in a.items()}


def kernel(**inputs):
    import concourse.bacc as bacc
    from concourse.bass_utils import run_bass_kernel_spmd

    nc = bacc.Bacc("TRN2", target_bir_lowering=False, num_devices=1)
    arrays = {f"in_{n}": v for n, v in lay_out(inputs).items()}
    io = {n[3:]: nc.dram_tensor(n, v.shape, mybir.dt.from_np(v.dtype), kind="ExternalInput").ap() for n, v in arrays.items()}
    io["out"] = nc.dram_tensor("out", (P, NT, D), F32, kind="ExternalOutput").ap()
    build(nc, io)
    r = run_bass_kernel_spmd(nc, [arrays], core_ids=[0])
    return np.ascontiguousarray(np.asarray(r.results[0]["out"]).transpose(1, 0, 2)).reshape(B, S, D)
```

```python
from contextlib import ExitStack

import numpy as np
import concourse.bass as bass
from concourse import mybir

F32 = mybir.dt.float32
BF16 = mybir.dt.bfloat16
I32 = mybir.dt.int32
ALU = mybir.AluOpType
ACT = mybir.ActivationFunctionType
AX = mybir.AxisListType.X

B, S, D = 32, 64, 128
T = B * S
P = 128
NT = T // P
NQ = NT // 4
H, HD = 16, 8
F = 512
FC = F // P
E, TOPK = 8, 2
CAP = TOPK * ((T + E - 1) // E)
LN_EPS = 1e-5
RMS_EPS = 1e-6
NEG = -1e30
KEEP = int(0.125 * S)
NSEL = KEEP - 1
BPS = P // KEEP
NS = B // BPS
BT = NT // NS
VW = 2 * (HD + 1)


def constants():
    p = np.arange(P)
    pos, seq = p % S, p // S
    k = np.arange(S)
    c = {}
    c["ident"] = np.eye(P)
    c["band"] = np.where(np.abs(pos[:, None] - k[None, :]) <= 32, 0.0, NEG)
    W = 16
    ok = (k[None] <= pos[:, None]) & (k[None] >= pos[:, None] - (W - 1)) & (k[None] <= 2 * pos[:, None] - (W - 1))
    c["window"] = np.where(ok, 0.0, NEG)
    npad = np.where(pos < W - 1, np.minimum(pos + 1, W - 1 - pos), 0)
    c["npad"] = npad[:, None]
    c["pad_ceiling"] = np.where(npad > 0, 0.0, -NEG)[:, None]
    c["head_of_row"] = ((p % 64)[:, None] // HD == np.arange(8)[None])
    c["earlier_row"] = p[:, None] < p[None, :]
    c["ones"] = np.ones((P, P))
    c["fold"] = pos[:, None] == k[None]
    for b in (0, 1):
        c[f"dup{b}"] = (seq[:, None] == b) & (pos[:, None] == pos[None, :])
    same = seq[:, None] == seq[None, :]
    c["same_seq"] = same
    c["same_seq_before"] = same & (p[None, :] < p[:, None])
    c["row_index"] = np.tile(p[None, :], (P, 1))
    c["decay_steps"] = np.maximum(p[None, :] - 1 - p[:, None], 0)
    c["causal"] = same & (p[None, :] > p[:, None]) & (pos[:, None] > 0)
    c["steps"] = np.tile(np.maximum(k - 1.0, 0.0)[None], (P, 8))
    c["carry"] = np.tile((k > 0)[None], (P, 8))
    c["first_choice"] = np.tile(E - np.arange(E)[None], (P, 1))
    c["expert_base"] = np.tile((CAP * np.arange(E))[None], (P, 1))
    c["spare"] = E * CAP + P * np.arange(TOPK * NT)[None] + p[:, None]
    c["slot_base"] = KEEP * ((2 * np.arange(NT)[None] + seq[:, None]) % BPS) + 1
    sp, sk = p % 64, k
    c["slot_block"] = np.where((sp[:, None] // KEEP == sk[None] // KEEP) & (sk[None] % KEEP < NSEL), 0.0, NEG)
    c["inv_freq"] = np.tile((1.0 / np.float32(10000.0) ** (np.arange(0, HD, 2, dtype=np.float32) / np.float32(HD)))[None], (P, 1))
    c["scan_carry"] = np.tile((np.arange(2 * NT) > 0)[None], (P, E))
    at, cols = {}, []
    n = 0
    for name, a in c.items():
        a = np.asarray(a, np.float32)
        at[name] = (n, a.shape[1])
        n += a.shape[1]
        cols.append(a)
    return at, np.ascontiguousarray(np.concatenate(cols, 1))


CONST_AT, CONST = constants()


def build(nc, io):
    with ExitStack() as ctx:
        def sb(name, shape, dt=F32):
            return ctx.enter_context(nc.sbuf_tensor(name, [P] + shape, dt))

        def sem(name):
            return ctx.enter_context(nc.semaphore(name))

        x_tok = sb("x_tok", [NT, D])
        x_side = sb("x_side", [NT, D])
        work = sb("work", [NT, D])
        xT0 = sb("xT0", [T + 1])
        xT = xT0[:, 1:T + 1]
        ctxT = sb("ctxT", [T])
        q_diag = sb("q_diag", [NT, 2, P])
        k_comp = sb("k_comp", [NT, 2, S])
        v_pair = sb("v_pair", [B, H // 2, VW])
        k_heads = sb("k_heads", [2, 2, 8, S])
        probs = sb("probs", [2, H * S])
        probsT = sb("probsT", [2, H * S])
        neg_max = sb("neg_max", [2, H])
        neg_max0 = sb("neg_max0", [4, H])
        pad_exp = sb("pad_exp", [4, H])
        denom = sb("denom", [2, H])
        r_denom = sb("r_denom", [2, H])
        stats = sb("stats", [NT, 6])
        mv = sb("mv", [NT, 2])
        var_e = sb("var_e", [NT, 1])
        rstd = sb("rstd", [NT, 1])
        neg_half = sb("neg_half", [NT])
        con = sb("con", [CONST.shape[1]])
        ident_bf = sb("ident_bf", [P], BF16)
        mask_bf = sb("mask_bf", [2, S], BF16)
        rows = sb("rows", [8, D])
        cols = sb("cols", [64])
        aw1 = sb("aw1", [F])
        aw2 = sb("aw2", [FC, D])
        wq = sb("wq", [D])
        wk = sb("wk", [D])
        wv = sb("wv", [D])
        wo = sb("wo", [D])
        wg = sb("wg", [E])
        mw1 = sb("mw1", [E, F])
        mw2 = sb("mw2", [E, FC, D])
        mb1 = sb("mb1", [E, FC])
        mb2 = sb("mb2", [E, D])
        hT = sb("hT", [2, FC, 512])

        hT_flat = hT[:, :, :, :].rearrange("p a f n -> p (a f n)")
        wcomb = sb("wcomb", [4 * P])
        decay = sb("decay", [P])
        seq_mask = sb("seq_mask", [3, P])
        pos_i = sb("pos_i", [NT], I32)
        w_pos = sb("w_pos", [2, NT])
        fqkv = sb("fqkv", [3 * D])
        wqkv = sb("wqkv", [3 * D])
        fwo = sb("fwo", [D])
        fw1 = sb("fw1", [F])
        fw2 = sb("fw2", [FC, D])
        slot_x0 = sb("slot_x0", [NS, D])
        slot_x = sb("slot_x", [NS, D])
        slot_wp = sb("slot_wp", [2 * NS])
        slot_mask = sb("slot_mask", [NS, S])
        slot_s = sb("slot_s", [8])
        slot_angle = sb("slot_angle", [2, NS, 4])
        slot_trig = sb("slot_trig", [2, NS, 4])
        routing = sb("routing", [2048])
        ROUTE = {"onehot": 0, "logits": 256, "eq": 384, "gate": 512, "tot": 640, "run": 896, "at": 1152, "m0": 1408,
                 "m1": 1424, "c": 1440, "e": 1456, "gt": 1472, "tie": 1488, "ge": 1504}

        place = sb("place", [2, TOPK * NT], I32)
        expert_in = nc.dram_tensor("expert_in", (E * CAP + TOPK * T, D), F32, kind="Internal").ap()
        expert_out = nc.dram_tensor("expert_out", (E * CAP, D), F32, kind="Internal").ap()

        def expert_x(e):
            return q_diag[:, 2 * e:2 * e + 2].rearrange("p t g n -> p (t g) n")

        def expert_y(e):
            return probsT[:, e % 2, 0:512].rearrange("p (t d) -> p t d", d=D)

        def fetched(k, t):
            return x_side[:, t] if k == 0 else k_comp[:, t].rearrange("p g s -> p (g s)")

        def route(name, n):
            return routing[:, ROUTE[name]:ROUTE[name] + n]

        def sel(t):
            return mw1[:, t // 4, (t % 4) * P:(t % 4 + 1) * P]

        def selT(t):
            return mw1[:, 4 + t // 4, (t % 4) * P:(t % 4 + 1) * P]

        def rope_z(g, which, half):
            at = 3072 + g * 512 + which * 256 + half * P
            return hT_flat[:, at:at + P]

        def scrap(i):
            return probsT[:, :, :].rearrange("p a n -> p (a n)")[:, i * P:(i + 1) * P]

        def seqs(ap):
            return ap.rearrange("p (b s) -> p b s", s=S)

        def rec_b(q, i):
            return hT[:, q % 2, i]

        def con_at(name):
            a, n = CONST_AT[name]
            return con[:, a:a + n]

        ident = con_at("ident")
        COL = {"bq": 0, "bk": 2, "b1": 4, "u": 8, "w": 9, "ln1": 10, "ln2": 11, "router": 12, "decay": 13,
               "log_alpha": 14, "router_b": 15, "half_alpha": 16, "log_gamma": 17, "ed": 18, "eg": 19, "t": 20, "t2": 21, "t3": 22}

        def col(name, n=1):
            return cols[:, COL[name]:COL[name] + n]

        bank = ctx.enter_context(nc.psum_tensor("bank", [P, 8, 512], F32))

        s_con = sem("s_con")
        s_x = sem("s_x")
        s_attn_in = sem("s_attn_in")
        s_w = sem("s_w")
        s_w2 = sem("s_w2")
        s_out = sem("s_out")
        s_setup = sem("s_setup")
        stage_end = sem("stage_end")
        s_dve = sem("s_dve")
        s_pool = sem("s_pool")
        s_act = sem("s_act")
        s_pe = sem("s_pe")

        def names(stage, *what):
            return {n: sem(f"{stage}_{n}") for n in what}

        class Chain:
            def __init__(self, eng, s):
                self.eng, self.s, self.n = eng, s, 0

            def __call__(self, ins):
                self.n += 1
                ins.then_inc(self.s, 1)
                self.eng.wait_ge(self.s, self.n)

        def end_stage(eng, n):
            eng.drain().then_inc(stage_end, 1)
            eng.wait_ge(stage_end, 4 * n)

        ATT = ("spread", "scores", "shifted", "exp", "transposed", "evacuated", "weighted", "taken", "max", "pad")
        att = {s: names(s, *(ATT if s == "cross" else ATT[:-2])) for s in ("self", "cross", "slots")}
        LNS = ("stats", "rstd", "y", "yT", "yT_out")
        norm_sems = names("norm", *LNS)
        ln = {s: {**norm_sems, "tiles": NT * i, "quads": NQ * i}
              for i, s in enumerate(("ln1", "ln3", "ln4", "ln5", "ln6", "ln7", "ln8"))}
        ln["ln2"] = {**names("norm2", "stats", "rstd"), "tiles": 0, "quads": 0}
        s_h, s_hT, s_o, s_o_free, s_h_free = (sem(n) for n in ("ffn_h", "ffn_hT", "ffn_out", "ffn_out_free", "ffn_h_free"))
        s_mh, s_mhT, s_mo, s_mo_free, s_mh_free = (sem(n) for n in ("moe_h", "moe_hT", "moe_out", "moe_out_free", "moe_h_free"))
        s_side = sem("s_side")
        s_qkv, s_qv_free, s_k_free = sem("s_qkv"), sem("s_qv_free"), sem("s_k_free")
        s_oT, s_oTs, s_wo, s_wo_free = sem("s_oT"), sem("s_oTs"), sem("s_wo"), sem("s_wo_free")
        s_r = names("route", "logits", "chosen", "ranks", "gap", "exp", "slots")
        s_moe = names("experts", "zeroed", "placed", "turned", "xT", "out")
        s_moe_in = [sem(f"moe_in{e}") for e in range(E)]
        s_moe_st = [sem(f"moe_stored{i}") for i in (0, 1)]
        s_fetch = [sem(f"moe_fetched{i}") for i in range(4)]
        s_lin = names("lin", "w", "w_sb", "consts", "one_plus", "scores", "masked", "v", "v_sb", "read", "taken")
        s_rec = names("rec", "ready", "rates", "exp", "ekv", "sum", "tok", "taken")
        s_sel = names("sel", "weights", "wcol", "rows", "ranked", "sel", "half", "half_sb", "gathered", "turned", "selT", "back")
        s_slot = names("slot", "squares", "rms", "hn", "pe", "act", "angle", "trig", "rope", "keys", "values")

        block = ctx.enter_context(nc.Block())

        def head_view(ap):
            return ap.rearrange("p (h k) -> p h k", k=S)

        o_view = bank[:, 6, 0:H * (HD + 1)].rearrange("p (h e) -> p h e", e=HD + 1)

        def att_spread(pool, s, n):
            hm = con_at("head_of_row")[:, None, :, None].to_broadcast([P, 2, 8, S])
            for i in range(n):
                if i >= 2:
                    pool.wait_ge(s["scores"], i - 1)
                nc.gpsimd.tensor_tensor(k_heads[:, i % 2], k_comp[:, i, :, None, :].to_broadcast([P, 2, 8, S]),
                                        hm, ALU.mult).then_inc(s["spread"], 1)

        def att_pe(pe, s, n, mask_lhs, mask_of):
            def scores(i):
                pe.wait_ge(s["spread"], i + 1)
                if i >= 2:
                    pe.wait_ge(s["shifted"], i - 1)
                for g in (0, 1):
                    out = bank[:, 2 * (i % 2) + g, :]
                    nc.tensor.matmul(out, q_diag[:, i, g], k_heads[:, i % 2, g].rearrange("p h k -> p (h k)"),
                                     start=True, stop=False)
                    last = nc.tensor.matmul(out, mask_lhs, mask_of(i), start=False, stop=True)
                last.then_inc(s["scores"], 1)

            def turn(i):
                pe.wait_ge(s["exp"], i + 1)
                if i >= 1:
                    pe.wait_ge(s["evacuated"], i)
                for hp in range(H // 2):
                    last = nc.tensor.transpose(bank[:, 4 + hp // 4, (hp % 4) * P:(hp % 4 + 1) * P],
                                               probs[:, i % 2, hp * P:(hp + 1) * P], ident)
                last.then_inc(s["transposed"], 1)

            def weigh(i):
                pe.wait_ge(s["evacuated"], i + 1)
                if i >= 1:
                    pe.wait_ge(s["taken"], i)
                for b in (0, 1):
                    for hp in range(H // 2):
                        at = hp * P + b * S
                        last = nc.tensor.matmul(bank[b * S:(b + 1) * S, 6, hp * VW:(hp + 1) * VW],
                                                probsT[:, i % 2, at:at + S], v_pair[:, 2 * i + b, hp],
                                                start=True, stop=True)
                last.then_inc(s["weighted"], 1)

            for i in range(n + 2):
                if i < n:
                    scores(i)
                if 1 <= i <= n:
                    turn(i - 1)
                if i >= 2:
                    weigh(i - 2)

        def att_act(act, s, n, pad):
            def evac(i):
                act.wait_ge(s["transposed"], i + 1)
                if i >= 2:
                    act.wait_ge(s["weighted"], i - 1)
                nc.scalar.copy(probsT[:, i % 2], bank[:, 4:6, :].rearrange("p a n -> p (a n)")).then_inc(s["evacuated"], 1)

            for i in range(n):
                if i >= 1:
                    evac(i - 1)
                if pad:
                    act.wait_ge(s["max"], i + 1)
                    if i >= 4:
                        act.wait_ge(s["taken"], i - 3)
                    nc.scalar.activation(pad_exp[:, i % 4], neg_max0[:, i % 4], ACT.Exp).then_inc(s["pad"], 1)
                act.wait_ge(s["shifted"], i + 1)
                nc.scalar.activation(probs[:, i % 2], probs[:, i % 2], ACT.Exp).then_inc(s["exp"], 1)
            evac(n - 1)

        def att_dve(dve, s, n, pad, link):
            def shift(i):
                m = neg_max[:, i % 2]
                sc = bank[:, 2 * (i % 2):2 * (i % 2) + 2, :].rearrange("p a (h k) -> p (a h) k", k=S)
                dve.wait_ge(s["scores"], i + 1)
                link(nc.vector.tensor_reduce(m, sc, AX, ALU.max, negate=True))
                if pad:
                    link(nc.vector.tensor_scalar(m, m, con_at("pad_ceiling"), None, ALU.min))
                    if i >= 4:
                        dve.wait_ge(s["pad"], i - 3)
                    nc.vector.tensor_scalar(neg_max0[:, i % 4], m, 0.0, None, ALU.min).then_inc(s["max"], 1)
                if i >= 2:
                    dve.wait_ge(s["transposed"], i - 1)
                nc.vector.tensor_tensor(head_view(probs[:, i % 2]), sc, m[:, :, None].to_broadcast([P, H, S]),
                                        ALU.add).then_inc(s["shifted"], 1)

            def take(i):
                d, r = denom[:, i % 2], r_denom[:, i % 2]
                dve.wait_ge(s["weighted"], i + 1)
                if pad:
                    dve.wait_ge(s["pad"], i + 1)
                    link(nc.vector.scalar_tensor_tensor(d, pad_exp[:, i % 4], con_at("npad"), o_view[:, :, HD],
                                                        ALU.mult, ALU.add))
                    link(nc.vector.reciprocal(r, d))
                else:
                    link(nc.vector.reciprocal(r, o_view[:, :, HD]))
                nc.vector.tensor_tensor(work[:, i].rearrange("p (h d) -> p h d", d=HD), o_view[:, :, 0:HD],
                                        r[:, :, None].to_broadcast([P, H, HD]), ALU.mult).then_inc(s["taken"], 1)

            for i in range(n + 2):
                if i < n:
                    shift(i)
                if i >= 2:
                    take(i - 2)

        def ln_stats(s, t):
            def f(link):
                link(nc.vector.bn_stats(stats[:, t], work[:, t]))
                nc.vector.bn_aggr(mv[:, t], stats[:, t]).then_inc(s["stats"], 1)
            return f

        def ln_apply(dve, s, t, out):
            dve.wait_ge(s["rstd"], s["tiles"] + t + 1)
            return nc.vector.tensor_scalar(out, work[:, t], mv[:, t, 0:1], rstd[:, t], ALU.subtract, ALU.mult)

        def ln_dve(dve, s, link, head, tail, lag=2):
            for t in range(NT + lag):
                if t < NT:
                    head(t)
                    ln_stats(s, t)(link)
                if t >= lag:
                    tail(t - lag)

        def rstd_of(pool, s, t, link, eps=LN_EPS):
            pool.wait_ge(s["stats"], s["tiles"] + t + 1)
            link(nc.gpsimd.tensor_scalar(var_e[:, t], mv[:, t, 1:2], eps, None, ALU.add))
            nc.gpsimd.tensor_tensor(rstd[:, t], var_e[:, t], neg_half[:, t:t + 1], ALU.pow).then_inc(s["rstd"], 1)

        def ln_pool(pool, s, link, eps=LN_EPS):
            for t in range(NT):
                rstd_of(pool, s, t, link, eps)

        def ln_pe(pe, s, quad, src):
            bk = 6 + quad % 2
            if s["quads"] + quad >= 2:
                pe.wait_ge(s["yT_out"], s["quads"] + quad - 1)
            for j in range(4):
                t = 4 * quad + j
                pe.wait_ge(s["y"], s["tiles"] + t + 1)
                last = nc.tensor.transpose(bank[:, bk, j * P:(j + 1) * P], src[:, t], ident)
            last.then_inc(s["yT"], 1)

        def ln_act(act, s, quad):
            act.wait_ge(s["yT"], s["quads"] + quad + 1)
            nc.scalar.copy(xT[:, quad * 512:(quad + 1) * 512], bank[:, 6 + quad % 2, :]).then_inc(s["yT_out"], 1)

        LOADS = ((rows[:, :, :], "rows"), (cols[:, 0:16], "cols"), (aw1[:, :], "L0_attn_W1"),
                 (aw2[:, :, :], "L0_attn_W2"), (wq[:, :], "wq"), (wk[:, :], "wk"), (wv[:, :], "wv"),
                 (wo[:, :], "wo"), (wg[:, :], "L0_ffn_wg"), (ctxT[:, :], "ctxT"), (mw1[:, :, :], "mw1"),
                 (mw2[:, :, :, :], "mw2"), (mb1[:, :, :], "mb1"), (mb2[:, :, :], "mb2"),
                 (wcomb[:, 0:2 * P], "w_read_write"), (seq_mask[:, :, :], "seq_mask"), (pos_i[:, :], "pos"),
                 (fqkv[:, :], "fqkv"), (fwo[:, :], "L1_ffn_wo"), (fw1[:, :], "L1_ffn_w1"), (fw2[:, :, :], "fw2"))
        N_W = len(LOADS)

        @block.sync
        def _(sp):
            sp.dma_start(con[:, :], io["const"]).then_inc(s_con, 16)
            sp.dma_start(k_comp[:, :, :, :], io["k_self"]).then_inc(s_attn_in, 16)
            sp.dma_start(q_diag[:, :, :, :], io["q_self"]).then_inc(s_attn_in, 16)
            sp.dma_start(v_pair[:, :, :, :], io["v_self"]).then_inc(s_attn_in, 16)
            sp.dma_start(x_tok[:, :, :], io["x"]).then_inc(s_x, 16)
            for dst, src in LOADS:
                sp.dma_start(dst, io[src]).then_inc(s_w, 16)
            sp.wait_ge(s_setup, 3)
            sp.dma_start(expert_in[0:E * CAP, :].rearrange("(n p) d -> p n d", p=P),
                         hT[:, 0, 0, None, 0:D].to_broadcast([P, E * CAP // P, D])).then_inc(s_moe["zeroed"], 16)
            sp.wait_ge(s_w, 16 * N_W)
            sp.wait_ge(s_x, 16)
            sp.wait_ge(s_moe["zeroed"], 16)
            sp.wait_ge(s_moe["placed"], 16 * TOPK * NT)
            for e in range(E):
                sp.dma_start(expert_x(e), expert_in[e * CAP:(e + 1) * CAP, :].rearrange("(n p) d -> p n d", p=P))                    .then_inc(s_moe_in[e], 16)
            for e in range(E):
                sp.wait_ge(s_moe["out"], e + 1)
                sp.dma_start(expert_out[e * CAP:(e + 1) * CAP, :].rearrange("(n p) d -> p n d", p=P), expert_y(e))                    .then_inc(s_moe_st[e % 2], 16)
            for q in range(NQ):
                sp.wait_ge(ln["ln8"]["y"], ln["ln8"]["tiles"] + 4 * q + 4)
                sp.dma_start(io["out"][:, 4 * q:4 * q + 4], x_tok[:, 4 * q:4 * q + 4]).then_inc(s_out, 16)
            sp.wait_ge(s_out, 16 * NQ)
            sp.wait_ge(stage_end, 4)

        @block.gpsimd
        def _(pool):
            link = Chain(pool, s_pool)
            tt, ts = nc.gpsimd.tensor_tensor, nc.gpsimd.tensor_scalar
            link(nc.gpsimd.memset(neg_half[:, :], -0.5))
            link(nc.gpsimd.memset(hT[:, 0, 0, 0:D], 0.0))
            nc.gpsimd.memset(xT0[:, 0:1], 0.0).then_inc(s_setup, 1)
            pool.wait_ge(s_con, 16)
            pool.wait_ge(s_attn_in, 48)
            att_spread(pool, att["self"], NT)
            ln_pool(pool, ln["ln1"], link)
            for q in range(NQ):
                side = x_side[:, 4 * q:4 * q + 4]
                pool.wait_ge(ln["ln1"]["yT"], q + 1)
                tt(side, side, rows[:, 4:5].to_broadcast([P, 4, D]), ALU.add).then_inc(s_side, 1)
            for t in range(NT + 2):
                if t < NT:
                    rstd_of(pool, ln["ln2"], t, link)
                if t >= 2:
                    rstd_of(pool, ln["ln3"], t - 2, link)
            for q in range(NQ):
                pool.wait_ge(ln["ln3"]["y"], ln["ln3"]["tiles"] + 4 * q + 4)
                tt(x_side[:, 4 * q:4 * q + 4], x_tok[:, 4 * q:4 * q + 4], rows[:, 6:7].to_broadcast([P, 4, D]),
                   ALU.add).then_inc(s_side, 1)
            pool.wait_ge(s_k_free, NQ)
            att_spread(pool, att["cross"], NT)
            ln_pool(pool, ln["ln4"], link)
            pool.wait_ge(s_r["slots"], 1)
            for j in range(TOPK * NT):
                nc.gpsimd.indirect_dma_start(
                    out=expert_in[:, :], out_offset=bass.IndirectOffsetOnAxis(ap=place[:, 0, j:j + 1], axis=0),
                    in_=x_tok[:, j % NT], in_offset=None).then_inc(s_moe["placed"], 16)
            pool.wait_ge(s_moe["placed"], 16 * TOPK * NT)
            for b in (0, 1):
                pool.wait_ge(s_moe_st[b], 16 * (E // 2))
            for t in range(NT):
                for k in (0, 1):
                    nc.gpsimd.indirect_dma_start(
                        out=fetched(k, t), out_offset=None, in_=expert_out[:, :],
                        in_offset=bass.IndirectOffsetOnAxis(ap=place[:, 1, k * NT + t:k * NT + t + 1], axis=0))                        .then_inc(s_fetch[t % 4], 16)
                if t >= 2:
                    rstd_of(pool, ln["ln5"], t - 2, link)
            for t in range(NT - 2, NT):
                rstd_of(pool, ln["ln5"], t, link)
            ln_pool(pool, ln["ln6"], link, LN_EPS / 4)
            for q in range(NQ):
                if q >= 2:
                    pool.wait_ge(s_rec["sum"], q - 1)
                pool.wait_ge(s_rec["exp"], q + 1)
                tt(seqs(rec_b(q, 1))[:, :, 2:S], seqs(rec_b(q, 0))[:, :, 1:S - 1],
                   seqs(ctxT[:, q * 512:(q + 1) * 512])[:, :, 1:S - 1], ALU.mult).then_inc(s_rec["ekv"], 1)
                if q >= 1:
                    for t in range(4 * q - 4, 4 * q):
                        rstd_of(pool, ln["ln7"], t, link)
            for t in range(NT - 4, NT):
                rstd_of(pool, ln["ln7"], t, link)
            def rms(n):
                pool.wait_ge(s_slot["squares"], n)
                link(ts(slot_s[:, 2:4], slot_s[:, 0:2], 1.0 / D, RMS_EPS, ALU.mult, ALU.add))
                tt(slot_s[:, 4:6], slot_s[:, 2:4], neg_half[:, 0:2], ALU.pow).then_inc(s_slot["rms"], 1)
            rms(1)
            pool.wait_ge(s_slot["keys"], 1)
            att_spread(pool, att["slots"], NS)
            rms(2)
            ln_pool(pool, ln["ln8"], link)
            end_stage(pool, 1)

        @block.tensor
        def _(pe):
            mm, tr = nc.tensor.matmul, nc.tensor.transpose

            def cols4(bk, j, n=P):
                return bank[:, bk, j * n:(j + 1) * n]

            pe.wait_ge(s_con, 16)
            pe.wait_ge(s_attn_in, 48)
            pe.wait_ge(s_setup, 3)
            mb = lambda j: (lambda i: mask_bf[:, j, None, :].to_broadcast([P, 8, S]))
            att_pe(pe, att["self"], NT, ident_bf[:, :], mb(0))
            pe.wait_ge(att["self"]["taken"], NT)
            pe.wait_ge(s_w, 16 * N_W)
            for q in range(NQ + 1):
                if q < NQ:
                    ln_pe(pe, ln["ln1"], q, x_side)
                    pe.wait_ge(ln["ln1"]["yT_out"], q + 1)
                    for f in range(FC):
                        if q >= 1:
                            pe.wait_ge(s_hT, FC * (q - 1) + f + 1)
                        mm(bank[:, f], aw1[:, f * P:(f + 1) * P], xT[:, q * 512:(q + 1) * 512], start=True, stop=True)\
                            .then_inc(s_h, 1)
                if q >= 1:
                    u = q - 1
                    pe.wait_ge(s_hT, FC * u + FC)
                    if u >= 2:
                        pe.wait_ge(s_o_free, 4 * (u - 1))
                    for j in range(4):
                        for f in range(FC):
                            last = mm(cols4(4 + u % 2, j), hT[:, u % 2, f, j * P:(j + 1) * P], aw2[:, f],
                                      start=f == 0, stop=f == FC - 1)
                        last.then_inc(s_o, 1)
            for q in range(NQ):
                ln_pe(pe, ln["ln3"], q, x_tok)
            for q in range(NQ):
                b0 = 3 * (q % 2)
                if q == 1:
                    pe.wait_ge(s_o_free, NT)
                if q >= 2:
                    pe.wait_ge(s_qv_free, q - 1)
                    pe.wait_ge(s_k_free, q - 1)
                for w, src, bk in ((wk, ctxT, b0 + 1), (wq, xT, b0)):
                    if src is xT:
                        pe.wait_ge(ln["ln3"]["yT_out"], ln["ln3"]["quads"] + q + 1)
                    sv = src[:, q * 512:(q + 1) * 512].rearrange("p (t b s) -> p t b s", b=2, s=S)
                    for g in (0, 1):
                        for b in (0, 1):
                            mm(bank[b * 64:(b + 1) * 64, bk, g * 256:(g + 1) * 256], w[:, g * 64:(g + 1) * 64],
                               sv[:, :, b, :], start=True, stop=True)
                for j in range(8):
                    at = (8 * q + j) * S
                    for h in (0, 1):
                        last = mm(bank[h * 64:(h + 1) * 64, b0 + 2, j * 64:(j + 1) * 64], ctxT[:, at:at + S],
                                  wv[:, :].rearrange("p (a h e) -> p a h e", h=2, e=HD)[:, :, h], start=True, stop=True)
                last.then_inc(s_qkv, 1)
            pe.wait_ge(s_qv_free, NQ)
            pe.wait_ge(s_k_free, NQ)
            att_pe(pe, att["cross"], NT, ident_bf[:, :], mb(1))
            for q in range(NQ + 3):
                if q < NQ:
                    if q >= 2:
                        pe.wait_ge(s_oTs, q - 1)
                    pe.wait_ge(att["cross"]["taken"], 4 * q + 4)
                    for j in range(4):
                        last = tr(cols4(q % 2, j), work[:, 4 * q + j], ident)
                    last.then_inc(s_oT, 1)
                if 1 <= q <= NQ:
                    u = q - 1
                    pe.wait_ge(s_oTs, u + 1)
                    if u >= 2:
                        pe.wait_ge(s_wo_free, 4 * (u - 1))
                    for j in range(4):
                        mm(cols4(2 + u % 2, j), probsT[:, u % 2, j * P:(j + 1) * P], wo[:, :], start=True, stop=True)\
                            .then_inc(s_wo, 1)
                if q == 2:
                    pe.wait_ge(att["cross"]["taken"], NT)
                if 2 <= q <= NQ + 1:
                    ln_pe(pe, ln["ln4"], q - 2, x_tok)
                if q >= 3:
                    u = q - 3
                    pe.wait_ge(ln["ln4"]["yT_out"], ln["ln4"]["quads"] + u + 1)
                    for t in range(4 * u, 4 * u + 4):
                        last = mm(bank[:, 5, t * E:(t + 1) * E], xT[:, t * P:(t + 1) * P], wg[:, :], start=True, stop=True)
            last.then_inc(s_r["logits"], 1)
            pe.wait_ge(s_r["chosen"], 1)
            oh = route("onehot", 2 * NT * E)
            mm(bank[:, 0, 0:256], con_at("earlier_row"), oh, start=True, stop=True).then_inc(s_r["ranks"], 1)
            mm(bank[:, 1, 0:256], con_at("ones"), oh, start=True, stop=True).then_inc(s_r["ranks"], 1)
            tr(bank[:, 3, 0:P], wcomb[:, P:2 * P], ident).then_inc(s_lin["w"], 1)
            pe.wait_ge(s_lin["w_sb"], 1)
            mm(bank[:, 2, 0:P], wcomb[:, 0:P], wcomb[:, 2 * P:3 * P], start=True, stop=True).then_inc(s_lin["w"], 1)
            pe.wait_ge(s_lin["w_sb"], 2)
            def turn_in(e):
                pe.wait_ge(s_moe_in[e], 16)
                if e >= 2:
                    pe.wait_ge(s_moe["xT"], e - 1)
                for j in range(4):
                    last = tr(cols4(6 + e % 2, j), expert_x(e)[:, j], ident)
                last.then_inc(s_moe["turned"], 1)
            turn_in(0)
            for e in range(E + 1):
                if e < E:
                    pe.wait_ge(s_moe["xT"], e + 1)
                    for f in range(FC):
                        if e >= 1:
                            pe.wait_ge(s_mhT, FC * (e - 1) + f + 1)
                        mm(bank[:, f], mw1[:, e, f * P:(f + 1) * P], probs[:, e % 2, 0:512], start=True, stop=True)                            .then_inc(s_mh, 1)
                if e + 1 < E:
                    turn_in(e + 1)
                if e >= 1:
                    v = e - 1
                    pe.wait_ge(s_mhT, FC * v + FC)
                    if v >= 2:
                        pe.wait_ge(s_moe["out"], v - 1)
                    for j in range(4):
                        for f in range(FC):
                            last = mm(cols4(4 + v % 2, j), hT[:, v % 2, f, j * P:(j + 1) * P], mw2[:, v, f],
                                      start=f == 0, stop=f == FC - 1)
                    last.then_inc(s_mo, 1)
            for q in range(NQ):
                ln_pe(pe, ln["ln5"], q, x_tok)
            for q in range(NQ + 2):
                if q < NQ:
                    if q >= 2:
                        pe.wait_ge(s_lin["masked"], q - 1)
                        pe.wait_ge(s_lin["v_sb"], q - 1)
                    pe.wait_ge(ln["ln5"]["yT_out"], ln["ln5"]["quads"] + q + 1)
                    for j in range(4):
                        at = (4 * q + j) * P
                        last = mm(cols4(q % 2, j), xT0[:, at:at + P], xT[:, at:at + P], start=True, stop=True)
                    last.then_inc(s_lin["scores"], 1)
                    for j in range(4):
                        at = (4 * q + j) * P
                        last = mm(cols4(2 + q % 2, j), xT[:, at:at + P], wcomb[:, 3 * P:4 * P], start=True, stop=True)
                    last.then_inc(s_lin["v"], 1)
                if 1 <= q <= NQ:
                    u = q - 1
                    pe.wait_ge(s_lin["masked"], u + 1)
                    pe.wait_ge(s_lin["v_sb"], u + 1)
                    if u >= 2:
                        pe.wait_ge(s_lin["taken"], 4 * (u - 1))
                    for j in range(4):
                        mm(cols4(4 + u % 2, j), probs[:, u % 2, j * P:(j + 1) * P], probsT[:, u % 2, j * P:(j + 1) * P],
                           start=True, stop=True).then_inc(s_lin["read"], 1)
                if q >= 2:
                    ln_pe(pe, ln["ln6"], q - 2, x_tok)
            for q in range(NQ + 1):
                if q < NQ:
                    pe.wait_ge(s_rec["sum"], q + 1)
                    if q >= 2:
                        pe.wait_ge(s_rec["taken"], q - 1)
                    for j in range(4):
                        last = tr(cols4(q % 2, j), probsT[:, q % 2, j * P:(j + 1) * P], ident)
                    last.then_inc(s_rec["tok"], 1)
                if q >= 1:
                    ln_pe(pe, ln["ln7"], q - 1, x_tok)
            pe.wait_ge(s_rec["taken"], NQ)
            for t in range(NT):
                if t % 4 == 0:
                    pe.wait_ge(ln["ln7"]["yT_out"], ln["ln7"]["quads"] + t // 4 + 1)
                last = mm(bank[:, 0, t:t + 1], xT[:, t * P:(t + 1) * P], col("router"), start=True, stop=True)
            last.then_inc(s_sel["weights"], 1)
            pe.wait_ge(s_sel["wcol"], 1)
            for q in range(NQ):
                if q >= 2:
                    pe.wait_ge(s_sel["ranked"], 4 * (q - 1))
                for j in range(4):
                    t = 4 * q + j
                    last = tr(cols4(1 + q % 2, j), w_pos[:, 0, t:t + 1].to_broadcast([P, P]), ident)
                last.then_inc(s_sel["rows"], 1)
            for t in range(NT):
                g, i = t // BT, t % BT
                pe.wait_ge(s_sel["sel"], t + 1)
                mm(bank[:, 3, g * P:(g + 1) * P], sel(t), x_tok[:, t], start=i == 0, stop=i == BT - 1)
            for t in range(NT):
                g, i = t // BT, t % BT
                mm(bank[:, 4, 2 * g:2 * g + 2], sel(t), w_pos[:, :, t], start=i == 0, stop=i == BT - 1)
            for q in range(NQ + 1):
                if q < NQ:
                    if q >= 2:
                        pe.wait_ge(s_sel["half_sb"], q - 1)
                    for j in range(4):
                        t = 4 * q + j
                        last = mm(cols4(5 + q % 2, j), seq_mask[:, min(t, 2)], sel(t), start=True, stop=True)
                    last.then_inc(s_sel["half"], 1)
                if q >= 1:
                    pe.wait_ge(s_sel["half_sb"], q)
                    for j in range(4):
                        t = 4 * (q - 1) + j
                        g, i = t // BT, t % BT
                        last = mm(bank[:, 7, g * P:(g + 1) * P], probs[:, (q - 1) % 2, j * P:(j + 1) * P], sel(t),
                                  start=i == 0, stop=i == BT - 1)
            last.then_inc(s_sel["gathered"], 1)
            pe.wait_ge(s_sel["ranked"], NT)
            for q in range(NQ):
                bk = (0, 1, 2, 0)[q]
                if q == 3:
                    pe.wait_ge(s_sel["selT"], 1)
                for j in range(4):
                    last = tr(cols4(bk, j), sel(4 * q + j), ident)
                last.then_inc(s_sel["turned"], 1)
            pe.wait_ge(s_slot["hn"], 1)
            pe.wait_ge(s_sel["selT"], NQ)
            for g in range(NS):
                last = tr(cols4(0, g), hT_flat[:, g * P:(g + 1) * P], ident)
            last.then_inc(s_slot["pe"], 1)
            pe.wait_ge(s_slot["act"], 1)
            for g in range(NS):
                last = mm(bank[:, 1 + g, 0:3 * D], hT_flat[:, 256 + g * P:256 + (g + 1) * P], wqkv[:, :], start=True, stop=True)
            last.then_inc(s_slot["pe"], 1)
            pe.wait_ge(s_slot["rope"], 1)
            for g in range(NS):
                for half in (0, 1):
                    tr(cols4(3, 2 * g + half), rope_z(g, 0, half), ident)
                    last = mm(cols4(4, 2 * g + half, S), rope_z(g, 1, half), con_at("fold"), start=True, stop=True)
            pe.wait_ge(s_slot["act"], 2)
            for g in range(NS):
                for b in (0, 1):
                    last = mm(cols4(5, 2 * g + b), con_at(f"dup{b}"), hT_flat[:, 512 + g * P:512 + (g + 1) * P], start=True, stop=True)
            last.then_inc(s_slot["pe"], 1)
            pe.wait_ge(s_slot["keys"], 1)
            pe.wait_ge(s_slot["values"], 1)
            att_pe(pe, att["slots"], NS, ident, lambda i: slot_mask[:, i, None, :].to_broadcast([P, 8, S]))
            pe.wait_ge(att["slots"]["taken"], NS)
            for g in range(NS):
                last = tr(cols4(7, g), work[:, g], ident)
            last.then_inc(s_slot["pe"], 1)
            pe.wait_ge(s_slot["act"], 3)
            for g in range(NS):
                last = mm(cols4(7, 2 + g), hT_flat[:, g * P:(g + 1) * P], fwo[:, :], start=True, stop=True)
            last.then_inc(s_slot["pe"], 1)
            pe.wait_ge(s_slot["hn"], 2)
            for g in range(NS):
                last = tr(cols4(0, g), hT_flat[:, g * P:(g + 1) * P], ident)
            last.then_inc(s_slot["pe"], 1)
            pe.wait_ge(s_slot["act"], 4)
            for f in range(FC):
                last = mm(bank[:, 1 + f // 2, (f % 2) * 256:(f % 2 + 1) * 256], fw1[:, f * P:(f + 1) * P], hT_flat[:, 256:512],
                          start=True, stop=True)
            last.then_inc(s_slot["pe"], 1)
            pe.wait_ge(s_slot["act"], 5)
            for g in range(NS):
                for f in range(FC):
                    at = 1024 + f * 256 + g * P
                    last = mm(cols4(3, g), hT_flat[:, at:at + P], fw2[:, f], start=f == 0, stop=f == FC - 1)
            last.then_inc(s_slot["pe"], 1)
            pe.wait_ge(s_slot["hn"], 3)
            for q in range(NQ):
                for j in range(4):
                    t = 4 * q + j
                    last = mm(cols4(4 + q, j), selT(t), slot_x[:, t // BT], start=True, stop=True)
                last.then_inc(s_sel["back"], 1)
            end_stage(pe, 1)

        @block.scalar
        def _(act):
            link = Chain(act, s_act)
            A, cp = nc.scalar.activation, nc.scalar.copy
            att_act(act, att["self"], NT, False)
            act.wait_ge(s_w, 16 * N_W)
            act.wait_ge(s_moe["zeroed"], 16)
            for q in range(NQ):
                ln_act(act, ln["ln1"], q)
                if q >= 2:
                    act.wait_ge(s_o, 4 * (q - 1))
                for f in range(FC):
                    act.wait_ge(s_h, FC * q + f + 1)
                    A(hT[:, q % 2, f], bank[:, f], ACT.Relu, bias=cols[:, COL["b1"] + f:COL["b1"] + f + 1]).then_inc(s_hT, 1)
            for q in range(NQ):
                ln_act(act, ln["ln3"], q)
            for q in range(NQ):
                act.wait_ge(s_qkv, q + 1)
                for g in (0, 1):
                    last = A(k_comp[:, 4 * q:4 * q + 4, g, :],
                             bank[:, 3 * (q % 2) + 1, g * 256:(g + 1) * 256].rearrange("p (t s) -> p t s", s=S),
                             ACT.Identity, bias=cols[:, COL["bk"] + g:COL["bk"] + g + 1])
                last.then_inc(s_k_free, 1)
            att_act(act, att["cross"], NT, True)
            for q in range(NQ + 2):
                if q < NQ:
                    act.wait_ge(s_oT, q + 1)
                    if q >= 2:
                        act.wait_ge(s_wo, 4 * (q - 1))
                    cp(probsT[:, q % 2, 0:512], bank[:, q % 2]).then_inc(s_oTs, 1)
                if q >= 2:
                    ln_act(act, ln["ln4"], q - 2)
            act.wait_ge(s_r["gap"], 1)
            A(route("e", NT), route("e", NT), ACT.Exp).then_inc(s_r["exp"], 1)
            link(A(col("t"), col("decay"), ACT.Exp, scale=-1.0))
            A(col("t3"), col("log_alpha"), ACT.Exp).then_inc(s_lin["consts"], 1)
            act.wait_ge(s_lin["one_plus"], 1)
            link(A(col("log_gamma"), col("t2"), ACT.Ln))
            link(nc.scalar.mul(col("log_gamma"), col("log_gamma"), -1.0))
            A(decay[:, :], con_at("decay_steps"), ACT.Exp, scale=col("log_gamma")).then_inc(s_lin["consts"], 1)
            act.wait_ge(s_lin["w"], 1)
            cp(wcomb[:, 2 * P:3 * P], bank[:, 3, 0:P]).then_inc(s_lin["w_sb"], 1)
            act.wait_ge(s_lin["w"], 2)
            cp(wcomb[:, 3 * P:4 * P], bank[:, 2, 0:P]).then_inc(s_lin["w_sb"], 1)
            def input_out(e):
                act.wait_ge(s_moe["turned"], e + 1)
                if e >= 2:
                    act.wait_ge(s_mh, FC * (e - 1))
                cp(probs[:, e % 2, 0:512], bank[:, 6 + e % 2]).then_inc(s_moe["xT"], 1)
            input_out(0)
            for e in range(E):
                if e >= 2:
                    act.wait_ge(s_mo, e - 1)
                for f in range(FC):
                    act.wait_ge(s_mh, FC * e + f + 1)
                    A(hT[:, e % 2, f], bank[:, f], ACT.Relu, bias=mb1[:, e, f:f + 1]).then_inc(s_mhT, 1)
                if e + 1 < E:
                    input_out(e + 1)
            for q in range(NQ):
                ln_act(act, ln["ln5"], q)
            for q in range(NQ + 2):
                if q < NQ:
                    act.wait_ge(s_lin["v"], q + 1)
                    if q >= 2:
                        act.wait_ge(s_lin["read"], 4 * (q - 1))
                    cp(probsT[:, q % 2, 0:512], bank[:, 2 + q % 2]).then_inc(s_lin["v_sb"], 1)
                if q >= 2:
                    ln_act(act, ln["ln6"], q - 2)
            act.wait_ge(s_rec["ready"], 1)
            A(col("ed"), col("w"), ACT.Exp, scale=-1.0)
            A(col("eg"), col("w"), ACT.Exp).then_inc(s_rec["rates"], 1)
            for q in range(NQ + 1):
                if q < NQ:
                    k = xT[:, q * 512:(q + 1) * 512]
                    act.wait_ge(ln["ln6"]["yT_out"], ln["ln6"]["quads"] + q + 1)
                    if q >= 2:
                        act.wait_ge(s_rec["sum"], q - 1)
                    A(rec_b(q, 0), k, ACT.Exp)
                    A(seqs(rec_b(q, 2))[:, :, 2:S], seqs(k)[:, :, 1:S - 1], ACT.Exp, scale=-1.0)
                    A(rec_b(q, 3), k, ACT.Exp, bias=col("u")).then_inc(s_rec["exp"], 1)
                if q >= 1:
                    u = q - 1
                    act.wait_ge(s_rec["tok"], u + 1)
                    cp(work[:, 4 * u:4 * u + 4].rearrange("p t d -> p (t d)"), bank[:, u % 2]).then_inc(s_rec["taken"], 1)
            for q in range(NQ):
                ln_act(act, ln["ln7"], q)
            for q in range(NQ):
                act.wait_ge(s_sel["half"], q + 1)
                if q >= 2:
                    act.wait_ge(s_sel["half"], q + 1)
                cp(probs[:, q % 2, 0:512], bank[:, 5 + q % 2]).then_inc(s_sel["half_sb"], 1)
            for q in range(NQ):
                act.wait_ge(s_sel["turned"], q + 1)
                cp(mw1[:, 4 + q, :], bank[:, (0, 1, 2, 0)[q]]).then_inc(s_sel["selT"], 1)
            act.wait_ge(s_slot["angle"], 1)
            A(slot_trig[:, :, :, :], slot_angle[:, :, :, :], ACT.Sin).then_inc(s_slot["trig"], 1)
            act.wait_ge(s_slot["pe"], 1)
            cp(hT_flat[:, 256:512], bank[:, 0, 0:256]).then_inc(s_slot["act"], 1)
            act.wait_ge(s_slot["pe"], 2)
            cp(hT_flat[:, 512:768].rearrange("p (g n) -> p g n", g=NS), bank[:, 1:3, 2 * D:3 * D]).then_inc(s_slot["act"], 1)
            act.wait_ge(s_slot["pe"], 3)
            cp(q_diag[:, 0:NS].rearrange("p t g n -> p (t g n)"), bank[:, 3])
            cp(k_comp[:, 0:NS].rearrange("p t g n -> p (t g n)"), bank[:, 4, 0:256]).then_inc(s_slot["keys"], 1)
            att_act(act, att["slots"], NS, False)
            act.wait_ge(s_slot["pe"], 4)
            cp(hT_flat[:, 0:256], bank[:, 7, 0:256]).then_inc(s_slot["act"], 1)
            act.wait_ge(s_slot["pe"], 6)
            cp(hT_flat[:, 256:512], bank[:, 0, 0:256]).then_inc(s_slot["act"], 1)
            act.wait_ge(s_slot["pe"], 7)
            A(hT_flat[:, 1024:2048], bank[:, 1:3, :].rearrange("p a n -> p (a n)"), ACT.Gelu_apprx_tanh).then_inc(s_slot["act"], 1)
            end_stage(act, 1)

        @block.vector
        def _(dve):
            link = Chain(dve, s_dve)
            tt, ts, stt, cp = nc.vector.tensor_tensor, nc.vector.tensor_scalar, nc.vector.scalar_tensor_tensor, nc.vector.tensor_copy
            dve.wait_ge(s_con, 16)
            cp(ident_bf[:, :], ident).then_inc(s_setup, 1)
            a = CONST_AT["band"][0]
            cp(mask_bf[:, :, :].rearrange("p a n -> p (a n)"), con[:, a:a + 2 * S]).then_inc(s_setup, 1)
            att_dve(dve, att["self"], NT, False, link)
            dve.wait_ge(s_x, 16)
            dve.wait_ge(s_w, 16 * N_W)
            s = ln["ln1"]

            def head(t):
                link(tt(work[:, t], work[:, t], x_tok[:, t], ALU.add))

            def tail(t):
                link(ln_apply(dve, s, t, x_side[:, t]))
                link(tt(x_side[:, t], x_side[:, t], rows[:, 0], ALU.mult))
                tt(x_side[:, t], x_side[:, t], rows[:, 1], ALU.add).then_inc(s["y"], 1)
            ln_dve(dve, s, link, head, tail)
            for t in range(NT + 4):
                if t < NT:
                    dve.wait_ge(s_side, t // 4 + 1)
                    dve.wait_ge(s_o, t + 1 if t < 0 else 4 * (t // 4) + 4)
                    x = tt(work[:, t], bank[:, 4 + (t // 4) % 2, (t % 4) * P:(t % 4 + 1) * P], x_side[:, t], ALU.add)
                    x.then_inc(s_o_free, 1)
                    dve.wait_ge(s_o_free, t + 1)
                    ln_stats(ln["ln2"], t)(link)
                if 2 <= t < NT + 2:
                    u = t - 2
                    link(ln_apply(dve, ln["ln2"], u, work[:, u]))
                    link(tt(work[:, u], work[:, u], rows[:, 2], ALU.mult))
                    link(tt(work[:, u], work[:, u], rows[:, 3], ALU.add))
                    link(tt(work[:, u], work[:, u], x_tok[:, u], ALU.add))
                    ln_stats(ln["ln3"], u)(link)
                if t >= 4:
                    ln_apply(dve, ln["ln3"], t - 4, x_tok[:, t - 4]).then_inc(ln["ln3"]["y"], 1)
            for q in range(NQ):
                b0 = 3 * (q % 2)
                dve.wait_ge(s_qkv, q + 1)
                for b in (0, 1):
                    r = slice(64 * b, 64 * b + 64)
                    for g in (0, 1):
                        ts(q_diag[r, 4 * q:4 * q + 4, g, 64 * b:64 * b + 64],
                           bank[r, b0, g * 256:(g + 1) * 256].rearrange("p (t s) -> p t s", s=S),
                           cols[r, COL["bq"] + g:COL["bq"] + g + 1], HD ** -0.5, ALU.add, ALU.mult)
                    last = tt(v_pair[r, 8 * q:8 * q + 8, :, b * (HD + 1):b * (HD + 1) + HD],
                              bank[r, b0 + 2].rearrange("p (j a e) -> p j a e", a=H // 2, e=HD),
                              rows[r, 5].rearrange("p (a h e) -> p a h e", h=2, e=HD)[:, None, :, b]
                              .to_broadcast([64, 8, H // 2, HD]), ALU.add)
                last.then_inc(s_qv_free, 1)
            att_dve(dve, att["cross"], NT, True, link)
            s = ln["ln4"]

            def head(t):
                dve.wait_ge(s_wo, 4 * (t // 4) + 4)
                dve.wait_ge(s_side, NQ + t // 4 + 1)
                tt(work[:, t], bank[:, 2 + (t // 4) % 2, (t % 4) * P:(t % 4 + 1) * P], x_side[:, t], ALU.add).then_inc(s_wo_free, 1)
                dve.wait_ge(s_wo_free, t + 1)

            def tail(t):
                ln_apply(dve, ln["ln4"], t, x_tok[:, t]).then_inc(ln["ln4"]["y"], 1)
            ln_dve(dve, s, link, head, tail)
            def v3(name):
                return route(name, NT * E).rearrange("p (t e) -> p t e", e=E)

            def over_e(ap):
                return ap[:, :, None].to_broadcast([P, NT, E])
            lg, eq = v3("logits"), v3("eq")
            first = con_at("first_choice")[:, None, :].to_broadcast([P, NT, E])
            dve.wait_ge(s_r["logits"], 1)
            link(cp(route("logits", NT * E), bank[:, 5, 0:NT * E]))
            one = route("onehot", 2 * NT * E).rearrange("p (k t e) -> p k t e", k=2, e=E)
            for k in (0, 1):
                m, c = route("m%d" % k, NT), route("c", NT)
                link(nc.vector.tensor_reduce(m, lg, AX, ALU.max))
                link(tt(eq, lg, over_e(m), ALU.is_equal))
                link(tt(eq, eq, first, ALU.mult))
                link(nc.vector.tensor_reduce(c, eq, AX, ALU.max))
                last = tt(one[:, k], eq, over_e(c), ALU.is_equal)
                if k == 0:
                    link(last)
                    link(stt(lg, one[:, 0], -3e38, lg, ALU.mult, ALU.add))
                else:
                    last.then_inc(s_r["chosen"], 1)
            tt(route("e", NT), route("m1", NT), route("m0", NT), ALU.subtract).then_inc(s_r["gap"], 1)
            dve.wait_ge(s_r["exp"], 1)
            link(ts(route("m0", NT), route("e", NT), 1.0, None, ALU.add))
            link(nc.vector.reciprocal(route("m0", NT), route("m0", NT)))
            link(tt(route("m1", NT), route("e", NT), route("m0", NT), ALU.mult))
            tot, run, at = route("tot", 256), route("run", 256), route("at", 256)
            dve.wait_ge(s_r["ranks"], 2)
            link(cp(tot.rearrange("p (e n) -> p n e", e=E), bank[:, 1, 0:256].rearrange("p (n e) -> p n e", e=E)))
            link(nc.vector.tensor_tensor_scan(run, con_at("scan_carry"), tot, 0.0, ALU.mult, ALU.add))
            link(tt(run, run, tot, ALU.subtract))
            link(tt(at.rearrange("p (n e) -> p n e", e=E), bank[:, 0, 0:256].rearrange("p (n e) -> p n e", e=E),
                    run.rearrange("p (e n) -> p n e", e=E), ALU.add))
            ok, n = route("tot", 256), TOPK * NT
            link(stt(ok, at, float(CAP), route("onehot", 256), ALU.is_lt, ALU.mult))
            link(tt(at.rearrange("p (n e) -> p n e", e=E), at.rearrange("p (n e) -> p n e", e=E),
                    con_at("expert_base")[:, None, :].to_broadcast([P, n, E]), ALU.add))
            link(tt(at, at, ok, ALU.mult))
            slot, valid = route("eq", n), route("logits", n)
            link(nc.vector.tensor_reduce(slot, at.rearrange("p (n e) -> p n e", e=E), AX, ALU.add))
            link(nc.vector.tensor_reduce(valid, ok.rearrange("p (n e) -> p n e", e=E), AX, ALU.add))
            link(tt(route("m0", n), route("m0", n), valid, ALU.mult))
            link(cp(place[:, 1], slot))
            link(tt(valid, valid, con_at("spare"), ALU.mult))
            link(tt(slot, slot, valid, ALU.subtract))
            link(tt(slot, slot, con_at("spare"), ALU.add))
            cp(place[:, 0], slot).then_inc(s_r["slots"], 1)
            dve.wait_ge(s_lin["consts"], 1)
            link(ts(col("half_alpha"), col("t3"), 0.5, None, ALU.mult))
            ts(col("t2"), col("t"), 1.0, None, ALU.add).then_inc(s_lin["one_plus"], 1)
            dve.wait_ge(s_lin["consts"], 2)
            link(tt(decay[:, :], decay[:, :], con_at("causal"), ALU.mult))
            s = ln["ln5"]
            for e in range(E):
                dve.wait_ge(s_mo, e + 1)
                if e >= 2:
                    dve.wait_ge(s_moe_st[e % 2], 16 * (e // 2))
                tt(expert_y(e), bank[:, 4 + e % 2].rearrange("p (t d) -> p t d", d=D),
                   mb2[:, e:e + 1].to_broadcast([P, 4, D]), ALU.add).then_inc(s_moe["out"], 1)

            def head(t):
                dve.wait_ge(s_fetch[t % 4], 32 * (t // 4 + 1))
                link(stt(work[:, t], fetched(0, t), route("m0", NT)[:, t:t + 1], x_tok[:, t], ALU.mult, ALU.add))
                link(stt(work[:, t], fetched(1, t), route("m1", NT)[:, t:t + 1], work[:, t], ALU.mult, ALU.add))

            def tail(t):
                ln_apply(dve, s, t, x_tok[:, t]).then_inc(s["y"], 1)
            ln_dve(dve, s, link, head, tail)
            s = ln["ln6"]
            for q in range(NQ + 2):
                if q < NQ:
                    dve.wait_ge(s_lin["scores"], q + 1)
                    if q >= 2:
                        dve.wait_ge(s_lin["read"], 4 * (q - 1))
                    tt(probs[:, q % 2, 0:512].rearrange("p (t n) -> p t n", n=P), bank[:, q % 2].rearrange("p (t n) -> p t n", n=P),
                       decay[:, None, :].to_broadcast([P, 4, P]), ALU.mult).then_inc(s_lin["masked"], 1)
                if 1 <= q <= NQ:
                    for t in range(4 * q - 4, 4 * q):
                        dve.wait_ge(s_lin["read"], 4 * q)
                        stt(work[:, t], bank[:, 4 + (q - 1) % 2, (t % 4) * P:(t % 4 + 1) * P], col("half_alpha"), x_tok[:, t],
                            ALU.mult, ALU.add).then_inc(s_lin["taken"], 1)
                        dve.wait_ge(s_lin["taken"], t + 1)
                        ln_stats(s, t)(link)
                if q >= 2:
                    for t in range(4 * q - 8, 4 * q - 4):
                        ln_apply(dve, s, t, x_tok[:, t]).then_inc(s["y"], 1)
            s = ln["ln7"]
            for j in (0, 1):
                for i in (1, 2):
                    last = nc.vector.memset(seqs(rec_b(j, i))[:, :, 0:2], 0.0)
            last.then_inc(s_rec["ready"], 1)
            dve.wait_ge(s_rec["rates"], 1)
            ed, eg = probsT[:, 0, 512:1024], probsT[:, 1, 512:1024]
            link(ts(ed, con_at("carry"), col("ed"), None, ALU.mult))
            link(ts(eg, con_at("carry"), col("eg"), None, ALU.mult))
            for q in range(NQ + 2):
                if q < NQ:
                    a, bb, m = probs[:, q % 2, 0:512], probs[:, q % 2, 512:1024], probsT[:, q % 2, 0:512]
                    c = ctxT[:, q * 512:(q + 1) * 512]
                    dve.wait_ge(s_rec["exp"], q + 1)
                    link(nc.vector.tensor_tensor_scan(bb, eg, rec_b(q, 2), 0.0, ALU.mult, ALU.add))
                    dve.wait_ge(s_rec["ekv"], q + 1)
                    link(nc.vector.tensor_tensor_scan(a, ed, rec_b(q, 1), 0.0, ALU.mult, ALU.add))
                    link(tt(bb, bb, c, ALU.mult))
                    link(tt(bb, bb, con_at("steps"), ALU.add))
                    link(tt(bb, bb, rec_b(q, 3), ALU.mult))
                    link(tt(bb, bb, a, ALU.add))
                    if q >= 2:
                        dve.wait_ge(s_rec["tok"], q - 1)
                    tt(m, bb, xT[:, q * 512:(q + 1) * 512], ALU.add).then_inc(s_rec["sum"], 1)
                if 1 <= q <= NQ:
                    dve.wait_ge(s_rec["taken"], q)
                    for t in range(4 * q - 4, 4 * q):
                        ln_stats(s, t)(link)
                if q >= 2:
                    for t in range(4 * q - 8, 4 * q - 4):
                        ln_apply(dve, s, t, x_tok[:, t]).then_inc(s["y"], 1)
            cp(w_pos[:, 1], pos_i[:, :])
            dve.wait_ge(s_sel["weights"], 1)
            ts(w_pos[:, 0], bank[:, 0, 0:NT], col("router_b"), None, ALU.add).then_inc(s_sel["wcol"], 1)
            dve.wait_ge(s_sel["wcol"], 1)
            gt, tie, ge = route("gt", NT), route("tie", NT), route("ge", NT)
            for t in range(NT):
                dve.wait_ge(s_sel["rows"], t // 4 + 1)
                if t >= 5:
                    dve.wait_ge(s_sel["ranked"], t - 4)
                row = bank[:, 1 + (t // 4) % 2, (t % 4) * P:(t % 4 + 1) * P]
                for n, op, m, o in ((0, ALU.is_gt, "same_seq", gt), (1, ALU.is_equal, "same_seq_before", tie), (2, ALU.is_ge, "same_seq", ge)):
                    last = stt(scrap((t % 5) * 3 + n), row, w_pos[:, 0, t:t + 1], con_at(m), op, ALU.mult, accum_out=o[:, t:t + 1])
                last.then_inc(s_sel["ranked"], 1)
            dve.wait_ge(s_sel["ranked"], NT)
            link(tt(gt, gt, tie, ALU.add))
            link(ts(tie, gt, float(NSEL), None, ALU.is_lt))
            link(tt(gt, gt, con_at("slot_base"), ALU.add))
            link(tt(gt, gt, tie, ALU.mult))
            link(ts(gt, gt, -1.0, None, ALU.add))
            link(ts(ge, ge, float(NSEL), 1.0, ALU.is_gt, ALU.add))
            for t in range(NT):
                ts(sel(t), con_at("row_index"), gt[:, t:t + 1], None, ALU.is_equal).then_inc(s_sel["sel"], 1)
            dve.wait_ge(s_sel["gathered"], 1)
            cp(slot_x0[:, :, :].rearrange("p g d -> p (g d)"), bank[:, 3, 0:NS * D])
            cp(slot_wp[:, :], bank[:, 4, 0:2 * NS])
            for b in (0, 1):
                r = slice(64 * b, 64 * b + 64)
                tt(slot_mask[r], bank[r, 7, 0:NS * P].rearrange("p (g b k) -> p g b k", b=2, k=S)[:, :, b],
                   con_at("slot_block")[r, None, :].to_broadcast([64, NS, S]), ALU.add)
            def squares_of(src):
                for g in range(NS):
                    last = stt(scrap(g + 4 * (src is slot_x)), src[:, g], 1.0, src[:, g], ALU.mult, ALU.mult,
                               accum_out=slot_s[:, g:g + 1])
                last.then_inc(s_slot["squares"], 1)

            def scaled(src, n):
                dve.wait_ge(s_slot["rms"], n)
                for g in range(NS):
                    last = ts(hT_flat[:, g * P:(g + 1) * P], src[:, g], slot_s[:, 4 + g:5 + g], None, ALU.mult)
                last.then_inc(s_slot["hn"], 1)
            ts(wqkv[:, 0:D], fqkv[:, 0:D], col("ln1"), HD ** -0.5, ALU.mult, ALU.mult)
            ts(wqkv[:, D:3 * D], fqkv[:, D:3 * D], col("ln1"), None, ALU.mult)
            link(ts(fw1[:, :], fw1[:, :], col("ln2"), None, ALU.mult))
            squares_of(slot_x0)
            link(nc.vector.memset(hT_flat[:, 3072:4096], 0.0))
            ang, k = slot_angle[:, 0], slot_angle[:, 1]
            for g in range(NS):
                link(ts(ang[:, g], con_at("inv_freq"), slot_wp[:, 2 * g + 1:2 * g + 2], None, ALU.mult))
            link(ts(k, ang, float(1 / (2 * np.pi)), 12582912.0, ALU.mult, ALU.add))
            link(ts(k, k, -12582912.0, None, ALU.add))
            link(stt(ang, k, -6.28125, ang, ALU.mult, ALU.add))
            link(stt(ang, k, float(-(2 * np.pi - 6.28125)), ang, ALU.mult, ALU.add))
            link(ts(ang, ang, 3.1415925, -3.1415925, ALU.min, ALU.max))
            link(stt(k, ang, -1.0, ang, ALU.mult, ALU.max))
            ts(k, k, -1.0, float(np.pi / 2), ALU.mult, ALU.add).then_inc(s_slot["angle"], 1)
            scaled(slot_x0, 1)
            dve.wait_ge(s_slot["trig"], 1)
            dve.wait_ge(s_slot["act"], 2)
            for g in range(NS):
                qk = bank[:, 1 + g, 0:2 * D].rearrange("p (h e) -> p h e", e=HD)
                lo, hi = qk[:, :, 0:4], qk[:, :, 4:8]
                sin = slot_trig[:, 0, g, None, :].to_broadcast([P, 2 * H, 4])
                cos = slot_trig[:, 1, g, None, :].to_broadcast([P, 2 * H, 4])
                part = lambda i: hT_flat[:, 2048 + i * 128:2048 + (i + 1) * 128]
                for i, (x, y) in enumerate(((lo, cos), (hi, sin), (hi, cos), (lo, sin))):
                    last = tt(part(4 * g + i).rearrange("p (h e) -> p h e", e=4), x, y, ALU.mult)
                link(last)
                for b in (0, 1):
                    r = slice(64 * b, 64 * b + 64)
                    z = hT_flat[r, 3072 + g * 512:3072 + (g + 1) * 512].rearrange("p (x b h e) -> p x b h e", b=2, h=8, e=HD)[:, :, b]
                    pr = lambda i: part(4 * g + i)[r].rearrange("p (x h e) -> p x h e", h=8, e=4)
                    tt(z[:, :, :, 0:4], pr(0), pr(1), ALU.subtract)
                    last = tt(z[:, :, :, 4:8], pr(2), pr(3), ALU.add)
            last.then_inc(s_slot["rope"], 1)
            dve.wait_ge(s_slot["pe"], 3)
            for h in (0, 1):
                r = slice(64 * h, 64 * h + 64)
                last = cp(v_pair[r, 0:2 * NS, :, h * (HD + 1):h * (HD + 1) + HD],
                          bank[r, 5].rearrange("p (j a h e) -> p j a h e", a=H // 2, h=2, e=HD)[:, :, :, h])
            last.then_inc(s_slot["values"], 1)
            att_dve(dve, att["slots"], NS, False, link)
            dve.wait_ge(s_slot["pe"], 5)
            link(tt(slot_x[:, :, :].rearrange("p g d -> p (g d)"), bank[:, 7, 256:512], slot_x0[:, :, :].rearrange("p g d -> p (g d)"), ALU.add))
            squares_of(slot_x)
            scaled(slot_x, 2)
            dve.wait_ge(s_slot["pe"], 8)
            link(tt(slot_x[:, :, :].rearrange("p g d -> p (g d)"), bank[:, 3, 0:256], slot_x[:, :, :].rearrange("p g d -> p (g d)"), ALU.add))
            for g in range(NS):
                last = ts(slot_x[:, g], slot_x[:, g], slot_wp[:, 2 * g:2 * g + 1], None, ALU.mult)
            last.then_inc(s_slot["hn"], 1)
            s = ln["ln8"]

            def head(t):
                dve.wait_ge(s_sel["back"], t // 4 + 1)
                link(stt(work[:, t], x_tok[:, t], ge[:, t:t + 1], bank[:, 4 + t // 4, (t % 4) * P:(t % 4 + 1) * P], ALU.mult, ALU.add))

            def tail(t):
                ln_apply(dve, s, t, x_tok[:, t]).then_inc(s["y"], 1)
            ln_dve(dve, s, link, head, tail)
            end_stage(dve, 1)


def lay_out(i):
    f = lambda n: np.asarray(i[n])
    x, c = f("x"), f("ctx_1024")
    a = {"const": CONST}
    a["x"] = x.reshape(NT, P, D).transpose(1, 0, 2)
    xr = x.reshape(NT, 2, S, 2, 64).transpose(1, 4, 0, 3, 2)
    a["k_self"] = xr.reshape(P, NT, 2, S)
    q = np.zeros((2, 64, NT, 2, 2, S), np.float32)
    q[0, :, :, :, 0], q[1, :, :, :, 1] = xr[0], xr[1]
    a["q_self"] = q.reshape(P, NT, 2, P)
    v = np.zeros((2, S, B, H // 2, 2, HD + 1), np.float32)
    xv = x.reshape(B, S, H // 2, 2, HD).transpose(3, 1, 0, 2, 4)
    for h in (0, 1):
        v[h, :, :, :, h, 0:HD] = xv[h]
        v[h, :, :, :, h, HD] = 1.0
    a["v_self"] = v.reshape(P, B, H // 2, VW)
    a["ctxT"] = c.reshape(T, D).T
    a["rows"] = np.tile(np.stack([f(n) for n in ("L0_attn_ln1_g", "L0_attn_ln1_b", "L0_attn_ln2_g", "L0_attn_ln2_b",
                                                 "L0_attn_b2", "L0_xattn_bv", "L0_xattn_bo", "L0_xattn_bo")])[None], (P, 1, 1))
    one = lambda n: np.broadcast_to(f(n).reshape(1, 1), (P, 1))
    two = lambda n: np.tile(f(n).reshape(2, 64).T, (2, 1))
    a["cols"] = np.concatenate([two("L0_xattn_bq"), two("L0_xattn_bk"), f("L0_attn_b1").reshape(FC, P).T,
                                f("L1_xattn_u")[:, None], f("L1_xattn_w")[:, None], f("L1_ffn_ln1")[:, None],
                                f("L1_ffn_ln2")[:, None], f("L1_ffn_router_w"), one("L1_attn_decay"),
                                one("L1_attn_log_alpha"), one("L1_ffn_router_b")], 1)
    a["L0_attn_W1"] = f("L0_attn_W1")
    a["L0_attn_W2"] = f("L0_attn_W2").reshape(FC, P, D).transpose(1, 0, 2)
    for n, m in (("wq", "L0_xattn_Wq"), ("wk", "L0_xattn_Wk"), ("wv", "L0_xattn_Wv"), ("wo", "L0_xattn_Wo")):
        a[n] = f(m).T
    a["L0_ffn_wg"] = f("L0_ffn_wg")
    a["mw1"] = f("L0_ffn_w1").transpose(1, 0, 2)
    a["mw2"] = f("L0_ffn_w2").reshape(E, FC, P, D).transpose(2, 0, 1, 3)
    a["mb1"] = f("L0_ffn_b1").reshape(E, FC, P).transpose(2, 0, 1)
    a["mb2"] = np.tile(f("L0_ffn_b2")[None], (P, 1, 1))
    a["w_read_write"] = np.concatenate([f("L1_attn_W_write"), f("L1_attn_W_read")], 1)
    mask = f("L1_ffn_attention_mask")[:, 0, :S, :S]
    m = np.zeros((2, S, 3, 2, S), np.float32)
    for t in range(3):
        for b in (0, 1):
            m[b, :, t, b] = mask[min(2 * t + b, len(mask) - 1)]
    a["seq_mask"] = m.reshape(P, 3, P)
    pos = f("L1_ffn_position_ids")[:, :S]
    a["pos"] = pos[np.minimum(np.arange(B), len(pos) - 1)].reshape(NT, P).T
    a["fqkv"] = np.concatenate([f("L1_ffn_wq"), f("L1_ffn_wk"), f("L1_ffn_wv")], 1)
    a["L1_ffn_wo"], a["L1_ffn_w1"] = f("L1_ffn_wo"), f("L1_ffn_w1")
    a["fw2"] = f("L1_ffn_w2").reshape(FC, P, D).transpose(1, 0, 2)
    return {n: np.ascontiguousarray(v) for n, v in a.items()}


def kernel(**inputs):
    import concourse.bacc as bacc
    from concourse.bass_utils import run_bass_kernel_spmd

    nc = bacc.Bacc("TRN2", target_bir_lowering=False, num_devices=1)
    arrays = {f"in_{n}": v for n, v in lay_out(inputs).items()}
    io = {n[3:]: nc.dram_tensor(n, v.shape, mybir.dt.from_np(v.dtype), kind="ExternalInput").ap() for n, v in arrays.items()}
    io["out"] = nc.dram_tensor("out", (P, NT, D), F32, kind="ExternalOutput").ap()
    build(nc, io)
    r = run_bass_kernel_spmd(nc, [arrays], core_ids=[0])
    return np.ascontiguousarray(np.asarray(r.results[0]["out"]).transpose(1, 0, 2)).reshape(B, S, D)
```

```python
from contextlib import ExitStack

import numpy as np
import concourse.bass as bass
from concourse import mybir

F32 = mybir.dt.float32
BF16 = mybir.dt.bfloat16
I32 = mybir.dt.int32
ALU = mybir.AluOpType
ACT = mybir.ActivationFunctionType
AX = mybir.AxisListType.X

B, S, D = 32, 64, 128
T = B * S
P = 128
NT = T // P
NQ = NT // 4
H, HD = 16, 8
F = 512
FC = F // P
E, TOPK = 8, 2
CAP = TOPK * ((T + E - 1) // E)
CT = CAP // P
LN_EPS = 1e-5
RMS_EPS = 1e-6
NEG = -1e30
KEEP = int(0.125 * S)
NSEL = KEEP - 1
BPS = P // KEEP
NS = B // BPS
BT = NT // NS
VW = 2 * (HD + 1)


def constants():
    p = np.arange(P)
    pos, seq = p % S, p // S
    k = np.arange(S)
    c = {}
    c["ident"] = np.eye(P)
    c["band"] = np.where(np.abs(pos[:, None] - k[None, :]) <= 32, 0.0, NEG)
    W = 16
    ok = (k[None] <= pos[:, None]) & (k[None] >= pos[:, None] - (W - 1)) & (k[None] <= 2 * pos[:, None] - (W - 1))
    c["window"] = np.where(ok, 0.0, NEG)
    npad = np.where(pos < W - 1, np.minimum(pos + 1, W - 1 - pos), 0)
    c["npad"] = npad[:, None]
    c["pad_ceiling"] = np.where(npad > 0, 0.0, -NEG)[:, None]
    c["head_of_row"] = ((p % 64)[:, None] // HD == np.arange(8)[None])
    c["earlier_row"] = p[:, None] < p[None, :]
    c["ones"] = np.ones((P, P))
    c["fold"] = pos[:, None] == k[None]
    for b in (0, 1):
        c[f"dup{b}"] = (seq[:, None] == b) & (pos[:, None] == pos[None, :])
    same = seq[:, None] == seq[None, :]
    c["same_seq"] = same
    c["same_seq_before"] = same & (p[None, :] < p[:, None])
    c["row_index"] = np.tile(p[None, :], (P, 1))
    c["decay_steps"] = np.maximum(p[None, :] - 1 - p[:, None], 0)
    c["causal"] = same & (p[None, :] > p[:, None]) & (pos[:, None] > 0)
    c["steps"] = np.tile(np.maximum(k - 1.0, 0.0)[None], (P, 8))
    c["carry"] = np.tile((k > 0)[None], (P, 8))
    c["first_choice"] = np.tile(E - np.arange(E)[None], (P, 1))
    c["rank_base"] = np.tile((P * np.arange(CT))[None], (P, 1))
    c["row"] = p[:, None]
    c["tile_from_1"] = np.tile(1 + np.arange(TOPK * NT)[None], (P, 1))
    c["spare"] = P + TOPK * T + P * np.arange(E * CT)[None] + p[:, None]
    c["slot_base"] = KEEP * ((2 * np.arange(NT)[None] + seq[:, None]) % BPS) + 1
    sp, sk = p % 64, k
    c["slot_block"] = np.where((sp[:, None] // KEEP == sk[None] // KEEP) & (sk[None] % KEEP < NSEL), 0.0, NEG)
    c["inv_freq"] = np.tile((1.0 / np.float32(10000.0) ** (np.arange(0, HD, 2, dtype=np.float32) / np.float32(HD)))[None], (P, 1))
    c["scan_carry"] = np.tile((np.arange(2 * NT) > 0)[None], (P, E))
    at, cols = {}, []
    n = 0
    first = ("ident", "band", "window", "npad", "pad_ceiling", "head_of_row")
    for name in [*first, *(n for n in c if n not in first)]:
        a = c[name]
        a = np.asarray(a, np.float32)
        at[name] = (n, a.shape[1])
        n += a.shape[1]
        cols.append(a)
    return at, np.ascontiguousarray(np.concatenate(cols, 1))


CONST_AT, CONST = constants()


def build(nc, io):
    with ExitStack() as ctx:
        def sb(name, shape, dt=F32):
            return ctx.enter_context(nc.sbuf_tensor(name, [P] + shape, dt))

        def sem(name):
            return ctx.enter_context(nc.semaphore(name))

        x_tok = sb("x_tok", [NT, D])
        x_side = sb("x_side", [NT, D])
        work = sb("work", [NT, D])
        xT0 = sb("xT0", [T + 1])
        xT = xT0[:, 1:T + 1]
        ctxT = sb("ctxT", [T])
        q_diag = sb("q_diag", [NT, 2, P])
        k_comp = sb("k_comp", [NT, 2, S])
        v_pair = sb("v_pair", [B, H // 2, VW])
        k_heads = sb("k_heads", [2, 2, 8, S])
        probs = sb("probs", [2, H * S])
        probsT = sb("probsT", [2, H * S])
        neg_max = sb("neg_max", [2, H])
        neg_cap = sb("neg_cap", [2, H])
        neg_max0 = sb("neg_max0", [4, H])
        pad_exp = sb("pad_exp", [4, H])
        denom = sb("denom", [2, H])
        r_denom = sb("r_denom", [2, H])
        stats = sb("stats", [NT, 6])
        mv = sb("mv", [NT, 2])
        var_e = sb("var_e", [NT])
        rstd = sb("rstd", [NT])
        neg_half = sb("neg_half", [NT])
        con = sb("con", [CONST.shape[1]])
        ident_bf = sb("ident_bf", [P], BF16)
        mask_bf = sb("mask_bf", [2, S], BF16)
        row_index_bf = sb("row_index_bf", [P], BF16)
        rows = sb("rows", [8, D])
        cols = sb("cols", [64])
        aw1 = sb("aw1", [F])
        aw2 = sb("aw2", [FC, D])
        wq = sb("wq", [D])
        wk = sb("wk", [D])
        wv = sb("wv", [D])
        wo = sb("wo", [D])
        wg = sb("wg", [E])
        mw1 = sb("mw1", [E, F])
        mw2 = sb("mw2", [E, FC, D])
        mb1 = sb("mb1", [E, FC])
        mb2 = sb("mb2", [E, D])
        hT = sb("hT", [2, FC, 512])

        v_rows = hT[:, 1].rearrange("p f n -> p (f n)")

        hT_flat = hT[:, :, :, :].rearrange("p a f n -> p (a f n)")
        wcomb = sb("wcomb", [4 * P])
        decay = sb("decay", [P])
        seq_mask = sb("seq_mask", [3, P])
        pos_i = sb("pos_i", [NT], I32)
        w_pos = sb("w_pos", [2, NT])
        fqkv = sb("fqkv", [3 * D])
        wqkv = sb("wqkv", [3 * D])
        fwo = sb("fwo", [D])
        fw1 = sb("fw1", [F])
        fw2 = sb("fw2", [FC, D])
        slot_x0 = sb("slot_x0", [NS, D])
        slot_x = sb("slot_x", [NS, D])
        slot_wp = sb("slot_wp", [2 * NS])
        slot_mask = sb("slot_mask", [NS, S])
        slot_s = sb("slot_s", [8])
        slot_angle = sb("slot_angle", [2, NS, 4])
        slot_trig = sb("slot_trig", [2, NS, 4])
        routing = sb("routing", [2048])
        ROUTE = {"onehot": 0, "logits": 256, "eq": 384, "gate": 512, "tot": 640, "run": 896, "at": 1152, "m0": 1408,
                 "m1": 1424, "c": 1440, "e": 1456, "gt": 1472, "tie": 1488, "ge": 1504}

        place = sb("place", [2, E * CT], I32)
        inside = sb("inside", [3, TOPK * NT * CT])
        told_bf = sb("told_bf", [TOPK * NT, CT, 2], BF16)
        room_bf = sb("room_bf", [TOPK * NT, E], BF16)
        rank_row = sb("rank_row", [TOPK * NT], BF16)
        rank_hot = k_heads[:, :, :, :, :].rearrange("p a g h k -> p (a g h k)").bitcast(BF16).rearrange("p (n r) -> p n r", r=P)
        slot_hot = probs[:, 0].bitcast(BF16).rearrange("p (n e c) -> p n e c", e=E, c=2 * CT)
        token_rows = nc.dram_tensor("token_rows", (T, D), F32, kind="Internal").ap()
        choice_rows = nc.dram_tensor("choice_rows", (TOPK * T + E * CAP, D), F32, kind="Internal").ap()

        def expert_x(e):
            return q_diag[:, 2 * e:2 * e + 2].rearrange("p t g n -> p (t g) n")

        def expert_y(e):
            return probsT[:, e % 2, 0:512].rearrange("p (t d) -> p t d", d=D)

        def fetched(k, t):
            return x_side[:, t] if k == 0 else k_comp[:, t].rearrange("p g s -> p (g s)")

        with_b2 = routing[:, :].rearrange("p (t d) -> p t d", d=D)

        def route(name, n):
            return routing[:, ROUTE[name]:ROUTE[name] + n]

        def sel(t):
            return mw1[:, t // 4, (t % 4) * P:(t % 4 + 1) * P]

        def selT(t):
            return mw1[:, 4 + t // 4, (t % 4) * P:(t % 4 + 1) * P]

        def rope_z(g, which, half):
            at = 3072 + g * 512 + which * 256 + half * P
            return hT_flat[:, at:at + P]

        def scrap(i):
            return mw2[:, i // 4, i % 4]

        k_flat = k_heads[:, :, :, :, :].rearrange("p a g h k -> p (a g h k)")

        def masked(q):
            return k_flat[:, (q % 2) * 512:(q % 2 + 1) * 512]

        def values_sb(q):
            return k_flat[:, 1024 + (q % 2) * 512:1024 + (q % 2 + 1) * 512]

        def back(t):
            return bank[:, 4 + t // 4, (t % 4) * P:(t % 4 + 1) * P]

        def seqs(ap):
            return ap.rearrange("p (b s) -> p b s", s=S)

        def rec_b(q, i):
            return hT[:, q % 2, i]

        def con_at(name):
            a, n = CONST_AT[name]
            return con[:, a:a + n]

        ident = con_at("ident")
        COL = {"bq": 0, "bk": 2, "b1": 4, "u": 8, "w": 9, "ln1": 10, "ln2": 11, "router": 12, "decay": 13,
               "log_alpha": 14, "router_b": 15, "half_alpha": 16, "log_gamma": 17, "ed": 18, "eg": 19, "t": 20, "t2": 21, "t3": 22, "bq_scaled": 23}

        def col(name, n=1):
            return cols[:, COL[name]:COL[name] + n]

        bank = ctx.enter_context(nc.psum_tensor("bank", [P, 8, 512], F32))

        s_con = sem("s_con")
        s_x = sem("s_x")
        s_k_in = [sem(f"keys_in{q}") for q in range(NQ)]
        s_quad_in = [sem(f"quad_in{q}") for q in range(NQ)]
        s_built, s_v_clear = sem("s_built"), sem("s_v_clear")
        s_w = sem("s_w")
        s_out = sem("s_out")
        s_setup = sem("s_setup")
        stage_end = sem("stage_end")
        s_dve = sem("s_dve")
        s_pool = sem("s_pool")
        s_act = sem("s_act")
        s_pe = sem("s_pe")

        def names(stage, *what):
            return {n: sem(f"{stage}_{n}") for n in what}

        class Chain:
            def __init__(self, eng, s):
                self.eng, self.s, self.n = eng, s, 0

            def mark(self, ins):
                self.n += 1
                ins.then_inc(self.s, 1)
                return self.n

            def wait(self, n):
                self.eng.wait_ge(self.s, n)

            def __call__(self, ins):
                self.wait(self.mark(ins))

        def end_stage(eng, n):
            eng.drain().then_inc(stage_end, 1)
            eng.wait_ge(stage_end, 4 * n)

        ATT = ("spread", "scores", "shifted", "exp", "transposed", "evacuated", "weighted", "taken", "seeded", "max", "pad")
        att = {s: names(s, *ATT[:n]) for s, n in (("self", len(ATT) - 2), ("cross", len(ATT)), ("slots", len(ATT) - 3))}
        LNS = ("stats", "rstd", "y", "yT", "yT_out")
        norm_sems = names("norm", *LNS)
        ln = {s: {**norm_sems, "tiles": NT * i, "quads": NQ * i}
              for i, s in enumerate(("ln1", "ln3", "ln4", "ln5", "ln8"))}
        ln["ln2"] = {**names("norm2", "stats", "rstd"), "tiles": 0, "quads": 0}
        for s in ("ln6", "ln7"):
            ln[s] = {**names(s, *LNS), "tiles": 0, "quads": 0}
        ln["ln1"]["banks"] = ln["ln3"]["banks"] = (7,)
        ln["ln5"]["banks"], ln["ln6"]["banks"], ln["ln7"]["banks"] = (3,), (4,), (5,)
        s_h, s_hT, s_o = (sem(n) for n in ("ffn_h", "ffn_hT", "ffn_out"))
        s_mh, s_mhT, s_mo = (sem(n) for n in ("moe_h", "moe_hT", "moe_out"))
        s_side, s_shift = sem("s_side"), sem("s_shift")
        s_kv, s_q, s_v_free, s_k_free, s_q_free = (sem(n) for n in ("s_kv", "s_q", "s_v_free", "s_k_free", "s_q_free"))
        s_oT, s_oTs, s_wo = sem("s_oT"), sem("s_oTs"), sem("s_wo")
        s_r = names("route", "logits", "chosen", "ranks", "gap", "exp", "slots", "rows", "hot", "hot2", "found")
        s_moe = names("experts", "zeroed", "stored", "turned", "xT", "out")
        s_moe_in = [sem(f"moe_in{e}") for e in range(E)]
        s_moe_st = [sem(f"moe_placed{i}") for i in (0, 1)]
        s_lin = names("lin", "w", "w_sb", "consts", "one_plus", "scores", "masked", "v", "v_sb", "read", "taken", "gated", "added")
        s_rec = names("rec", "ready", "rates", "exp", "ekv", "sum", "tok", "taken", "scan", "exp_k")
        s_sel = names("sel", "weights", "wcol", "rows", "ranked", "sel", "half", "half_sb", "gathered", "turned", "selT", "back", "share", "kept", "out")
        s_slot = names("slot", "squares", "rms", "hn", "pe", "act", "angle", "trig", "rope", "keys", "values", "mask")

        block = ctx.enter_context(nc.Block())

        def head_view(ap):
            return ap.rearrange("p (h k) -> p h k", k=S)

        def o_view(i):
            return bank[:, 6 + i % 2, 0:H * (HD + 1)].rearrange("p (h e) -> p h e", e=HD + 1)

        def att_spread(pool, s, n, before=None, after=None, mult=nc.gpsimd.tensor_tensor, first=0):
            hm = con_at("head_of_row")[:, None, :, None].to_broadcast([P, 2, 8, S])
            for i in range(first, n):
                if before:
                    before(i)
                if i >= 2:
                    pool.wait_ge(s["scores"], i - 1)
                mult(k_heads[:, i % 2], k_comp[:, i, :, None, :].to_broadcast([P, 2, 8, S]),
                                        hm, ALU.mult).then_inc(s["spread"], 1)
                if after:
                    after(i)

        def att_pe(pe, s, n, mask_lhs, mask_of, seed, have_q=None, have_v=None, beside=None, after_first=None):
            def put_mask(bk):
                nc.tensor.matmul(bank[:, bk, :], mask_lhs, mask_of(bk // 2), start=True, stop=False)

            def scores(i):
                if have_q:
                    have_q(i)
                if i < 2 and seed:
                    put_mask(2 * i)
                    put_mask(2 * i + 1)
                elif i == 0:
                    put_mask(1)
                    put_mask(2)
                elif not seed:
                    put_mask(3)
                pe.wait_ge(s["spread"], i + 1)
                if i >= 2:
                    pe.wait_ge(s["seeded"], i - 1)
                for g in (0, 1):
                    last = nc.tensor.matmul(bank[:, 2 * (i % 2) + g, :], q_diag[:, i, g],
                                            k_heads[:, i % 2, g].rearrange("p h k -> p (h k)"),
                                            start=False, stop=True, skip_group_check=i >= 2)
                last.then_inc(s["scores"], 1)

            def turn(i):
                pe.wait_ge(s["exp"], i + 1)
                if i >= 1:
                    pe.wait_ge(s["evacuated"], i)
                for hp in range(H // 2):
                    last = nc.tensor.transpose(bank[:, 4 + hp // 4, (hp % 4) * P:(hp % 4 + 1) * P],
                                               probs[:, i % 2, hp * P:(hp + 1) * P], ident)
                last.then_inc(s["transposed"], 1)

            def weigh(i):
                if have_v:
                    have_v(i)
                pe.wait_ge(s["evacuated"], i + 1)
                if i >= 2:
                    pe.wait_ge(s["taken"], i - 1)
                for b in (0, 1):
                    for hp in range(H // 2):
                        at = hp * P + b * S
                        last = nc.tensor.matmul(bank[b * S:(b + 1) * S, 6 + i % 2, hp * VW:(hp + 1) * VW],
                                                probsT[:, i % 2, at:at + S], v_pair[:, 2 * i + b, hp],
                                                start=True, stop=True)
                last.then_inc(s["weighted"], 1)

            for i in range(n + 2):
                if i < n:
                    scores(i)
                if after_first and i == 0:
                    after_first()
                if beside and i == n:
                    beside(0)
                if 1 <= i <= n:
                    turn(i - 1)
                if beside and i == n + 1:
                    beside(1)
                if i >= 2:
                    weigh(i - 2)

        def att_act(act, s, n, pad, mask, beside=None):
            def put_mask(i):
                act.wait_ge(s["shifted"], i - 1)
                nc.scalar.copy(bank[:, 2 * (i % 2):2 * (i % 2) + 2, :].rearrange("p a (h k) -> p (a h) k", k=S),
                               mask[:, None, :].to_broadcast([P, H, S])).then_inc(s["seeded"], 1)

            def evac(i):
                act.wait_ge(s["transposed"], i + 1)
                if i >= 2:
                    act.wait_ge(s["weighted"], i - 1)
                nc.scalar.copy(probsT[:, i % 2], bank[:, 4:6, :].rearrange("p a n -> p (a n)")).then_inc(s["evacuated"], 1)

            for i in range(n):
                if i >= 1:
                    evac(i - 1)
                if pad:
                    act.wait_ge(s["max"], i + 1)
                    if i >= 4:
                        act.wait_ge(s["taken"], i - 3)
                    nc.scalar.activation(pad_exp[:, i % 4], neg_max0[:, i % 4], ACT.Exp).then_inc(s["pad"], 1)
                act.wait_ge(s["shifted"], i + 1)
                nc.scalar.activation(probs[:, i % 2], probs[:, i % 2], ACT.Exp).then_inc(s["exp"], 1)
                if i + 2 < n:
                    put_mask(i + 2)
            if beside:
                beside()
            evac(n - 1)

        def att_dve(dve, s, n, pad, link, also=None, beside=None):
            def step(i, j):
                if i is not None:
                    m, capped = neg_max[:, i % 2], neg_cap[:, i % 2]
                    sc = bank[:, 2 * (i % 2):2 * (i % 2) + 2, :].rearrange("p a (h k) -> p (a h) k", k=S)
                    dve.wait_ge(s["scores"], i + 1)
                    have_m = link.mark(nc.vector.tensor_reduce(m, sc, AX, ALU.max, negate=True))
                if j is not None:
                    d, r = denom[:, j % 2], r_denom[:, j % 2]
                    sums = o_view(j)[:, :, HD]
                    dve.wait_ge(s["weighted"], j + 1)
                    if pad:
                        dve.wait_ge(s["pad"], j + 1)
                        have_d = link.mark(nc.vector.scalar_tensor_tensor(
                            d, pad_exp[:, j % 4], con_at("npad"), sums, ALU.mult, ALU.add))
                    else:
                        have_r = link.mark(nc.vector.reciprocal(r, sums))
                if also:
                    also(i if i is not None else j + 3)
                if i is not None:
                    link.wait(have_m)
                    if pad:
                        if i >= 4:
                            dve.wait_ge(s["pad"], i - 3)
                        nc.vector.tensor_scalar(neg_max0[:, i % 4], m, 0.0, None, ALU.min).then_inc(s["max"], 1)
                        have_m = link.mark(nc.vector.tensor_scalar(capped, m, con_at("pad_ceiling"), None, ALU.min))
                        m = capped
                if j is not None and pad:
                    link.wait(have_d)
                    have_r = link.mark(nc.vector.reciprocal(r, d))
                if i is not None:
                    link.wait(have_m)
                    if i >= 2:
                        dve.wait_ge(s["transposed"], i - 1)
                    nc.vector.tensor_tensor(head_view(probs[:, i % 2]), sc, m[:, :, None].to_broadcast([P, H, S]),
                                            ALU.add).then_inc(s["shifted"], 1)
                if j is not None:
                    link.wait(have_r)
                    nc.vector.tensor_tensor(work[:, j].rearrange("p (h d) -> p h d", d=HD), o_view(j)[:, :, 0:HD],
                                            r[:, :, None].to_broadcast([P, H, HD]), ALU.mult).then_inc(s["taken"], 1)

            for i in range(n + 3):
                if beside and i == n + 2:
                    beside()
                step(i if i < n else None, i - 3 if i >= 3 else None)

        def ln_stats(s, t):
            def f(link):
                link(nc.vector.bn_stats(stats[:, t], work[:, t]))
                nc.vector.bn_aggr(mv[:, t], stats[:, t]).then_inc(s["stats"], 1)
            return f

        def ln_apply(dve, s, t, out):
            dve.wait_ge(s["rstd"], s["quads"] + t // 4 + 1)
            return nc.vector.tensor_scalar(out, work[:, t], mv[:, t, 0:1], rstd[:, t:t + 1], ALU.subtract, ALU.mult)

        def ln_dve(dve, s, link, head, tail, lag=8):
            summed, told = {}, {}
            for t in range(NT + lag):
                if t < NT:
                    summed[t] = link.mark(head(t))
                if 1 <= t <= NT:
                    link.wait(summed[t - 1])
                    told[t - 1] = link.mark(nc.vector.bn_stats(stats[:, t - 1], work[:, t - 1]))
                if 2 <= t <= NT + 1:
                    link.wait(told[t - 2])
                    nc.vector.bn_aggr(mv[:, t - 2], stats[:, t - 2]).then_inc(s["stats"], 1)
                if t >= lag:
                    tail(t - lag)

        def rstd_of(pool, s, q, link, eps=LN_EPS):
            t = 4 * q
            pool.wait_ge(s["stats"], s["tiles"] + t + 4)
            link(nc.gpsimd.tensor_scalar(var_e[:, t:t + 4], mv[:, t:t + 4, 1], eps, None, ALU.add))
            nc.gpsimd.tensor_tensor(rstd[:, t:t + 4], var_e[:, t:t + 4], neg_half[:, t:t + 4], ALU.pow).then_inc(s["rstd"], 1)

        def ln_pool(pool, s, link, eps=LN_EPS):
            for q in range(NQ):
                rstd_of(pool, s, q, link, eps)

        def ln_pe(pe, s, quad, src, other=None):
            banks = s.get("banks", (6, 7))
            bk = banks[quad % len(banks)] if other is None else other
            if s["quads"] + quad >= len(banks):
                pe.wait_ge(s["yT_out"], s["quads"] + quad + 1 - len(banks))
            for j in range(4):
                t = 4 * quad + j
                pe.wait_ge(s["y"], s["tiles"] + t + 1)
                last = nc.tensor.transpose(bank[:, bk, j * P:(j + 1) * P], src[:, t], ident)
            last.then_inc(s["yT"], 1)

        def ln_act(act, s, quad, other=None):
            act.wait_ge(s["yT"], s["quads"] + quad + 1)
            banks = s.get("banks", (6, 7))
            nc.scalar.copy(xT[:, quad * 512:(quad + 1) * 512],
                           bank[:, banks[quad % len(banks)] if other is None else other, :]).then_inc(s["yT_out"], 1)

        LOADS = ((rows[:, :, :], "rows"), (cols[:, 0:16], "cols"), (aw1[:, :], "L0_attn_W1"),
                 (aw2[:, :, :], "L0_attn_W2"), (wq[:, :], "wq"), (wk[:, :], "wk"), (wv[:, :], "wv"),
                 (wo[:, :], "wo"), (wg[:, :], "L0_ffn_wg"), (ctxT[:, :], "ctxT"), (mw1[:, :, :], "mw1"),
                 (mw2[:, :, :, :], "mw2"), (mb1[:, :, :], "mb1"), (mb2[:, :, :], "mb2"),
                 (wcomb[:, 0:2 * P], "w_read_write"), (seq_mask[:, :, :], "seq_mask"), (pos_i[:, :], "pos"),
                 (fqkv[:, :], "fqkv"), (fwo[:, :], "L1_ffn_wo"), (fw1[:, :], "L1_ffn_w1"), (fw2[:, :, :], "fw2"))
        N_W = len(LOADS) + 1
        SHIFTS = [("ln5", 2), ("ln7", 0), ("ln5", 3), ("ln7", 1), ("ln7", 2)]
        BY_ACT = 2
        LAST_BANKS = (5, 6, 7, 4)
        AHEAD = 4
        CON_FIRST = sum(CONST_AT["head_of_row"])

        @block.sync
        def _(sp):
            sp.dma_start(con[:, 0:CON_FIRST], io["const"][:, 0:CON_FIRST]).then_inc(s_con, 16)
            for q in range(NQ):
                sp.dma_start(k_comp[:, 4 * q:4 * q + 4], io["k_self"][:, 4 * q:4 * q + 4]).then_inc(s_k_in[q], 16)
                sp.dma_start(v_rows[:, 512 * q:512 * (q + 1)], io["v_self"][:, 512 * q:512 * (q + 1)]).then_inc(s_quad_in[q], 16)
            sp.dma_start(x_tok[:, :, :], io["x"]).then_inc(s_x, 16)
            sp.dma_start(con[:, CON_FIRST:], io["const"][:, CON_FIRST:]).then_inc(s_w, 16)
            for dst, src in LOADS:
                sp.dma_start(dst, io[src]).then_inc(s_w, 16)
            sp.wait_ge(s_setup, 3)
            sp.dma_start(choice_rows[0:TOPK * T, :].rearrange("(n p) d -> p n d", p=P),
                         hT[:, 0, 0, None, 0:D].to_broadcast([P, TOPK * NT, D])).then_inc(s_moe["zeroed"], 16)
            sp.wait_ge(s_w, 16 * N_W)
            sp.wait_ge(s_x, 16)
            for q in range(NQ):
                sp.wait_ge(ln["ln4"]["y"], ln["ln4"]["tiles"] + 4 * q + 4)
                sp.dma_start(token_rows[q * 512:(q + 1) * 512, :].rearrange("(n p) d -> p n d", p=P),
                             x_tok[:, 4 * q:4 * q + 4]).then_inc(s_moe["stored"], 16)
            sp.wait_ge(s_moe["stored"], 16 * NQ)
            for b in (0, 1):
                sp.wait_ge(s_moe_st[b], 16 * CT * E // 2)
            for q in range(NQ):
                for k, dst in ((0, x_side[:, 4 * q:4 * q + 4]), (1, k_comp[:, 4 * q:4 * q + 4].rearrange("p t g s -> p t (g s)"))):
                    at = k * T + q * 512
                    sp.dma_start(dst, choice_rows[at:at + 512, :].rearrange("(n p) d -> p n d", p=P)).then_inc(s_quad_in[q], 16)
            for q in range(NQ):
                if q < BY_ACT:
                    sp.wait_ge(s_sel["out"], q + 1)
                else:
                    sp.wait_ge(ln["ln8"]["y"], ln["ln8"]["tiles"] + 4 * (q - BY_ACT) + 4)
                sp.dma_start(io["out"][:, 4 * q:4 * q + 4], x_tok[:, 4 * q:4 * q + 4]).then_inc(s_out, 16)
            sp.wait_ge(s_out, 16 * NQ)
            sp.wait_ge(stage_end, 4)

        @block.gpsimd
        def _(pool):
            link = Chain(pool, s_pool)
            tt, ts = nc.gpsimd.tensor_tensor, nc.gpsimd.tensor_scalar
            link(nc.gpsimd.memset(neg_half[:, :], -0.5))
            link(nc.gpsimd.memset(hT[:, 0, 0, 0:D], 0.0))
            nc.gpsimd.memset(xT0[:, 0:1], 0.0).then_inc(s_setup, 1)
            nc.gpsimd.memset(v_pair[:, :, :, :], 0.0).then_inc(s_v_clear, 1)
            pool.wait_ge(s_v_clear, 1)
            for h in (0, 1):
                nc.gpsimd.memset(v_pair[64 * h:64 * h + 64, :, :, h * (HD + 1) + HD], 1.0).then_inc(s_v_clear, 1)
                pool.wait_ge(s_v_clear, 2 + h)
            pool.wait_ge(s_con, 16)

            def keys_here(i):
                if i % 4 == 0:
                    pool.wait_ge(s_k_in[i // 4], 16)

            def norm1(i):
                if i % 4 == 3 and 0 <= (i - 11) // 4 < NQ:
                    rstd_of(pool, ln["ln1"], (i - 11) // 4, link)
                if i == 14:
                    pool.wait_ge(s_w, 16 * N_W)
                q = (i - 16) // 4
                if i % 4 == 0 and 0 <= q < NQ:
                    pool.wait_ge(ln["ln1"]["y"], 4 * q + 4)
                    tt(with_b2[:, 4 * q:4 * q + 4], x_side[:, 4 * q:4 * q + 4], rows[:, 4:5].to_broadcast([P, 4, D]),
                       ALU.add).then_inc(s_side, 1)
                    link(tt(x_tok[:, 4 * q:4 * q + 4], x_tok[:, 4 * q:4 * q + 4], rows[:, 3:4].to_broadcast([P, 4, D]), ALU.add))
            att_spread(pool, att["self"], NT, keys_here, norm1)
            for i in range(NT, 2 * NT):
                norm1(i)
            for q in range(NQ + 1):
                if q < NQ:
                    rstd_of(pool, ln["ln2"], q, link)
                if q == NQ:
                    pool.wait_ge(s_k_free, 1)
                    att_spread(pool, att["cross"], 1)
                if q >= 1:
                    rstd_of(pool, ln["ln3"], q - 1, link)
            def cross_keys(i):
                if i % 4 == 0:
                    pool.wait_ge(s_k_free, i // 4 + 1)

            def add_bo(i):
                q = i - 2
                if 0 <= q < NQ:
                    pool.wait_ge(ln["ln3"]["y"], ln["ln3"]["tiles"] + 4 * q + 4)
                    tt(x_side[:, 4 * q:4 * q + 4], x_tok[:, 4 * q:4 * q + 4], rows[:, 6:7].to_broadcast([P, 4, D]),
                       ALU.add).then_inc(s_side, 1)
            att_spread(pool, att["cross"], NT, cross_keys, add_bo, first=1)
            ln_pool(pool, ln["ln4"], link)
            pool.wait_ge(s_r["rows"], 1)
            for c in range(TOPK * NT // 8):
                r = slice(8 * c, 8 * c + 8)
                tt(slot_hot[:, r], room_bf[:, r, :, None].to_broadcast([P, 8, E, 2 * CT]),
                   told_bf[:, r].rearrange("p n j c -> p n (j c)")[:, :, None, :].to_broadcast([P, 8, E, 2 * CT]),
                   ALU.mult).then_inc(s_r["hot2"], 1)
            def fetch(e):
                for j in range(CT):
                    nc.gpsimd.indirect_dma_start(
                        out=expert_x(e)[:, j], out_offset=None, in_=token_rows[:, :],
                        in_offset=bass.IndirectOffsetOnAxis(ap=place[:, 0, e * CT + j:e * CT + j + 1], axis=0)).then_inc(s_moe_in[e], 16)
            pool.wait_ge(s_moe["stored"], 16 * NQ)
            pool.wait_ge(s_moe["zeroed"], 16)
            pool.wait_ge(s_r["slots"], 1)
            for e in range(AHEAD):
                fetch(e)
            for e in range(E):
                pool.wait_ge(s_moe["out"], e + 1)
                for j in range(CT):
                    at = e * CT + j
                    if e == E - 1:
                        pool.wait_ge(s_moe["out"], e + j + 1)
                    nc.gpsimd.indirect_dma_start(
                        out=choice_rows[:, :], out_offset=bass.IndirectOffsetOnAxis(ap=place[:, 1, at:at + 1], axis=0),
                        in_=expert_y(e)[:, j], in_offset=None).then_inc(s_moe_st[e % 2], 16)
                if e + AHEAD < E:
                    fetch(e + AHEAD)
            def add_first(q):
                pool.wait_ge(s_lin["gated"], q)
                side = x_side[:, 4 * q:4 * q + 4]
                tt(side, side, x_tok[:, 4 * q:4 * q + 4], ALU.add).then_inc(s_lin["added"], 1)
            rstd_of(pool, ln["ln5"], 0, link)
            add_first(1)
            for w in range(NQ + 2):
                if w + 1 < NQ:
                    rstd_of(pool, ln["ln5"], w + 1, link)
                if w + 2 < NQ:
                    add_first(w + 2)
                q = w - 1
                if 0 <= q < NQ:
                    rstd_of(pool, ln["ln6"], q, link, LN_EPS / 4)
                if w >= 2:
                    rstd_of(pool, ln["ln7"], w - 2, link)
                if 0 <= q < NQ:
                    if q >= 2:
                        pool.wait_ge(s_rec["sum"], q - 1)
                    pool.wait_ge(s_rec["exp_k"], q + 1)
                    tt(seqs(rec_b(q, 1))[:, :, 2:S], seqs(rec_b(q, 0))[:, :, 1:S - 1],
                       seqs(ctxT[:, q * 512:(q + 1) * 512])[:, :, 1:S - 1], ALU.mult).then_inc(s_rec["ekv"], 1)
            def keep(q):
                pool.wait_ge(s_sel["share"], q + 1)
                for t in range(4 * q, 4 * q + 4):
                    last = ts(x_side[:, t], x_tok[:, t], route("ge", NT)[:, t:t + 1], None, ALU.mult)
                last.then_inc(s_sel["kept"], 1)
            for q in range(NQ - 1):
                keep(q)
            def rms(n):
                pool.wait_ge(s_slot["squares"], n)
                link(ts(slot_s[:, 2:4], slot_s[:, 0:2], 1.0 / D, RMS_EPS, ALU.mult, ALU.add))
                tt(slot_s[:, 4:6], slot_s[:, 2:4], neg_half[:, 0:2], ALU.pow).then_inc(s_slot["rms"], 1)
            rms(1)
            keep(NQ - 1)
            rms(2)
            ln_pool(pool, ln["ln8"], link)
            end_stage(pool, 1)

        @block.tensor
        def _(pe):
            mm, tr = nc.tensor.matmul, nc.tensor.transpose

            def cols4(bk, j, n=P):
                return bank[:, bk, j * n:(j + 1) * n]

            pe.wait_ge(s_con, 16)
            pe.wait_ge(s_setup, 3)
            mb = lambda j: (lambda i: mask_bf[:, j, None, :].to_broadcast([P, 8, S]))
            def turn_first(k):
                if k == 0:
                    pe.wait_ge(att["self"]["shifted"], NT - 1)
                    ln_pe(pe, ln["ln1"], 0, x_side, 1)
            att_pe(pe, att["self"], NT, ident_bf[:, :], mb(0), True,
                   lambda i: pe.wait_ge(s_built, 2 * (i // 4) + 1), lambda i: pe.wait_ge(s_built, 2 * (i // 4) + 2),
                   turn_first)
            pe.wait_ge(att["self"]["taken"], NT)
            def project(w, src, bk, q):
                sv = src[:, q * 512:(q + 1) * 512].rearrange("p (t b s) -> p t b s", b=2, s=S)
                for g in (0, 1):
                    for b in (0, 1):
                        last = mm(bank[b * 64:(b + 1) * 64, bk, g * 256:(g + 1) * 256], w[:, g * 64:(g + 1) * 64],
                                  sv[:, :, b, :], start=True, stop=True)
                return last

            def keys_values(q):
                if q >= 1:
                    pe.wait_ge(s_v_free, q)
                    pe.wait_ge(s_k_free, q)
                project(wk, ctxT, 5, q)
                for j in range(8):
                    at = (8 * q + j) * S
                    for h in (0, 1):
                        last = mm(bank[h * 64:(h + 1) * 64, 6, j * 64:(j + 1) * 64], ctxT[:, at:at + S],
                                  wv[:, :].rearrange("p (a h e) -> p a h e", h=2, e=HD)[:, :, h], start=True, stop=True)
                last.then_inc(s_kv, 1)

            pe.wait_ge(s_w, 16 * N_W)
            for q in range(NQ):
                pe.wait_ge(ln["ln1"]["yT_out"], q + 1)
                for f in range(FC):
                    if q >= 1:
                        pe.wait_ge(s_hT, FC * (q - 1) + f + 1)
                    mm(bank[:, f], aw1[:, f * P:(f + 1) * P], xT[:, q * 512:(q + 1) * 512], start=True, stop=True)\
                        .then_inc(s_h, 1)
                if q + 1 < NQ:
                    ln_pe(pe, ln["ln1"], q + 1, x_side)
                keys_values(q)
                pe.wait_ge(s_hT, FC * q + FC)
                if q >= 1:
                    pe.wait_ge(ln["ln2"]["stats"], 4 * q)
                for j in range(4):
                    for f in range(FC):
                        last = mm(cols4(4, j), hT[:, q % 2, f, j * P:(j + 1) * P], aw2[:, f],
                                  start=f == 0, stop=f == FC - 1)
                    last.then_inc(s_o, 1)
            def queries(q):
                ln_pe(pe, ln["ln3"], q, x_tok)
                if q >= 2:
                    pe.wait_ge(s_q_free, q - 1)
                pe.wait_ge(ln["ln3"]["yT_out"], ln["ln3"]["quads"] + q + 1)
                project(wq, xT, 2 + q % 2, q).then_inc(s_q, 1)
            for q in range(NQ - 1):
                queries(q)
            def cross_queries(i):
                pe.wait_ge(s_q_free, 1 if i == 0 else NQ)
                if i == 1:
                    pe.wait_ge(s_k_free, NQ)
                    pe.wait_ge(s_v_free, NQ)
            def logits(q):
                pe.wait_ge(ln["ln4"]["yT_out"], ln["ln4"]["quads"] + q + 1)
                for t in range(4 * q, 4 * q + 4):
                    last = mm(bank[:, 0, t * E:(t + 1) * E], xT[:, t * P:(t + 1) * P], wg[:, :], start=True, stop=True)
                return last

            def turn_out(q):
                if q >= 2:
                    pe.wait_ge(s_oTs, q - 1)
                pe.wait_ge(att["cross"]["taken"], 4 * q + 4)
                for j in range(4):
                    last = tr(cols4(q % 2, j), work[:, 4 * q + j], ident)
                last.then_inc(s_oT, 1)

            def project_out(q):
                pe.wait_ge(s_oTs, q + 1)
                for j in range(4):
                    last = mm(cols4(2 + q, j), masked(q)[:, j * P:(j + 1) * P], wo[:, :], start=True, stop=True)
                last.then_inc(s_wo, 1)

            def beside(k):
                pe.wait_ge(att["cross"]["shifted"], NT - 1 + k)
                if k == 0:
                    turn_out(0)
                    turn_out(1)
                else:
                    project_out(0)
            att_pe(pe, att["cross"], NT, ident_bf[:, :], mb(1), True, cross_queries, beside=beside,
                   after_first=lambda: queries(NQ - 1))
            project_out(1)
            turn_out(2)
            project_out(2)
            turn_out(3)
            project_out(3)
            for q in range(NQ):
                ln_pe(pe, ln["ln4"], q, x_tok)
                if q == 0:
                    pe.wait_ge(s_oTs, NQ)
                else:
                    logits(q - 1)
            logits(NQ - 1).then_inc(s_r["logits"], 1)
            pe.wait_ge(s_r["chosen"], 1)
            oh = route("onehot", 2 * NT * E)
            mm(bank[:, 0, 0:256], con_at("earlier_row"), oh, start=True, stop=True).then_inc(s_r["ranks"], 1)
            mm(bank[:, 1, 0:256], con_at("ones"), oh, start=True, stop=True).then_inc(s_r["ranks"], 1)
            for n in range(TOPK * NT):
                if n % 8 == 0:
                    pe.wait_ge(s_r["hot"], n // 8 + 1)
                    pe.wait_ge(s_r["hot2"], n // 8 + 1)
                last = mm(bank[:, 4, 0:E * 2 * CT], rank_hot[:, n], slot_hot[:, n].rearrange("p e c -> p (e c)"),
                          start=n == 0, stop=n == TOPK * NT - 1)
            last.then_inc(s_r["found"], 1)
            tr(bank[:, 3, 0:P], wcomb[:, P:2 * P], ident).then_inc(s_lin["w"], 1)
            pe.wait_ge(s_lin["w_sb"], 1)
            mm(bank[:, 2, 0:P], wcomb[:, 0:P], wcomb[:, 2 * P:3 * P], start=True, stop=True).then_inc(s_lin["w"], 1)
            pe.wait_ge(s_lin["w_sb"], 2)
            def turn_in(e):
                pe.wait_ge(s_moe_in[e], 16 * CT)
                if e >= 2:
                    pe.wait_ge(s_moe["xT"], e - 1)
                for j in range(4):
                    last = tr(cols4(6 + e % 2, j), expert_x(e)[:, j], ident)
                last.then_inc(s_moe["turned"], 1)
            def hidden(e):
                pe.wait_ge(s_moe["xT"], e + 1)
                for f in range(FC):
                    if e >= 1:
                        pe.wait_ge(s_mhT, FC * (e - 1) + f + 1)
                    mm(bank[:, f], mw1[:, e, f * P:(f + 1) * P], probs[:, e % 2, 0:512], start=True, stop=True).then_inc(s_mh, 1)

            def output(v, out_bank, next_in=None):
                pe.wait_ge(s_mhT, FC * v + FC)
                for j in range(4):
                    for f in range(FC):
                        last = mm(cols4(out_bank(j), j), hT[:, v % 2, f, j * P:(j + 1) * P], mw2[:, v, f],
                                  start=f == 0, stop=f == FC - 1)
                    if j == 2 and next_in:
                        turn_in(next_in)
                    if v == E - 1:
                        last.then_inc(s_mo, 1)
                if v < E - 1:
                    last.then_inc(s_mo, 1)

            turn_in(0)
            hidden(0)
            turn_in(1)
            for e in range(1, E - 1):
                hidden(e)
                if e >= 3:
                    pe.wait_ge(s_moe["out"], e - 2)
                output(e - 1, lambda j: 4 + (e - 1) % 2, e + 1)
            pe.wait_ge(s_moe["out"], E - 3)
            output(E - 2, lambda j: 4 + (E - 2) % 2)
            hidden(E - 1)
            pe.wait_ge(s_moe["out"], E - 1)
            output(E - 1, lambda j: LAST_BANKS[j])
            def spread_weights(q):
                pe.wait_ge(s_sel["wcol"], q + 1)
                if q >= 1:
                    pe.wait_ge(s_sel["ranked"], 4 * q)
                for j in range(4):
                    last = tr(cols4(7, j), w_pos[:, 0, 4 * q + j:4 * q + j + 1].to_broadcast([P, P]), ident)
                last.then_inc(s_sel["rows"], 1)

            def gather(q):
                for t in range(4 * q, 4 * q + 4):
                    g, i = t // BT, t % BT
                    pe.wait_ge(s_sel["sel"], t + 1)
                    mm(bank[:, 3, g * P:(g + 1) * P], sel(t), x_tok[:, t], start=i == 0, stop=i == BT - 1)
                for t in range(4 * q, 4 * q + 4):
                    g, i = t // BT, t % BT
                    last = mm(bank[:, 0, 2 * g:2 * g + 2], sel(t), w_pos[:, :, t], start=i == 0, stop=i == BT - 1)
                if q == NQ - 1:
                    last.then_inc(s_sel["gathered"], 1)
                if q >= 1:
                    pe.wait_ge(s_sel["half_sb"], q)
                else:
                    pe.wait_ge(s_lin["taken"], NQ)
                for t in range(4 * q, 4 * q + 4):
                    last = mm(cols4(2, t % 4), seq_mask[:, min(t, 2)], sel(t), start=True, stop=True)
                last.then_inc(s_sel["half"], 1)

            def gather_mask(q):
                pe.wait_ge(s_sel["half_sb"], q + 1)
                if q == 0:
                    pe.wait_ge(ln["ln6"]["yT_out"], NQ)
                for t in range(4 * q, 4 * q + 4):
                    g, i = t // BT, t % BT
                    last = mm(bank[:, 4, g * P:(g + 1) * P], masked(q)[:, (t % 4) * P:(t % 4 + 1) * P], sel(t),
                              start=i == 0, stop=i == BT - 1)
                return last

            for w in range(NQ + 3):
                q = w - 3
                if q >= 0:
                    pe.wait_ge(ln["ln7"]["yT_out"], q + 1)
                    if q >= 1:
                        pe.wait_ge(s_sel["wcol"], q)
                    for t in range(4 * q, 4 * q + 4):
                        last = mm(bank[:, 6, t:t + 1], xT[:, t * P:(t + 1) * P], col("router"), start=True, stop=True)
                    last.then_inc(s_sel["weights"], 1)
                q = w
                if q < NQ:
                    ln_pe(pe, ln["ln5"], q, x_tok)
                    if q >= 3:
                        pe.wait_ge(s_rec["taken"], q - 2)
                    if q >= 1:
                        pe.wait_ge(s_lin["masked"], q)
                        pe.wait_ge(s_lin["v_sb"], q)
                    pe.wait_ge(ln["ln5"]["yT_out"], ln["ln5"]["quads"] + q + 1)
                    for j in range(4):
                        at = (4 * q + j) * P
                        last = mm(cols4(0, j), xT0[:, at:at + P], xT[:, at:at + P], start=True, stop=True)
                    last.then_inc(s_lin["scores"], 1)
                    for j in range(4):
                        at = (4 * q + j) * P
                        last = mm(cols4(1, j), xT[:, at:at + P], wcomb[:, 3 * P:4 * P], start=True, stop=True)
                    last.then_inc(s_lin["v"], 1)
                q = w - 2
                if 0 <= q < NQ:
                    pe.wait_ge(s_rec["sum"], q + 1)
                    pe.wait_ge(s_lin["v_sb"], min(w + 1, NQ))
                    if q >= 1:
                        pe.wait_ge(s_rec["taken"], q)
                    for j in range(4):
                        last = tr(cols4(1, j), probsT[:, q % 2, j * P:(j + 1) * P], ident)
                    last.then_inc(s_rec["tok"], 1)
                if w >= 3:
                    spread_weights(w - 3)
                q = w
                if q < NQ:
                    pe.wait_ge(s_lin["masked"], q + 1)
                    pe.wait_ge(s_lin["v_sb"], q + 1)
                    if q >= 1:
                        pe.wait_ge(s_lin["taken"], q)
                    for j in range(4):
                        last = mm(cols4(2, j), masked(q)[:, j * P:(j + 1) * P], values_sb(q)[:, j * P:(j + 1) * P],
                                  start=True, stop=True)
                    last.then_inc(s_lin["read"], 1)
                if 1 <= w <= NQ:
                    ln_pe(pe, ln["ln6"], w - 1, x_tok)
                if w >= NQ:
                    gather(w - NQ)
                if w > NQ:
                    gather_mask(w - NQ - 1)
                if 2 <= w <= NQ + 1:
                    ln_pe(pe, ln["ln7"], w - 2, x_tok)
            gather(NQ - 1)
            gather_mask(NQ - 2)
            gather_mask(NQ - 1).then_inc(s_sel["gathered"], 1)
            pe.wait_ge(s_sel["ranked"], NT)
            for q in range(NQ):
                bk = 5 + 2 * (q % 2)
                if q >= 2:
                    pe.wait_ge(s_sel["selT"], q - 1)
                for j in range(4):
                    last = tr(cols4(bk, j), sel(4 * q + j), ident)
                last.then_inc(s_sel["turned"], 1)
            pe.wait_ge(s_slot["hn"], 1)
            pe.wait_ge(s_sel["selT"], NQ)
            for g in range(NS):
                last = tr(cols4(0, g), hT_flat[:, g * P:(g + 1) * P], ident)
            last.then_inc(s_slot["pe"], 1)
            pe.wait_ge(s_slot["act"], 1)
            for g in range(NS):
                last = mm(bank[:, 1 + g, 0:3 * D], hT_flat[:, 256 + g * P:256 + (g + 1) * P], wqkv[:, :], start=True, stop=True)
            last.then_inc(s_slot["pe"], 1)
            pe.wait_ge(s_slot["act"], 2)
            for g in range(NS):
                for b in (0, 1):
                    last = mm(cols4(5, 2 * g + b), con_at(f"dup{b}"), hT_flat[:, 512 + g * P:512 + (g + 1) * P], start=True, stop=True)
            mask_of_slots = lambda i: slot_mask[:, i, None, :].to_broadcast([P, 8, S])
            pe.wait_ge(s_slot["mask"], 1)
            mm(bank[:, 0, :], ident, mask_of_slots(0), start=True, stop=False)
            pe.wait_ge(s_slot["rope"], 1)
            for g in range(NS):
                for half in (0, 1):
                    tr(cols4(3, 2 * g + half), rope_z(g, 0, half), ident)
                    last = mm(cols4(4, 2 * g + half, S), rope_z(g, 1, half), con_at("fold"), start=True, stop=True)
            last.then_inc(s_slot["pe"], 1)
            att_pe(pe, att["slots"], NS, ident, mask_of_slots, False,
                   lambda i: i == 1 and pe.wait_ge(s_slot["keys"], 1),
                   lambda i: pe.wait_ge(s_slot["values"], 1))
            pe.wait_ge(att["slots"]["taken"], NS)
            for g in range(NS):
                last = tr(cols4(7, g), work[:, g], ident)
            last.then_inc(s_slot["pe"], 1)
            pe.wait_ge(s_slot["act"], 3)
            for g in range(NS):
                last = mm(cols4(7, 2 + g), hT_flat[:, g * P:(g + 1) * P], fwo[:, :], start=True, stop=True)
            last.then_inc(s_slot["pe"], 1)
            def left_of_x(q):
                mm(bank[:, 4 + q], ident, x_side[:, 4 * q:4 * q + 4].rearrange("p t d -> p (t d)"), start=True, stop=True)
            pe.wait_ge(s_sel["kept"], NQ)
            left_of_x(0)
            left_of_x(1)
            pe.wait_ge(s_slot["hn"], 2)
            for g in range(NS):
                last = tr(cols4(0, g), hT_flat[:, g * P:(g + 1) * P], ident)
            last.then_inc(s_slot["pe"], 1)
            pe.wait_ge(s_slot["act"], 4)
            left_of_x(2)
            for f in range(FC):
                last = mm(bank[:, 1 + f // 2, (f % 2) * 256:(f % 2 + 1) * 256], fw1[:, f * P:(f + 1) * P], hT_flat[:, 256:512],
                          start=True, stop=True)
            last.then_inc(s_slot["pe"], 1)
            left_of_x(3)
            pe.wait_ge(s_slot["act"], 5)
            for g in range(NS):
                for f in range(FC):
                    at = 1024 + f * 256 + g * P
                    last = mm(cols4(3, g), hT_flat[:, at:at + P], fw2[:, f], start=f == 0, stop=f == FC - 1)
            last.then_inc(s_slot["pe"], 1)
            pe.wait_ge(s_slot["hn"], 3)
            for q in range(NQ):
                for j in range(4):
                    t = 4 * q + j
                    last = mm(cols4(4 + q, j), selT(t), slot_x[:, t // BT], start=False, stop=True, skip_group_check=True)
                last.then_inc(s_sel["back"], 1)
            end_stage(pe, 1)

        @block.scalar
        def _(act):
            link = Chain(act, s_act)
            A, cp = nc.scalar.activation, nc.scalar.copy
            att_act(act, att["self"], NT, False, con_at("band"), lambda: ln_act(act, ln["ln1"], 0, 1))
            act.wait_ge(s_w, 16 * N_W)
            act.wait_ge(s_moe["zeroed"], 16)
            def keys_out(q):
                act.wait_ge(s_kv, q + 1)
                for g in (0, 1):
                    last = A(k_comp[:, 4 * q:4 * q + 4, g, :],
                             bank[:, 5, g * 256:(g + 1) * 256].rearrange("p (t s) -> p t s", s=S),
                             ACT.Identity, bias=cols[:, COL["bk"] + g:COL["bk"] + g + 1])
                last.then_inc(s_k_free, 1)

            for q in range(NQ):
                if q >= 2:
                    act.wait_ge(s_o, 4 * (q - 1))
                for f in range(FC):
                    act.wait_ge(s_h, FC * q + f + 1)
                    A(hT[:, q % 2, f], bank[:, f], ACT.Relu, bias=cols[:, COL["b1"] + f:COL["b1"] + f + 1]).then_inc(s_hT, 1)
                if q + 1 < NQ:
                    ln_act(act, ln["ln1"], q + 1)
                keys_out(q)
            def queries_out(q):
                ln_act(act, ln["ln3"], q)
                act.wait_ge(s_q, q + 1)
                for b in (0, 1):
                    r = slice(64 * b, 64 * b + 64)
                    for g in (0, 1):
                        last = A(q_diag[r, 4 * q:4 * q + 4, g, 64 * b:64 * b + 64],
                                 bank[r, 2 + q % 2, g * 256:(g + 1) * 256].rearrange("p (t s) -> p t s", s=S),
                                 ACT.Identity, bias=cols[r, COL["bq_scaled"] + g:COL["bq_scaled"] + g + 1], scale=HD ** -0.5)
                last.then_inc(s_q_free, 1)

            for q in range(NQ):
                queries_out(q)
            def turned_out(q):
                act.wait_ge(s_oT, q + 1)
                if q >= 2:
                    act.wait_ge(s_wo, q - 1)
                cp(masked(q), bank[:, q % 2]).then_inc(s_oTs, 1)

            att_act(act, att["cross"], NT, True, con_at("window"), lambda: turned_out(0))
            for q in range(1, NQ):
                turned_out(q)
            for q in range(NQ):
                ln_act(act, ln["ln4"], q)
            act.wait_ge(s_r["gap"], 1)
            A(route("e", NT), route("e", NT), ACT.Exp).then_inc(s_r["exp"], 1)
            link(A(col("t"), col("decay"), ACT.Exp, scale=-1.0))
            A(col("t3"), col("log_alpha"), ACT.Exp).then_inc(s_lin["consts"], 1)
            A(col("ed"), col("w"), ACT.Exp, scale=-1.0)
            A(col("eg"), col("w"), ACT.Exp).then_inc(s_rec["rates"], 1)
            act.wait_ge(s_lin["one_plus"], 1)
            link(A(col("log_gamma"), col("t2"), ACT.Ln))
            link(nc.scalar.mul(col("log_gamma"), col("log_gamma"), -1.0))
            A(decay[:, :], con_at("decay_steps"), ACT.Exp, scale=col("log_gamma")).then_inc(s_lin["consts"], 1)
            act.wait_ge(s_lin["w"], 1)
            cp(wcomb[:, 2 * P:3 * P], bank[:, 3, 0:P]).then_inc(s_lin["w_sb"], 1)
            act.wait_ge(s_lin["w"], 2)
            cp(wcomb[:, 3 * P:4 * P], bank[:, 2, 0:P]).then_inc(s_lin["w_sb"], 1)
            def input_out(e):
                act.wait_ge(s_moe["turned"], e + 1)
                if e >= 2:
                    act.wait_ge(s_mh, FC * (e - 1))
                cp(probs[:, e % 2, 0:512], bank[:, 6 + e % 2]).then_inc(s_moe["xT"], 1)
            input_out(0)
            for e in range(E):
                if e >= 2:
                    act.wait_ge(s_mo, e - 1)
                for f in range(FC):
                    act.wait_ge(s_mh, FC * e + f + 1)
                    A(hT[:, e % 2, f], bank[:, f], ACT.Relu, bias=mb1[:, e, f:f + 1]).then_inc(s_mhT, 1)
                if e + 1 < E:
                    input_out(e + 1)
            def gate(q):
                act.wait_ge(s_quad_in[q], 48)
                for t in range(4 * q, 4 * q + 4):
                    A(fetched(0, t), fetched(0, t), ACT.Copy, scale=route("m0", NT)[:, t:t + 1])
                    last = A(fetched(1, t), fetched(1, t), ACT.Copy, scale=route("m1", NT)[:, t:t + 1])
                last.then_inc(s_lin["gated"], 1)
            def half_out(q):
                act.wait_ge(s_sel["half"], q + 1)
                cp(masked(q), bank[:, 2]).then_inc(s_sel["half_sb"], 1)
            def norm_act(name, q):
                if (name, q) in SHIFTS:
                    act.wait_ge(s_shift, SHIFTS.index((name, q)) + 1)
                    for t in range(4 * q, 4 * q + 4):
                        A(x_tok[:, t], work[:, t], ACT.Identity, bias=var_e[:, t:t + 1], scale=rstd[:, t:t + 1])\
                            .then_inc(ln[name]["y"], 1)
            act.wait_ge(s_r["slots"], 1)
            gate(1)
            for w in range(NQ + 2):
                if w + 2 < NQ:
                    gate(w + 2)
                q = w
                if q < NQ:
                    norm_act("ln5", q)
                    ln_act(act, ln["ln5"], q)
                    act.wait_ge(s_lin["v"], q + 1)
                    if q >= 2:
                        act.wait_ge(s_lin["read"], q - 1)
                    cp(values_sb(q), bank[:, 1]).then_inc(s_lin["v_sb"], 1)
                q = w - 2
                if q >= 0:
                    act.wait_ge(s_rec["tok"], q + 1)
                    cp(work[:, 4 * q:4 * q + 4].rearrange("p t d -> p (t d)"), bank[:, 1]).then_inc(s_rec["taken"], 1)
                q = w - 1
                if 0 <= q < NQ:
                    ln_act(act, ln["ln6"], q)
                    k = xT[:, q * 512:(q + 1) * 512]
                    act.wait_ge(ln["ln6"]["yT_out"], q + 1)
                    act.wait_ge(s_rec["ready"], 1)
                    if q >= 2:
                        act.wait_ge(s_rec["sum"], q - 1)
                    A(seqs(rec_b(q, 2))[:, :, 2:S], seqs(k)[:, :, 1:S - 1], ACT.Exp, scale=-1.0).then_inc(s_rec["scan"], 1)
                    A(rec_b(q, 0), k, ACT.Exp).then_inc(s_rec["exp_k"], 1)
                    A(rec_b(q, 3), k, ACT.Exp, bias=col("u")).then_inc(s_rec["exp"], 1)
                if w >= NQ:
                    half_out(w - NQ)
                if w >= 2:
                    norm_act("ln7", w - 2)
                    ln_act(act, ln["ln7"], w - 2)
            for q in (NQ - 2, NQ - 1):
                half_out(q)
            for q in range(NQ):
                act.wait_ge(s_sel["turned"], q + 1)
                cp(mw1[:, 4 + q, :], bank[:, 5 + 2 * (q % 2)]).then_inc(s_sel["selT"], 1)
            act.wait_ge(s_slot["pe"], 1)
            cp(hT_flat[:, 256:512], bank[:, 0, 0:256]).then_inc(s_slot["act"], 1)
            act.wait_ge(s_slot["angle"], 1)
            A(slot_trig[:, :, :, :], slot_angle[:, :, :, :], ACT.Sin).then_inc(s_slot["trig"], 1)
            act.wait_ge(s_slot["pe"], 2)
            cp(hT_flat[:, 512:768].rearrange("p (g n) -> p g n", g=NS), bank[:, 1:3, 2 * D:3 * D]).then_inc(s_slot["act"], 1)
            act.wait_ge(s_slot["pe"], 3)
            cp(q_diag[:, 0:NS].rearrange("p t g n -> p (t g n)"), bank[:, 3])
            cp(k_comp[:, 0:NS].rearrange("p t g n -> p (t g n)"), bank[:, 4, 0:256]).then_inc(s_slot["keys"], 1)
            att_act(act, att["slots"], NS, False, None)
            act.wait_ge(s_slot["pe"], 4)
            cp(hT_flat[:, 0:256], bank[:, 7, 0:256]).then_inc(s_slot["act"], 1)
            act.wait_ge(s_slot["pe"], 6)
            cp(hT_flat[:, 256:512], bank[:, 0, 0:256]).then_inc(s_slot["act"], 1)
            act.wait_ge(s_slot["pe"], 7)
            A(hT_flat[:, 1024:2048], bank[:, 1:3, :].rearrange("p a n -> p (a n)"), ACT.Gelu_apprx_tanh).then_inc(s_slot["act"], 1)
            for q in range(BY_ACT):
                act.wait_ge(s_shift, len(SHIFTS) + q + 1)
                for t in range(4 * q, 4 * q + 4):
                    last = A(x_tok[:, t], back(t), ACT.Identity, bias=var_e[:, t:t + 1], scale=rstd[:, t:t + 1])
                last.then_inc(s_sel["out"], 1)
            end_stage(act, 1)

        @block.vector
        def _(dve):
            link = Chain(dve, s_dve)
            tt, ts, stt, cp = nc.vector.tensor_tensor, nc.vector.tensor_scalar, nc.vector.scalar_tensor_tensor, nc.vector.tensor_copy
            dve.wait_ge(s_con, 16)
            cp(ident_bf[:, :], ident).then_inc(s_setup, 1)
            a = CONST_AT["band"][0]
            cp(mask_bf[:, :, :].rearrange("p a n -> p (a n)"), con[:, a:a + 2 * S]).then_inc(s_setup, 1)
            link(nc.vector.memset(q_diag[:, :, :, :], 0.0))
            dve.wait_ge(s_v_clear, 3)

            def build_quad(q):
                dve.wait_ge(s_k_in[q], 16)
                for b in (0, 1):
                    r = slice(64 * b, 64 * b + 64)
                    last = cp(q_diag[r, 4 * q:4 * q + 4, :, 64 * b:64 * b + 64], k_comp[r, 4 * q:4 * q + 4])
                last.then_inc(s_built, 1)
                dve.wait_ge(s_quad_in[q], 16)
                for h in (0, 1):
                    r = slice(64 * h, 64 * h + 64)
                    last = cp(v_pair[r, 8 * q:8 * q + 8, :, h * (HD + 1):h * (HD + 1) + HD],
                              v_rows[r, 512 * q:512 * (q + 1)].rearrange("p (b a e) -> p b a e", a=H // 2, e=HD))
                last.then_inc(s_built, 1)

            s1, summed, told, centred = ln["ln1"], {}, {}, {}

            def norm1(i):
                if i % 4 == 1 and i // 4 + 1 < NQ:
                    build_quad(i // 4 + 1)
                if i == 4:
                    dve.wait_ge(s_x, 16)
                t = i - 4
                if 0 <= t < NT:
                    dve.wait_ge(att["self"]["taken"], t + 1)
                    summed[t] = link.mark(tt(work[:, t], work[:, t], x_tok[:, t], ALU.add))
                t = i - 5
                if 0 <= t < NT:
                    link.wait(summed[t])
                    told[t] = link.mark(nc.vector.bn_stats(stats[:, t], work[:, t]))
                t = i - 6
                if 0 <= t < NT:
                    link.wait(told[t])
                    nc.vector.bn_aggr(mv[:, t], stats[:, t]).then_inc(s1["stats"], 1)
                t = i - 7
                if i == 7:
                    dve.wait_ge(s_w, 16 * N_W)
                if 0 <= t < NT:
                    dve.wait_ge(s1["stats"], t + 1)
                    centred[t] = link.mark(stt(x_side[:, t], work[:, t], mv[:, t, 0:1], rows[:, 0], ALU.subtract, ALU.mult))
                t = i - 11
                if 0 <= t < NT:
                    link.wait(centred[t])
                    dve.wait_ge(s1["rstd"], t // 4 + 1)
                    stt(x_side[:, t], x_side[:, t], rstd[:, t:t + 1], rows[:, 1], ALU.mult, ALU.add).then_inc(s1["y"], 1)

            build_quad(0)
            att_dve(dve, att["self"], NT, False, link, norm1)
            for i in range(NT + 3, NT + 11):
                norm1(i)
            ts(cols[:, COL["bq_scaled"]:COL["bq_scaled"] + 2], cols[:, 0:2], HD ** -0.5, None, ALU.mult)

            def told_quad(s, q, summed):
                tiles = range(4 * q, 4 * q + 4)
                n = []
                for t in tiles:
                    link.wait(summed[t % 4])
                    n.append(link.mark(nc.vector.bn_stats(stats[:, t], work[:, t])))
                for t in tiles:
                    link.wait(n[t % 4])
                    nc.vector.bn_aggr(mv[:, t], stats[:, t]).then_inc(s["stats"], 1)

            def sum_quad(q):
                tiles = range(4 * q, 4 * q + 4)
                dve.wait_ge(s_side, q + 1)
                dve.wait_ge(s_o, 4 * q + 4)
                told_quad(ln["ln2"], q, [link.mark(tt(work[:, t], bank[:, 4, (t % 4) * P:(t % 4 + 1) * P],
                                                      with_b2[:, t], ALU.add)) for t in tiles])
                dve.wait_ge(ln["ln2"]["stats"], 4 * q + 4)
                return [link.mark(stt(work[:, t], work[:, t], mv[:, t, 0:1], rows[:, 2], ALU.subtract, ALU.mult)) for t in tiles]

            def second_norm(q, centred):
                tiles = range(4 * q, 4 * q + 4)
                dve.wait_ge(ln["ln2"]["rstd"], q + 1)
                n = []
                for t in tiles:
                    link.wait(centred[t % 4])
                    n.append(link.mark(stt(work[:, t], work[:, t], rstd[:, t:t + 1], x_tok[:, t], ALU.mult, ALU.add)))
                told_quad(ln["ln3"], q, n)

            def third_norm(q):
                for t in range(4 * q, 4 * q + 4):
                    ln_apply(dve, ln["ln3"], t, x_tok[:, t]).then_inc(ln["ln3"]["y"], 1)

            def values_out(q):
                dve.wait_ge(s_kv, q + 1)
                for b in (0, 1):
                    r = slice(64 * b, 64 * b + 64)
                    last = tt(v_pair[r, 8 * q:8 * q + 8, :, b * (HD + 1):b * (HD + 1) + HD],
                              bank[r, 6].rearrange("p (j a e) -> p j a e", a=H // 2, e=HD),
                              rows[r, 5].rearrange("p (a h e) -> p a h e", h=2, e=HD)[:, None, :, b]
                              .to_broadcast([64, 8, H // 2, HD]), ALU.add)
                last.then_inc(s_v_free, 1)

            for q in range(NQ):
                values_out(q)
                c = sum_quad(q)
                if q >= 1:
                    third_norm(q - 1)
                second_norm(q, c)
            third_norm(NQ - 1)
            def projected(q):
                r = slice(4 * q, 4 * q + 4)
                dve.wait_ge(s_wo, q + 1)
                dve.wait_ge(s_side, NQ + q + 1)
                n = link.mark(tt(work[:, r], bank[:, 2 + q].rearrange("p (t n) -> p t n", n=P), x_side[:, r], ALU.add))
                told_quad(ln["ln4"], q, [n] * 4)
            att_dve(dve, att["cross"], NT, True, link, beside=lambda: projected(0))
            for q in range(1, NQ + 1):
                if q < NQ:
                    projected(q)
                for t in range(4 * q - 4, 4 * q):
                    ln_apply(dve, ln["ln4"], t, x_tok[:, t]).then_inc(ln["ln4"]["y"], 1)
            def v3(name):
                return route(name, NT * E).rearrange("p (t e) -> p t e", e=E)

            def over_e(ap):
                return ap[:, :, None].to_broadcast([P, NT, E])
            link(cp(row_index_bf[:, :], con_at("row_index")))
            lg, eq = v3("logits"), v3("eq")
            first = con_at("first_choice")[:, None, :].to_broadcast([P, NT, E])
            dve.wait_ge(s_r["logits"], 1)
            link(cp(route("logits", NT * E), bank[:, 0, 0:NT * E]))
            one = route("onehot", 2 * NT * E).rearrange("p (k t e) -> p k t e", k=2, e=E)
            for k in (0, 1):
                m, c = route("m%d" % k, NT), route("c", NT)
                link(nc.vector.tensor_reduce(m, lg, AX, ALU.max))
                link(tt(eq, lg, over_e(m), ALU.is_equal))
                link(tt(eq, eq, first, ALU.mult))
                link(nc.vector.tensor_reduce(c, eq, AX, ALU.max))
                last = tt(one[:, k], eq, over_e(c), ALU.is_equal)
                if k == 0:
                    link(last)
                    link(stt(lg, one[:, 0], -3e38, lg, ALU.mult, ALU.add))
                else:
                    last.then_inc(s_r["chosen"], 1)
            tt(route("e", NT), route("m1", NT), route("m0", NT), ALU.subtract).then_inc(s_r["gap"], 1)
            dve.wait_ge(s_r["exp"], 1)
            link(ts(route("m0", NT), route("e", NT), 1.0, None, ALU.add))
            link(nc.vector.reciprocal(route("m0", NT), route("m0", NT)))
            link(tt(route("m1", NT), route("e", NT), route("m0", NT), ALU.mult))
            tot, run, at = route("tot", 256), route("run", 256), route("at", 256)
            dve.wait_ge(s_r["ranks"], 2)
            link(cp(tot.rearrange("p (e n) -> p n e", e=E), bank[:, 1, 0:256].rearrange("p (n e) -> p n e", e=E)))
            link(nc.vector.tensor_tensor_scan(run, con_at("scan_carry"), tot, 0.0, ALU.mult, ALU.add))
            link(tt(run, run, tot, ALU.subtract))
            link(tt(at.rearrange("p (n e) -> p n e", e=E), bank[:, 0, 0:256].rearrange("p (n e) -> p n e", e=E),
                    run.rearrange("p (e n) -> p n e", e=E), ALU.add))
            ok, n = route("tot", 256), TOPK * NT
            link(stt(ok, at, float(CAP), route("onehot", 256), ALU.is_lt, ALU.mult))
            link(tt(at, at, ok, ALU.mult))
            rank, valid = route("eq", n), route("logits", n)
            v_ok = ok.rearrange("p (n e) -> p n e", e=E)
            link(nc.vector.tensor_reduce(rank, at.rearrange("p (n e) -> p n e", e=E), AX, ALU.add))
            def by_tile(i):
                return inside[:, i].rearrange("p (n j) -> p n j", j=CT)
            link(tt(by_tile(0), rank[:, :, None].to_broadcast([P, n, CT]),
                    con_at("rank_base")[:, None, :].to_broadcast([P, n, CT]), ALU.subtract))
            link(ts(inside[:, 1], inside[:, 0], 0.0, None, ALU.is_ge))
            link(stt(inside[:, 1], inside[:, 0], float(P), inside[:, 1], ALU.is_lt, ALU.mult))
            link(tt(inside[:, 2], inside[:, 0], inside[:, 1], ALU.mult))
            link(nc.vector.tensor_reduce(route("at", n), by_tile(2), AX, ALU.add))
            cp(rank_row[:, :], route("at", n))
            cp(room_bf[:, :, :].rearrange("p n e -> p (n e)"), ok)
            ts(told_bf[:, :, :, 0], by_tile(1), con_at("row"), None, ALU.mult)
            tt(told_bf[:, :, :, 1], by_tile(1), con_at("tile_from_1")[:, :, None].to_broadcast([P, n, CT]), ALU.mult)\
                .then_inc(s_r["rows"], 1)
            dve.wait_ge(s_r["rows"], 1)
            for c in range(n // 8):
                r = slice(8 * c, 8 * c + 8)
                tt(rank_hot[:, r], row_index_bf[:, None, :].to_broadcast([P, 8, P]),
                   rank_row[:, r, None].to_broadcast([P, 8, P]), ALU.is_equal).then_inc(s_r["hot"], 1)
            link(nc.vector.tensor_reduce(valid, v_ok, AX, ALU.add))
            link(tt(route("m0", n), route("m0", n), valid, ALU.mult))
            found = bank[:, 4, 0:E * 2 * CT].rearrange("p (s c) -> p s c", c=2)
            a, late, own = route("tot", E * CT), route("run", E * CT), route("at", E * CT)
            dve.wait_ge(s_r["found"], 1)
            link(ts(a, found[:, :, 1], float(P), float(-P), ALU.mult, ALU.add))
            link(tt(a, a, found[:, :, 0], ALU.add))
            link(ts(late, a, float(T), float(-T), ALU.is_ge, ALU.mult))
            link(stt(own, a, 0.0, con_at("spare"), ALU.is_lt, ALU.mult))
            link(tt(late, late, a, ALU.add))
            link(ts(place[:, 0], late, 0.0, None, ALU.max))
            tt(place[:, 1], own, a, ALU.add).then_inc(s_r["slots"], 1)
            dve.wait_ge(s_lin["consts"], 1)
            link(ts(col("half_alpha"), col("t3"), 0.5, None, ALU.mult))
            ts(col("t2"), col("t"), 1.0, None, ALU.add).then_inc(s_lin["one_plus"], 1)
            dve.wait_ge(s_lin["consts"], 2)
            link(tt(decay[:, :], decay[:, :], con_at("causal"), ALU.mult))
            dve.wait_ge(s_rec["rates"], 1)
            ed, eg = probsT[:, 0, 512:1024], probsT[:, 1, 512:1024]
            ts(ed, con_at("carry"), col("ed"), None, ALU.mult)
            ts(eg, con_at("carry"), col("eg"), None, ALU.mult)
            ts(wqkv[:, 0:D], fqkv[:, 0:D], col("ln1"), HD ** -0.5, ALU.mult, ALU.mult)
            ts(wqkv[:, D:3 * D], fqkv[:, D:3 * D], col("ln1"), None, ALU.mult)
            ts(fw1[:, :], fw1[:, :], col("ln2"), None, ALU.mult)
            link(cp(w_pos[:, 1], pos_i[:, :]))
            for e in range(E):
                dve.wait_ge(s_mo, e + 1)
                if e >= 2:
                    dve.wait_ge(s_moe_st[e % 2], 16 * CT * (e // 2))
                if e == E - 1:
                    for j in range(CT):
                        dve.wait_ge(s_mo, e + j + 1)
                        tt(expert_y(e)[:, j], bank[:, LAST_BANKS[j], j * P:(j + 1) * P], mb2[:, e], ALU.add).then_inc(s_moe["out"], 1)
                    break
                tt(expert_y(e), bank[:, 4 + e % 2].rearrange("p (t d) -> p t d", d=D),
                   mb2[:, e:e + 1].to_broadcast([P, 4, D]), ALU.add).then_inc(s_moe["out"], 1)

            for j in (0, 1):
                for i in (1, 2):
                    last = nc.vector.memset(seqs(rec_b(j, i))[:, :, 0:2], 0.0)
            last.then_inc(s_rec["ready"], 1)

            def quad(ap, q):
                return ap[:, 4 * q:4 * q + 4]

            def told(s, q, n=None):
                if n:
                    link.wait(n)
                marks = [link.mark(nc.vector.bn_stats(stats[:, t], work[:, t])) for t in range(4 * q, 4 * q + 4)]
                for t in range(4 * q, 4 * q + 4):
                    link.wait(marks[t % 4])
                    nc.vector.bn_aggr(mv[:, t], stats[:, t]).then_inc(s["stats"], 1)

            def shift(s, q):
                r = slice(4 * q, 4 * q + 4)
                dve.wait_ge(s["rstd"], s["quads"] + q + 1)
                stt(var_e[:, r], mv[:, r, 0], -1.0, rstd[:, r], ALU.mult, ALU.mult).then_inc(s_shift, 1)

            def norm(name, q):
                s = ln[name]
                if (name, q) in SHIFTS:
                    return shift(s, q)
                if name == "ln7":
                    dve.wait_ge(s["y"], 4 * q)
                for t in range(4 * q, 4 * q + 4):
                    ln_apply(dve, s, t, x_tok[:, t]).then_inc(s["y"], 1)

            def experts_sum(q):
                dve.wait_ge(s_quad_in[q], 48)
                if q >= 1:
                    dve.wait_ge(s_lin["added"], q)
                    dve.wait_ge(s_lin["gated"], q)
                if q == 0:
                    m = [link.mark(stt(work[:, t], fetched(0, t), route("m0", NT)[:, t:t + 1], x_tok[:, t], ALU.mult, ALU.add))
                         for t in range(4)]
                    m = [(link.wait(m[t]), link.mark(stt(work[:, t], fetched(1, t), route("m1", NT)[:, t:t + 1], work[:, t],
                                                         ALU.mult, ALU.add)))[1] for t in range(4)]
                    return told(ln["ln5"], q, m[-1])
                told(ln["ln5"], q, link.mark(tt(quad(work, q), quad(x_side, q), quad(k_comp, q).rearrange("p t g s -> p t (g s)"),
                                                ALU.add)))

            def mask_scores(q):
                dve.wait_ge(s_lin["scores"], q + 1)
                if q >= 2:
                    dve.wait_ge(s_lin["read"], q - 1)
                tt(masked(q).rearrange("p (t n) -> p t n", n=P), bank[:, 0].rearrange("p (t n) -> p t n", n=P),
                   decay[:, None, :].to_broadcast([P, 4, P]), ALU.mult).then_inc(s_lin["masked"], 1)

            def add_reads(q):
                dve.wait_ge(s_lin["read"], q + 1)
                stt(quad(work, q), bank[:, 2].rearrange("p (t n) -> p t n", n=P), col("half_alpha"), quad(x_tok, q),
                    ALU.mult, ALU.add).then_inc(s_lin["taken"], 1)
                dve.wait_ge(s_lin["taken"], q + 1)
                told(ln["ln6"], q)

            def recurrence(q):
                a, bb, m = probs[:, q % 2, 0:512], probs[:, q % 2, 512:1024], probsT[:, q % 2, 0:512]
                c = ctxT[:, q * 512:(q + 1) * 512]
                dve.wait_ge(s_rec["scan"], q + 1)
                link(nc.vector.tensor_tensor_scan(bb, eg, rec_b(q, 2), 0.0, ALU.mult, ALU.add))
                have_b = link.mark(tt(bb, bb, c, ALU.mult))
                dve.wait_ge(s_rec["ekv"], q + 1)
                have_a = link.mark(nc.vector.tensor_tensor_scan(a, ed, rec_b(q, 1), 0.0, ALU.mult, ALU.add))
                link.wait(have_b)
                link(tt(bb, bb, con_at("steps"), ALU.add))
                dve.wait_ge(s_rec["exp"], q + 1)
                link(tt(bb, bb, rec_b(q, 3), ALU.mult))
                link.wait(have_a)
                link(tt(bb, bb, a, ALU.add))
                if q >= 2:
                    dve.wait_ge(s_rec["tok"], q - 1)
                tt(m, bb, xT[:, q * 512:(q + 1) * 512], ALU.add).then_inc(s_rec["sum"], 1)

            gt, tie, ge = route("gt", NT), route("tie", NT), route("ge", NT)

            def weigh(q):
                dve.wait_ge(s_sel["weights"], q + 1)
                ts(w_pos[:, 0, 4 * q:4 * q + 4], bank[:, 6, 4 * q:4 * q + 4], col("router_b"), None, ALU.add).then_inc(s_sel["wcol"], 1)

            def rank(q):
                dve.wait_ge(s_sel["wcol"], q + 1)
                dve.wait_ge(s_sel["rows"], q + 1)
                for t in range(4 * q, 4 * q + 4):
                    if t >= 10:
                        dve.wait_ge(s_sel["ranked"], t - 9)
                    row = bank[:, 7, (t % 4) * P:(t % 4 + 1) * P]
                    for n, op, m, o in ((0, ALU.is_gt, "same_seq", gt), (1, ALU.is_equal, "same_seq_before", tie)):
                        counted = link.mark(stt(scrap((t % 10) * 3 + n), row, w_pos[:, 0, t:t + 1], con_at(m), op, ALU.mult,
                                                accum_out=o[:, t:t + 1]))
                r = slice(4 * q, 4 * q + 4)
                link.wait(counted)
                link(tt(gt[:, r], gt[:, r], tie[:, r], ALU.add))
                link(ts(tie[:, r], gt[:, r], float(NSEL), None, ALU.is_lt))
                link(tt(gt[:, r], gt[:, r], con_at("slot_base")[:, r], ALU.add))
                link(tt(gt[:, r], gt[:, r], tie[:, r], ALU.mult))
                link(ts(gt[:, r], gt[:, r], -1.0, None, ALU.add))
                for t in range(4 * q, 4 * q + 4):
                    ts(sel(t), con_at("row_index"), gt[:, t:t + 1], None, ALU.is_equal).then_inc(s_sel["sel"], 1)
                for t in range(4 * q, 4 * q + 4):
                    row = bank[:, 7, (t % 4) * P:(t % 4 + 1) * P]
                    stt(scrap((t % 10) * 3 + 2), row, w_pos[:, 0, t:t + 1], con_at("same_seq"), ALU.is_ge, ALU.mult,
                        accum_out=ge[:, t:t + 1]).then_inc(s_sel["ranked"], 1)
                dve.wait_ge(s_sel["ranked"], 4 * q + 4)
                ts(ge[:, r], ge[:, r], float(NSEL), 1.0, ALU.is_gt, ALU.add).then_inc(s_sel["share"], 1)

            experts_sum(0)
            for w in range(NQ + 3):
                if w == NQ + 2:
                    nc.vector.memset(hT_flat[:, 3072:4096], 0.0)
                if w == 0:
                    norm("ln5", 0)
                if w + 1 < NQ:
                    experts_sum(w + 1)
                if 1 <= w < NQ:
                    norm("ln5", w)
                if 2 <= w < NQ + 2:
                    recurrence(w - 2)
                if w >= 3:
                    weigh(w - 3)
                if 1 <= w <= NQ:
                    add_reads(w - 1)
                if w < NQ:
                    mask_scores(w)
                if 1 <= w <= NQ:
                    norm("ln6", w - 1)
                if 2 <= w < NQ + 2:
                    dve.wait_ge(s_rec["taken"], w - 1)
                    told(ln["ln7"], w - 2)
                if w >= 3:
                    rank(w - 3)
                if 2 <= w < NQ + 2:
                    norm("ln7", w - 2)
            dve.wait_ge(s_sel["gathered"], 1)
            cp(slot_wp[:, :], bank[:, 0, 0:2 * NS])
            link(cp(slot_x0[:, :, :].rearrange("p g d -> p (g d)"), bank[:, 3, 0:NS * D]))
            def squares_of(src):
                for g in range(NS):
                    last = stt(scrap(g + 4 * (src is slot_x)), src[:, g], 1.0, src[:, g], ALU.mult, ALU.mult,
                               accum_out=slot_s[:, g:g + 1])
                last.then_inc(s_slot["squares"], 1)

            def scaled(src, n):
                dve.wait_ge(s_slot["rms"], n)
                for g in range(NS):
                    last = ts(hT_flat[:, g * P:(g + 1) * P], src[:, g], slot_s[:, 4 + g:5 + g], None, ALU.mult)
                last.then_inc(s_slot["hn"], 1)
            squares_of(slot_x0)
            scaled(slot_x0, 1)
            ang, k = slot_angle[:, 0], slot_angle[:, 1]
            for g in range(NS):
                link(ts(ang[:, g], con_at("inv_freq"), slot_wp[:, 2 * g + 1:2 * g + 2], None, ALU.mult))
            link(ts(k, ang, float(1 / (2 * np.pi)), 12582912.0, ALU.mult, ALU.add))
            link(ts(k, k, -12582912.0, None, ALU.add))
            link(stt(ang, k, -6.28125, ang, ALU.mult, ALU.add))
            link(stt(ang, k, float(-(2 * np.pi - 6.28125)), ang, ALU.mult, ALU.add))
            link(ts(ang, ang, 3.1415925, -3.1415925, ALU.min, ALU.max))
            link(stt(k, ang, -1.0, ang, ALU.mult, ALU.max))
            ts(k, k, -1.0, float(np.pi / 2), ALU.mult, ALU.add).then_inc(s_slot["angle"], 1)
            dve.wait_ge(s_slot["trig"], 1)
            dve.wait_ge(s_slot["act"], 2)
            dve.wait_ge(s_sel["gathered"], 2)
            for b in (0, 1):
                r = slice(64 * b, 64 * b + 64)
                last = tt(slot_mask[r], bank[r, 4, 0:NS * P].rearrange("p (g b k) -> p g b k", b=2, k=S)[:, :, b],
                          con_at("slot_block")[r, None, :].to_broadcast([64, NS, S]), ALU.add)
            last.then_inc(s_slot["mask"], 1)
            for g in range(NS):
                qk = bank[:, 1 + g, 0:2 * D].rearrange("p (h e) -> p h e", e=HD)
                lo, hi = qk[:, :, 0:4], qk[:, :, 4:8]
                sin = slot_trig[:, 0, g, None, :].to_broadcast([P, 2 * H, 4])
                cos = slot_trig[:, 1, g, None, :].to_broadcast([P, 2 * H, 4])
                part = lambda i: hT_flat[:, 2048 + i * 128:2048 + (i + 1) * 128]
                for i, (x, y) in enumerate(((lo, cos), (hi, sin), (hi, cos), (lo, sin))):
                    last = tt(part(4 * g + i).rearrange("p (h e) -> p h e", e=4), x, y, ALU.mult)
                link(last)
                for b in (0, 1):
                    r = slice(64 * b, 64 * b + 64)
                    z = hT_flat[r, 3072 + g * 512:3072 + (g + 1) * 512].rearrange("p (x b h e) -> p x b h e", b=2, h=8, e=HD)[:, :, b]
                    pr = lambda i: part(4 * g + i)[r].rearrange("p (x h e) -> p x h e", h=8, e=4)
                    tt(z[:, :, :, 0:4], pr(0), pr(1), ALU.subtract)
                    last = tt(z[:, :, :, 4:8], pr(2), pr(3), ALU.add)
            last.then_inc(s_slot["rope"], 1)
            dve.wait_ge(s_slot["pe"], 3)
            for h in (0, 1):
                r = slice(64 * h, 64 * h + 64)
                last = cp(v_pair[r, 0:2 * NS, :, h * (HD + 1):h * (HD + 1) + HD],
                          bank[r, 5].rearrange("p (j a h e) -> p j a h e", a=H // 2, h=2, e=HD)[:, :, :, h])
            last.then_inc(s_slot["values"], 1)
            dve.wait_ge(s_slot["keys"], 1)
            att_spread(dve, att["slots"], NS, mult=tt)
            att_dve(dve, att["slots"], NS, False, link)
            dve.wait_ge(s_slot["pe"], 5)
            link(tt(slot_x[:, :, :].rearrange("p g d -> p (g d)"), bank[:, 7, 256:512], slot_x0[:, :, :].rearrange("p g d -> p (g d)"), ALU.add))
            squares_of(slot_x)
            scaled(slot_x, 2)
            dve.wait_ge(s_slot["pe"], 8)
            link(tt(slot_x[:, :, :].rearrange("p g d -> p (g d)"), bank[:, 3, 0:256], slot_x[:, :, :].rearrange("p g d -> p (g d)"), ALU.add))
            for g in range(NS):
                last = ts(slot_x[:, g], slot_x[:, g], slot_wp[:, 2 * g:2 * g + 1], None, ALU.mult)
            last.then_inc(s_slot["hn"], 1)
            s = ln["ln8"]

            for q in range(NQ):
                dve.wait_ge(s_sel["back"], q + 1)
                marks = [link.mark(nc.vector.bn_stats(stats[:, t], back(t))) for t in range(4 * q, 4 * q + 4)]
                for t in range(4 * q, 4 * q + 4):
                    link.wait(marks[t % 4])
                    nc.vector.bn_aggr(mv[:, t], stats[:, t]).then_inc(s["stats"], 1)
                if 1 <= q < 1 + BY_ACT:
                    shift(s, q - 1)
            for q in range(BY_ACT, NQ):
                dve.wait_ge(s["rstd"], s["quads"] + q + 1)
                for t in range(4 * q, 4 * q + 4):
                    ts(x_tok[:, t], back(t), mv[:, t, 0:1], rstd[:, t:t + 1], ALU.subtract, ALU.mult).then_inc(s["y"], 1)
            end_stage(dve, 1)


def lay_out(i):
    f = lambda n: np.asarray(i[n])
    x, c = f("x"), f("ctx_1024")
    a = {"const": CONST}
    a["x"] = x.reshape(NT, P, D).transpose(1, 0, 2)
    xr = x.reshape(NT, 2, S, 2, 64).transpose(1, 4, 0, 3, 2)
    a["k_self"] = xr.reshape(P, NT, 2, S)
    a["v_self"] = x.reshape(B, S, H // 2, 2, HD).transpose(3, 1, 0, 2, 4).reshape(P, B * (H // 2) * HD)
    a["ctxT"] = c.reshape(T, D).T
    a["rows"] = np.tile(np.stack([f(n) for n in ("L0_attn_ln1_g", "L0_attn_ln1_b", "L0_attn_ln2_g", "L0_attn_ln2_b",
                                                 "L0_attn_b2", "L0_xattn_bv", "L0_xattn_bo", "L0_xattn_bo")])[None], (P, 1, 1))
    one = lambda n: np.broadcast_to(f(n).reshape(1, 1), (P, 1))
    two = lambda n: np.tile(f(n).reshape(2, 64).T, (2, 1))
    a["cols"] = np.concatenate([two("L0_xattn_bq"), two("L0_xattn_bk"), f("L0_attn_b1").reshape(FC, P).T,
                                f("L1_xattn_u")[:, None], f("L1_xattn_w")[:, None], f("L1_ffn_ln1")[:, None],
                                f("L1_ffn_ln2")[:, None], f("L1_ffn_router_w"), one("L1_attn_decay"),
                                one("L1_attn_log_alpha"), one("L1_ffn_router_b")], 1)
    a["L0_attn_W1"] = f("L0_attn_W1")
    a["L0_attn_W2"] = f("L0_attn_W2").reshape(FC, P, D).transpose(1, 0, 2)
    for n, m in (("wq", "L0_xattn_Wq"), ("wk", "L0_xattn_Wk"), ("wv", "L0_xattn_Wv"), ("wo", "L0_xattn_Wo")):
        a[n] = f(m).T
    a["L0_ffn_wg"] = f("L0_ffn_wg")
    a["mw1"] = f("L0_ffn_w1").transpose(1, 0, 2)
    a["mw2"] = f("L0_ffn_w2").reshape(E, FC, P, D).transpose(2, 0, 1, 3)
    a["mb1"] = f("L0_ffn_b1").reshape(E, FC, P).transpose(2, 0, 1)
    a["mb2"] = np.tile(f("L0_ffn_b2")[None], (P, 1, 1))
    a["w_read_write"] = np.concatenate([f("L1_attn_W_write"), f("L1_attn_W_read")], 1)
    mask = f("L1_ffn_attention_mask")[:, 0, :S, :S]
    m = np.zeros((2, S, 3, 2, S), np.float32)
    for t in range(3):
        for b in (0, 1):
            m[b, :, t, b] = mask[min(2 * t + b, len(mask) - 1)]
    a["seq_mask"] = m.reshape(P, 3, P)
    pos = f("L1_ffn_position_ids")[:, :S]
    a["pos"] = pos[np.minimum(np.arange(B), len(pos) - 1)].reshape(NT, P).T
    a["fqkv"] = np.concatenate([f("L1_ffn_wq"), f("L1_ffn_wk"), f("L1_ffn_wv")], 1)
    a["L1_ffn_wo"], a["L1_ffn_w1"] = f("L1_ffn_wo"), f("L1_ffn_w1")
    a["fw2"] = f("L1_ffn_w2").reshape(FC, P, D).transpose(1, 0, 2)
    return {n: np.ascontiguousarray(v) for n, v in a.items()}


def kernel(**inputs):
    import concourse.bacc as bacc
    from concourse.bass_utils import run_bass_kernel_spmd

    nc = bacc.Bacc("TRN2", target_bir_lowering=False, num_devices=1)
    arrays = {f"in_{n}": v for n, v in lay_out(inputs).items()}
    io = {n[3:]: nc.dram_tensor(n, v.shape, mybir.dt.from_np(v.dtype), kind="ExternalInput").ap() for n, v in arrays.items()}
    io["out"] = nc.dram_tensor("out", (P, NT, D), F32, kind="ExternalOutput").ap()
    build(nc, io)
    r = run_bass_kernel_spmd(nc, [arrays], core_ids=[0])
    return np.ascontiguousarray(np.asarray(r.results[0]["out"]).transpose(1, 0, 2)).reshape(B, S, D)
```
